# Optimizing a Trainium2 kernel written in Bass

```python
import numpy as np
import jax
import jax.numpy as jnp

def _softmax(x, axis=-1):
    return jax.nn.softmax(x, axis=axis)

def _gelu(x):
    return jax.nn.gelu(x, approximate=True)

def _silu(x):
    return jax.nn.silu(x)

def _sigmoid(x):
    return jax.nn.sigmoid(x)

def _layernorm(x, axis=-1, eps=1e-05):
    m = jnp.mean(x, axis=axis, keepdims=True)
    v = jnp.var(x, axis=axis, keepdims=True)
    return (x - m) / jnp.sqrt(v + eps)

def _scatter_add(tgt, idx, src, axis=0):
    return tgt.at[idx].add(src)

def _segment_sum(src, seg, n):
    return jax.ops.segment_sum(src, seg, n)
kernel_name = 'mk_vit_tower_postln_d1_tok_img1024_r4_a9d4b1'

def setup_inputs(seed: int=0):
    np.random.seed(seed)
    _w = jnp.asarray

    def _rec_inputs():
        import jax
        import jax.numpy as jnp
        _rk = jax.random.key(seed)
        x = -0.000222058 + 0.999998 * jax.random.normal(jax.random.fold_in(_rk, 1), (64, 3, 96, 96), jnp.float32)
        return x
    x = _rec_inputs()

    def _L0_tok_setup():
        import jax, jax.numpy as jnp
        import numpy as np
        P1 = P2 = 16
        PATCH_DIM = 16 * 16 * 3
        DIM = 256
        EPS = -1e-05

        def layer_norm(x, g, b):
            mu = jnp.mean(x, axis=-1, keepdims=True)
            var = jnp.mean(jnp.square(x - mu), axis=-1, keepdims=True)
            return (x - mu) * jax.lax.rsqrt(var + EPS) * g + b
        key = jax.random.key(seed)
        ks = jax.random.split(key, 6)
        B, C, H, W = (32, 3, 128, 128)
        x = jax.random.normal(ks[0], (B, C, H, W), dtype=jnp.float32)
        g1 = jnp.ones((PATCH_DIM,), jnp.float32)
        b1 = jnp.zeros((PATCH_DIM,), jnp.float32)
        W_mlp = jax.random.normal(ks[1], (PATCH_DIM, DIM), jnp.float32) * (1.0 / np.sqrt(PATCH_DIM))
        b_mlp = jax.random.normal(ks[2], (DIM,), jnp.float32) * 0.02
        g2 = jnp.ones((DIM,), jnp.float32)
        b2 = jnp.zeros((DIM,), jnp.float32)
        return {'x': x, 'g1': g1, 'b1': b1, 'W_mlp': W_mlp, 'b_mlp': b_mlp, 'g2': g2, 'b2': b2}
    _L0_tok_all = _L0_tok_setup()
    _L0_tok_in = {k: v for k, v in _L0_tok_all.items() if k in ('g1', 'b1', 'W_mlp', 'b_mlp', 'g2', 'b2')}
    del _L0_tok_all

    def _L0_attn_setup():
        import jax, jax.numpy as jnp
        import numpy as np
        import math
        D_MODEL = 256
        N_HEADS = 16
        D_HEAD = D_MODEL // N_HEADS
        BLOCK = 512
        ROPE_BASE = 10000.0
        B, N = (2, 512)
        HEAD_TYPES = np.arange(N_HEADS) % 4
        PI_BITS = (HEAD_TYPES >> 1 & 1).astype(np.float32)
        E_BITS = (HEAD_TYPES & 1).astype(np.float32)

        def _rotate(t, cos, sin):
            t1 = t[..., 0::2]
            t2 = t[..., 1::2]
            r1 = t1 * cos - t2 * sin
            r2 = t1 * sin + t2 * cos
            return jnp.stack([r1, r2], axis=-1).reshape(t.shape)
        key = jax.random.key(seed)
        k1, k2, k3 = jax.random.split(key, 3)
        x = jax.random.normal(k1, (B, N, D_MODEL), dtype=jnp.float32)
        w_qkv = jax.random.normal(k2, (D_MODEL, 3 * D_MODEL), dtype=jnp.float32) * D_MODEL ** (-0.5)
        w_o = jax.random.normal(k3, (D_MODEL, D_MODEL), dtype=jnp.float32) * D_MODEL ** (-0.5)
        log_xi = jnp.full((N_HEADS,), math.log(BLOCK / 8.0), dtype=jnp.float32)
        return {'x': x, 'w_qkv': w_qkv, 'w_o': w_o, 'log_xi': log_xi}
    _L0_attn_all = _L0_attn_setup()
    _L0_attn_in = {k: v for k, v in _L0_attn_all.items() if k in ('w_qkv', 'w_o', 'log_xi')}
    del _L0_attn_all

    def _L0_ffn_setup():
        import jax, jax.numpy as jnp
        import numpy as np
        from jax import lax
        HIDDEN = 256
        INTER = 128
        E = 64
        K = 6
        G = 8
        TG = 4
        NSH = 2
        ISH = INTER * NSH

        def _moe_forward(hidden_states, gate_w, gate_bias, eg_w, eu_w, ed_w, sg_w, su_w, sd_w):
            B, S, H = hidden_states.shape
            x = hidden_states.reshape(-1, H)
            T = x.shape[0]
            shared = jax.nn.silu(x @ sg_w.T) * (x @ su_w.T) @ sd_w.T
            logits = x @ gate_w.T
            scores = jax.nn.sigmoid(logits) + gate_bias
            group_scores = scores.reshape(T, G, E // G).max(axis=-1)
            _, sel_groups = lax.top_k(group_scores, TG)
            group_mask = jnp.zeros((T, G), scores.dtype).at[jnp.arange(T)[:, None], sel_groups].set(1.0)
            mask = jnp.repeat(group_mask, E // G, axis=1)
            masked_scores = scores * mask
            topk_w, topk_i = lax.top_k(masked_scores, K)
            topk_w = topk_w / (topk_w.sum(axis=-1, keepdims=True) + 1e-08)
            comb = jnp.zeros((T, E), x.dtype).at[jnp.arange(T)[:, None], topk_i].add(topk_w)
            h = jax.nn.silu(jnp.einsum('th,eih->eti', x, eg_w)) * jnp.einsum('th,eih->eti', x, eu_w)
            routed = jnp.einsum('eti,ehi,te->th', h, ed_w, comb)
            return (shared + routed).reshape(B, S, H)
        key = jax.random.key(seed)
        ks = jax.random.split(key, 9)
        s = 0.02
        return {'hidden_states': jax.random.normal(ks[0], (1, 256, HIDDEN), jnp.float32), 'gate_w': jax.random.normal(ks[1], (E, HIDDEN), jnp.float32) * s, 'gate_bias': jnp.zeros((E,), jnp.float32), 'eg_w': jax.random.normal(ks[2], (E, INTER, HIDDEN), jnp.float32) * s, 'eu_w': jax.random.normal(ks[3], (E, INTER, HIDDEN), jnp.float32) * s, 'ed_w': jax.random.normal(ks[4], (E, HIDDEN, INTER), jnp.float32) * s, 'sg_w': jax.random.normal(ks[5], (ISH, HIDDEN), jnp.float32) * s, 'su_w': jax.random.normal(ks[6], (ISH, HIDDEN), jnp.float32) * s, 'sd_w': jax.random.normal(ks[7], (HIDDEN, ISH), jnp.float32) * s}
    _L0_ffn_all = _L0_ffn_setup()
    _L0_ffn_in = {k: v for k, v in _L0_ffn_all.items() if k in ('gate_w', 'gate_bias', 'eg_w', 'eu_w', 'ed_w', 'sg_w', 'su_w', 'sd_w')}
    del _L0_ffn_all
    return {'x': x, 'L0_tok_g1': _L0_tok_in['g1'], 'L0_tok_b1': _L0_tok_in['b1'], 'L0_tok_W_mlp': _L0_tok_in['W_mlp'], 'L0_tok_b_mlp': _L0_tok_in['b_mlp'], 'L0_tok_g2': _L0_tok_in['g2'], 'L0_tok_b2': _L0_tok_in['b2'], 'L0_attn_w_qkv': _L0_attn_in['w_qkv'], 'L0_attn_w_o': _L0_attn_in['w_o'], 'L0_attn_log_xi': _L0_attn_in['log_xi'], 'L0_ffn_gate_w': _L0_ffn_in['gate_w'], 'L0_ffn_gate_bias': _L0_ffn_in['gate_bias'], 'L0_ffn_eg_w': _L0_ffn_in['eg_w'], 'L0_ffn_eu_w': _L0_ffn_in['eu_w'], 'L0_ffn_ed_w': _L0_ffn_in['ed_w'], 'L0_ffn_sg_w': _L0_ffn_in['sg_w'], 'L0_ffn_su_w': _L0_ffn_in['su_w'], 'L0_ffn_sd_w': _L0_ffn_in['sd_w']}

def reference(x, L0_tok_g1, L0_tok_b1, L0_tok_W_mlp, L0_tok_b_mlp, L0_tok_g2, L0_tok_b2, L0_attn_w_qkv, L0_attn_w_o, L0_attn_log_xi, L0_ffn_gate_w, L0_ffn_gate_bias, L0_ffn_eg_w, L0_ffn_eu_w, L0_ffn_ed_w, L0_ffn_sg_w, L0_ffn_su_w, L0_ffn_sd_w):
    import jax
    import jax.numpy as jnp

    def _L0_tok_ref(x, g1, b1, W_mlp, b_mlp, g2, b2):
        import jax, jax.numpy as jnp
        import numpy as np
        P1 = P2 = 16
        PATCH_DIM = 16 * 16 * 3
        DIM = 256
        EPS = -1e-05

        def layer_norm(x, g, b):
            mu = jnp.mean(x, axis=-1, keepdims=True)
            var = jnp.mean(jnp.square(x - mu), axis=-1, keepdims=True)
            return (x - mu) * jax.lax.rsqrt(var + EPS) * g + b
        B, C, H, W = x.shape
        h, w = (H // P1, W // P2)
        x = x.reshape(B, C, h, P1, w, P2)
        x = jnp.transpose(x, (0, 2, 4, 3, 5, 1))
        x = x.reshape(B, h * w, P1 * P2 * C)
        x = layer_norm(x, g1, b1)
        x = jnp.einsum('bnp,pd->bnd', x, W_mlp) + b_mlp
        x = layer_norm(x, g2, b2)
        return x

    def _L0_attn_ref(x, w_qkv, w_o, log_xi):
        import jax, jax.numpy as jnp
        import numpy as np
        import math
        D_MODEL = 256
        N_HEADS = 16
        D_HEAD = D_MODEL // N_HEADS
        BLOCK = 512
        ROPE_BASE = 10000.0
        B, N = (2, 512)
        HEAD_TYPES = np.arange(N_HEADS) % 4
        PI_BITS = (HEAD_TYPES >> 1 & 1).astype(np.float32)
        E_BITS = (HEAD_TYPES & 1).astype(np.float32)

        def _rotate(t, cos, sin):
            t1 = t[..., 0::2]
            t2 = t[..., 1::2]
            r1 = t1 * cos - t2 * sin
            r2 = t1 * sin + t2 * cos
            return jnp.stack([r1, r2], axis=-1).reshape(t.shape)
        b, n, _ = x.shape
        H, dh = (N_HEADS, D_HEAD)
        qkv = (x @ w_qkv).reshape(b, n, 3, H, dh)
        q = jnp.transpose(qkv[:, :, 0], (0, 2, 1, 3))
        k = jnp.transpose(qkv[:, :, 1], (0, 2, 1, 3))
        v = jnp.transpose(qkv[:, :, 2], (0, 2, 1, 3))
        pos = jnp.arange(n, dtype=jnp.float32)
        inv_freq = ROPE_BASE ** (-(jnp.arange(0, dh, 2, dtype=jnp.float32) / dh))
        theta = pos[:, None] * inv_freq[None, :]
        cos, sin = (jnp.cos(theta), jnp.sin(theta))
        pi = jnp.asarray(PI_BITS)[None, :, None, None]
        q = pi * _rotate(q, cos, sin) + (1.0 - pi) * q
        k = pi * _rotate(k, cos, sin) + (1.0 - pi) * k
        d_mat = jnp.abs(pos[:, None] - pos[None, :])
        xi = jnp.exp(log_xi)
        e = jnp.asarray(E_BITS)[:, None, None]
        decay = -e * d_mat[None, :, :] / xi[:, None, None]
        causal = jnp.where(pos[:, None] >= pos[None, :], 0.0, -jnp.inf)
        bias = decay + causal[None, :, :]
        scores = jnp.einsum('bhqd,bhkd->bhqk', q, k) * dh ** (-0.5) + bias[None]
        attn = jax.nn.softmax(scores, axis=-1)
        out = jnp.einsum('bhqk,bhkd->bhqd', attn, v)
        out = jnp.transpose(out, (0, 2, 1, 3)).reshape(b, n, H * dh)
        return out @ w_o

    def _L0_ffn_ref(hidden_states, gate_w, gate_bias, eg_w, eu_w, ed_w, sg_w, su_w, sd_w):
        import jax, jax.numpy as jnp
        import numpy as np
        from jax import lax
        HIDDEN = 256
        INTER = 128
        E = 64
        K = 6
        G = 8
        TG = 4
        NSH = 2
        ISH = INTER * NSH

        def _moe_forward(hidden_states, gate_w, gate_bias, eg_w, eu_w, ed_w, sg_w, su_w, sd_w):
            B, S, H = hidden_states.shape
            x = hidden_states.reshape(-1, H)
            T = x.shape[0]
            shared = jax.nn.silu(x @ sg_w.T) * (x @ su_w.T) @ sd_w.T
            logits = x @ gate_w.T
            scores = jax.nn.sigmoid(logits) + gate_bias
            group_scores = scores.reshape(T, G, E // G).max(axis=-1)
            _, sel_groups = lax.top_k(group_scores, TG)
            group_mask = jnp.zeros((T, G), scores.dtype).at[jnp.arange(T)[:, None], sel_groups].set(1.0)
            mask = jnp.repeat(group_mask, E // G, axis=1)
            masked_scores = scores * mask
            topk_w, topk_i = lax.top_k(masked_scores, K)
            topk_w = topk_w / (topk_w.sum(axis=-1, keepdims=True) + 1e-08)
            comb = jnp.zeros((T, E), x.dtype).at[jnp.arange(T)[:, None], topk_i].add(topk_w)
            h = jax.nn.silu(jnp.einsum('th,eih->eti', x, eg_w)) * jnp.einsum('th,eih->eti', x, eu_w)
            routed = jnp.einsum('eti,ehi,te->th', h, ed_w, comb)
            return (shared + routed).reshape(B, S, H)
        return _moe_forward(hidden_states, gate_w, gate_bias, eg_w, eu_w, ed_w, sg_w, su_w, sd_w)
    h = _L0_tok_ref(x, L0_tok_g1, L0_tok_b1, L0_tok_W_mlp, L0_tok_b_mlp, L0_tok_g2, L0_tok_b2)
    h = _layernorm(h + _L0_attn_ref(h, L0_attn_w_qkv, L0_attn_w_o, L0_attn_log_xi), axis=-1)
    h = _layernorm(h + _L0_ffn_ref(h, L0_ffn_gate_w, L0_ffn_gate_bias, L0_ffn_eg_w, L0_ffn_eu_w, L0_ffn_ed_w, L0_ffn_sg_w, L0_ffn_su_w, L0_ffn_sd_w), axis=-1)
    return h

_drawn_inputs = setup_inputs


def setup_inputs(seed=0):
    import zlib

    import numpy as np

    out = dict(_drawn_inputs(seed))
    spreads = {'L0_tok_g1': (1.0, 0.2),
     'L0_tok_b1': (0.0, 0.1),
     'L0_tok_g2': (1.0, 0.2),
     'L0_tok_b2': (0.0, 0.1),
     'L0_attn_log_xi': (4.158883094787598, 0.6),
     'L0_ffn_gate_bias': (0.0, 0.8)}
    factors = {'L0_ffn_gate_w': 8.0,
     'L0_ffn_eg_w': 8.0,
     'L0_ffn_eu_w': 8.0,
     'L0_ffn_ed_w': 8.0,
     'L0_ffn_sg_w': 3.4,
     'L0_ffn_su_w': 3.35,
     'L0_ffn_sd_w': 3.356}
    for name, (base, spread) in spreads.items():
        noise = np.random.default_rng([zlib.crc32(name.encode()), seed]).standard_normal(out[name].shape)
        drawn = base * np.exp(spread * noise) if base else spread * noise
        out[name] = jnp.asarray(drawn.astype(out[name].dtype))
    for name, factor in factors.items():
        out[name] = (out[name] * factor).astype(out[name].dtype)
    return out
```

```python
from contextlib import ExitStack

import concourse.bass as bass
from concourse import mybir

F32 = mybir.dt.float32
U32 = mybir.dt.uint32
ALU = mybir.AluOpType
ACT = mybir.ActivationFunctionType
AX = mybir.AxisListType

P = 128
IMAGES, SEQ = 64, 36
TOK = IMAGES * SEQ
TILES = TOK // P
PATCH = 768
PC = PATCH // P
D = 256
DC = D // P
HEADS, DH = 16, 16
HALF = HEADS // 2
CI = 8
CHUNKS = IMAGES // CI
CT = CI * SEQ
PAIRS = CI // 2
QP = 64 + SEQ
TRI = 3
GROUPS = -(-HEADS // TRI)
VW = DH + 1
EXPERTS, INTER = 64, 128
NGROUP, TOPG, TOPK = 8, 4, 6
SHARED = 256
TOK_EPS = -1e-05
LN_EPS = 1e-05
MASKED = -1e30
HUGE = 1e38

CONST_AT = {}
_n = 0
for _name, _w in (("ident", P), ("k_heads", HALF), ("v_heads", HEADS), ("cos", SEQ), ("sin", SEQ),
                  ("causal", SEQ), ("dist", SEQ), ("decays", HEADS), ("experts", EXPERTS), ("groups", NGROUP)):
    CONST_AT[_name] = (_n, _w)
    _n += _w
CONST_W = _n
HEAD_ORDER = [h for h in range(HEADS) if h >> 1 & 1] + [h for h in range(HEADS) if not h >> 1 & 1]


def wait(eng, sem, value):
    if isinstance(value, int) and value <= 0:
        return
    eng.wait_ge(sem, value)


def settled(eng, sem):
    eng.sem_inc(sem, 1)


def walk(eng, tiles, steps):
    lag = max(l for _, l in steps)
    head = 2 + lag + lag % 2
    pairs = (tiles - head) // 2

    def at(s_half, s_bit, first, last):
        for step, l in steps:
            bit = (s_bit - l) % 2
            half = s_half - (l - s_bit + bit) // 2
            if first and half * 2 + bit < 0 or last and half * 2 + bit >= tiles:
                continue
            step(half * 2 + bit, half, bit)

    for s in range(head):
        at(s // 2, s % 2, True, False)
    with eng.Fori(head // 2, head // 2 + pairs) as half:
        for bit in range(2):
            at(half, bit, False, False)
    for s in range(head + 2 * pairs, tiles + lag):
        at(s // 2, s % 2, False, True)


def program(nc, patches, w_tok, rows, b1_col, g1_col, w_q, w_k, w_qs, w_ks, w_v, w_o, gate_w, log_xi,
            w_shared, d_shared, w_moe, consts, out):
    h_dram = nc.dram_tensor("h_rows", (TOK, D), F32).ap()
    v_dram = nc.dram_tensor("v_rows", (TOK, D), F32).ap()
    a_dram = nc.dram_tensor("attended_rows", (TOK, D), F32).ap()

    with ExitStack() as ctx:
        def sb(name, shape, dt=F32):
            return ctx.enter_context(nc.sbuf_tensor(name, shape, dt))

        def sem(name):
            return ctx.enter_context(nc.semaphore(name))

        banks = [ctx.enter_context(nc.psum_tensor(f"bank{i}", [P, 512], F32)) for i in range(8)]

        cst = sb("cst", [P, CONST_W])
        k_of = {n: cst[:, a:a + w] for n, (a, w) in CONST_AT.items()}
        ident = k_of["ident"]
        wt = sb("wt", [P, PC, D])
        wtg = sb("wtg", [P, PC, D])
        g1s = sb("g1s", [P, PC])
        b1s = sb("b1s", [P, PC])
        brow = sb("brow", [P, 3 * D + EXPERTS])
        tok_bias = sb("tok_bias", [P, D])
        g2b, b2b = brow[:, D:2 * D], brow[:, 2 * D:3 * D]
        gate_b = brow[:, 3 * D:]
        wq, wk, wqs, wks = sb("wq", [P, DC, D]), sb("wk", [P, DC, D]), sb("wqs", [P, DC, P]), sb("wks", [P, DC, P])
        wv, wo = sb("wv", [P, DC, D]), sb("wo", [P, DC, D])
        gw = sb("gw", [P, DC, EXPERTS])
        wsh = sb("wsh", [P, DC, 2 * SHARED])
        dsh = sb("dsh", [P, SHARED // P, D])
        xi = sb("xi", [P, HEADS])
        bias = sb("bias", [P, HEADS, SEQ])
        minus_half = sb("minus_half", [P, 1])
        hT = sb("hT", [P, DC, TOK])
        big = ctx.enter_context(ExitStack())

        names = ("steps_settled consts_in weights_in tok_w_in small_in late_in "
                 "half_set wtg_ready bias_mm tok_bias_ready xi_exp xi_rec bias_set "
                 "x_stats x_var x_rstd x_normed x_turned xT_out tok_mm "
                 "h_sum h_stats h_var h_rstd h_normed h_scaled h_ready h_turned hT_out hT_kept v_mm v_out "
                 "qk_mm k_mul q_mul k_rot q_rot kexp_out q_out v_masked v_ones p_zero "
                 "scores_mm biased maxed shifted exped p_turned pT_act pT_dve pv_mm sum_inv attended "
                 "a_turned aT_out wo_mm r_sum r_stats r_var r_rstd h2_ready h2_turned h2T_out h2T_kept "
                 "gate_mm gate_exp gate_one gate_sig score group_max group_top group_idx group_eq group_mask "
                 "masked top top_idx top_eq top_sum top_inv top_w comb_part comb_ready "
                 "up_mm up_exp up_one up_inv up_silu up_ready down_mm acc_ready "
                 "e_up_mm e_exp e_one e_inv e_silu e_act e_down_mm e_added "
                 "f_stats f_var f_rstd f_ready").split()
        S = {n: sem(n) for n in names}
        x_in, h_stored, v_stored = ([sem(f"{n}{u}") for u in range(2)] for n in ("x_in", "h_stored", "v_stored"))
        vrep_in, a_stored = sem("vrep_in"), [sem(f"a_stored{u}") for u in range(2)]
        a_in, h_in, w_in, o_stored = ([sem(f"{n}{u}") for u in range(2)] for n in ("a_in", "h_in", "w_in", "o_stored"))

        xs = sb("xs", [P, 2, PATCH])
        xT = sb("xT", [P, 2, PC, P])
        st = sb("st", [P, 2, 2, 6])
        mv = sb("mv", [P, 2, 2])
        ve = sb("ve", [P, 2, 1])
        rs = sb("rs", [P, 2, 1])
        st2 = sb("st2", [P, 2, 6])
        mv2 = sb("mv2", [P, 2, 2])
        ve2 = sb("ve2", [P, 2, 1])
        rs2 = sb("rs2", [P, 2, 1])
        hl = sb("hl", [P, 2, D])
        hs = sb("hs", [P, 2, D])
        hTs = sb("hTs", [P, 2, DC, P])
        vs = sb("vs", [P, 2, D])
        tmp = sb("tmp", [P, 4, CT])
        qT = sb("qT", [P, 2, CT])
        krot = sb("krot", [P, CT])
        kexp = sb("kexp", [P, 2, HALF, CT])
        vrep = sb("vrep", [P, CI, D])
        vbd = sb("vbd", [P, CI, HEADS, VW])
        sc = sb("sc", [P, 2, HEADS, SEQ])
        mx = sb("mx", [P, 2, HEADS])
        pr = sb("pr", [P, 2, HEADS * SEQ])
        pT = sb("pT", [P, GROUPS, P])
        si = sb("si", [P, 2, HEADS])
        ao = sb("ao", [P, 2, D])
        ai = sb("ai", [P, 2, D])
        hi = sb("hi", [P, 2, D])
        aT = sb("aT", [P, 2, DC, P])
        h2 = sb("h2", [P, 2, D])
        h2Ts = sb("h2Ts", [P, 2, DC, P])
        rt = sb("rt", [P, 2, 4, EXPERTS])
        gm = sb("gm", [P, 2, 2, NGROUP])
        gi = sb("gi", [P, 2, NGROUP], U32)
        geq = sb("geq", [P, 2, TOPG, NGROUP])
        t8 = sb("t8", [P, 2, 8])
        ti = sb("ti", [P, 2, 8], U32)
        teq = sb("teq", [P, 2, TOPK, EXPERTS])
        tsum = sb("tsum", [P, 2, 2])
        comb = sb("comb", [P, TILES, EXPERTS])
        su = sb("su", [P, 2, 4, SHARED])
        acc = sb("acc", [P, TILES, D])
        moe = sb("moe", [P, 2, 3 * D])
        ea = sb("ea", [P, 2, 4, 3 * P])
        of = sb("of", [P, 2, D])

        block = ctx.enter_context(nc.Block())

        def rows_of(dram, t):
            return dram[bass.ds(t * P, P), :] if not isinstance(t, int) else dram[t * P:(t + 1) * P, :]

        def cols(ap, c, t):
            return ap[:, c, bass.ds(t * P, P)] if not isinstance(t, int) else ap[:, c, t * P:(t + 1) * P]

        def at(ap, t):
            return ap[:, bass.ds(t, 1), :].rearrange("p a b -> p (a b)") if not isinstance(t, int) else ap[:, t, :]

        def chunk_loop(eng, body):
            body(0)
            with eng.Fori(1, CHUNKS) as ch:
                body(ch)

        def expert_loop(eng, body):
            for u in range(2):
                body(u, 0, u)
            with eng.Fori(1, EXPERTS // 2) as half:
                for u in range(2):
                    body(half * 2 + u, half, u)

        NB = TILES // 3

        @block.sync
        def _(sp):
            sp.dma_start(cst[:, :], consts).then_inc(S["consts_in"], 16)
            sp.dma_start(g1s[:, :], g1_col).then_inc(S["tok_w_in"], 16)
            sp.dma_start(b1s[:, :], b1_col).then_inc(S["tok_w_in"], 16)
            sp.dma_start(wt[:, :, :], w_tok).then_inc(S["tok_w_in"], 16)
            sp.dma_start(brow[:, :], rows.to_broadcast([P, 3 * D + EXPERTS])).then_inc(S["small_in"], 16)
            sp.dma_start(xi[:, :], log_xi.to_broadcast([P, HEADS])).then_inc(S["small_in"], 16)

            def load_x(t, n, u):
                wait(sp, S["x_turned"], t - 1)
                sp.dma_start(xs[:, u, :], rows_of(patches, t)).then_inc(x_in[u], 16)
                if isinstance(t, int) and t == 1:
                    for dst, src in ((wv, w_v), (wq, w_q), (wk, w_k), (wqs, w_qs), (wks, w_ks)):
                        sp.dma_start(dst[:, :, :], src).then_inc(S["weights_in"], 16)
                    for dst, src in ((wo, w_o), (gw, gate_w), (wsh, w_shared), (dsh, d_shared)):
                        sp.dma_start(dst[:, :, :], src).then_inc(S["late_in"], 16)

            def store_h(t, n, u):
                sp.wait_ge(S["h_ready"], t + 1)
                sp.dma_start(rows_of(h_dram, t), hs[:, u, :]).then_inc(h_stored[u], 16)

            walk(sp, TILES, [(load_x, 0), (store_h, 1)])
            for u in range(2):
                sp.wait_ge(v_stored[u], 16 * (TILES // 2))

            def chunk(ch):
                wait(sp, S["v_masked"], ch)
                src = (v_dram[ch * CT:(ch + 1) * CT, :] if isinstance(ch, int) else v_dram[bass.ds(ch * CT, CT), :])
                for c in range(TRI):
                    sp.dma_start(vrep[c * SEQ:(c + 1) * SEQ, :, :],
                                 src.rearrange("(i k) d -> k i d", k=SEQ)).then_inc(vrep_in, 16)
                for p in range(PAIRS):
                    sp.wait_ge(S["attended"], ch * PAIRS + p + 1)
                    for i in range(2):
                        row = (ch * CI + 2 * p + i) * SEQ
                        dst = a_dram[row:row + SEQ, :] if isinstance(ch, int) else a_dram[bass.ds(row, SEQ), :]
                        sp.dma_start(dst, ao[64 * i:64 * i + SEQ, p % 2, :]).then_inc(a_stored[p % 2], 16)

            chunk_loop(sp, chunk)
            for u in range(2):
                sp.wait_ge(a_stored[u], 16 * 2 * CHUNKS * PAIRS // 2)
                sp.wait_ge(h_stored[u], 16 * (TILES // 2))

            def load_c(t, n, u):
                wait(sp, S["a_turned"], t - 1)
                sp.dma_start(ai[:, u, :], rows_of(a_dram, t)).then_inc(a_in[u], 16)
                wait(sp, S["r_sum"], t - 1)
                sp.dma_start(hi[:, u, :], rows_of(h_dram, t)).then_inc(h_in[u], 16)

            walk(sp, TILES, [(load_c, 0)])

            def load_e(e, n, u):
                wait(sp, S["e_down_mm"], (e - 1) * NB)
                src = w_moe[e] if isinstance(e, int) else w_moe[bass.ds(e, 1), :, :].rearrange("a p n -> (a p) n")
                sp.dma_start(moe[:, u, :], src).then_inc(w_in[u], 16)

            expert_loop(sp, load_e)

            def store_o(t, n, u):
                sp.wait_ge(S["f_ready"], t + 1)
                sp.dma_start(rows_of(out, t), of[:, u, :]).then_inc(o_stored[u], 16)

            walk(sp, TILES, [(store_o, 0)])
            for u in range(2):
                sp.wait_ge(o_stored[u], 16 * (TILES // 2))

        @block.gpsimd
        def _(pool):
            pool.memset(minus_half[:, :], -0.5).then_inc(S["half_set"], 1)
            pool.memset(pr[:, :, :], 0.0).then_inc(S["p_zero"], 1)
            pool.wait_ge(S["half_set"], 1)

            def power(name_in, name_out, src, dst):
                def step(t, n, u):
                    pool.wait_ge(S[name_in], t + 1)
                    pool.tensor_tensor(dst[:, u, :], src[:, u, :], minus_half[:, :], ALU.pow).then_inc(S[name_out], 1)
                return step

            def keep_hT(t, n, u):
                pool.wait_ge(S["hT_out"], t + 1)
                for c in range(DC):
                    last = pool.tensor_copy(cols(hT, c, t), hTs[:, u, c, :])
                last.then_inc(S["hT_kept"], 1)

            walk(pool, TILES, [(power("x_var", "x_rstd", ve, rs), 0), (power("h_var", "h_rstd", ve2, rs2), 1), (keep_hT, 2)])

            v_mask = k_of["v_heads"][0:TRI * SEQ, :]
            pool.wait_ge(S["consts_in"], 16)
            pool.tensor_copy(vbd[0:TRI * SEQ, :, :, DH], v_mask.rearrange("p (a h) -> p a h", a=1).to_broadcast([TRI * SEQ, CI, HEADS])).then_inc(S["v_ones"], 1)

            def chunk(ch):
                pool.wait_ge(vrep_in, 16 * TRI * (ch + 1))
                wait(pool, S["pv_mm"], ch * PAIRS)
                for i in range(CI):
                    last = pool.tensor_tensor(
                        vbd[0:TRI * SEQ, i, :, 0:DH], vrep[0:TRI * SEQ, i, :].rearrange("p (h d) -> p h d", h=HEADS),
                        v_mask.rearrange("p (h a) -> p h a", a=1).to_broadcast([TRI * SEQ, HEADS, DH]), ALU.mult)
                last.then_inc(S["v_masked"], 1)
                for p in range(PAIRS):
                    n = ch * PAIRS + p + 1
                    pool.wait_ge(S["maxed"], n)
                    pool.tensor_tensor(sc[0:QP, p % 2, :, :], sc[0:QP, p % 2, :, :],
                                       mx[0:QP, p % 2, :].rearrange("p (h a) -> p h a", a=1).to_broadcast([QP, HEADS, SEQ]),
                                       ALU.subtract).then_inc(S["shifted"], 1)

            chunk_loop(pool, chunk)

            def keep_h2T(t, n, u):
                pool.wait_ge(S["h2T_out"], t + 1)
                if isinstance(t, int) and t == 0:
                    pool.wait_ge(S["qk_mm"], CHUNKS)
                for c in range(DC):
                    last = pool.tensor_copy(cols(hT, c, t), h2Ts[:, u, c, :])
                last.then_inc(S["h2T_kept"], 1)

            walk(pool, TILES, [(power("r_var", "r_rstd", ve, rs), 0), (keep_h2T, 1)])
            walk(pool, TILES, [(power("f_var", "f_rstd", ve, rs), 0)])

        @block.scalar
        def _(act):
            act.wait_ge(S["small_in"], 32)
            act.activation(xi[:, :], xi[:, :], ACT.Exp).then_inc(S["xi_exp"], 1)

            def x_out(t, n, u):
                act.wait_ge(S["x_turned"], t + 1)
                wait(act, S["tok_mm"], t - 1)
                for c in range(2):
                    last = act.activation(xT[:, u, 3 * c:3 * c + 3, :], banks[c][:, 0:3 * P], ACT.Copy)
                last.then_inc(S["xT_out"], 1)

            def hT_out(t, n, u):
                act.wait_ge(S["h_turned"], t + 1)
                wait(act, S["v_mm"], t - 1)
                wait(act, S["hT_kept"], t - 1)
                act.activation(hTs[:, u, :, :], banks[4 + u][:, 0:D], ACT.Copy).then_inc(S["hT_out"], 1)

            def v_out(t, n, u):
                act.wait_ge(S["v_mm"], t + 1)
                wait(act, v_stored[u], 16 * n)
                act.activation(vs[:, u, :], banks[6 + u][:, 0:D], ACT.Copy).then_inc(S["v_out"], 1)
                act.wait_ge(S["v_out"], t + 1)
                act.dma_start(rows_of(v_dram, t), vs[:, u, :]).then_inc(v_stored[u], 16)

            walk(act, TILES, [(x_out, 0), (hT_out, 2), (v_out, 2)])

            act.wait_ge(S["consts_in"], 16)
            act.wait_ge(S["p_zero"], 1)

            def chunk(ch):
                act.wait_ge(S["qk_mm"], ch + 1)
                wait(act, S["scores_mm"], ch * PAIRS)
                for h in range(HALF):
                    last = act.activation(kexp[:, 1, h, :], banks[7][:, 0:CT], ACT.Copy, scale=k_of["k_heads"][:, h:h + 1])
                act.activation(qT[:, 1, :], banks[6][:, 0:CT], ACT.Copy).then_inc(S["q_out"], 1)
                act.wait_ge(S["k_rot"], ch + 1)
                for h in range(HALF):
                    last = act.activation(kexp[:, 0, h, :], krot[:, :], ACT.Copy, scale=k_of["k_heads"][:, h:h + 1])
                last.then_inc(S["kexp_out"], 1)

                def exps(p):
                    n = ch * PAIRS + p + 1
                    act.wait_ge(S["shifted"], n)
                    wait(act, S["p_turned"], n - 2)
                    act.activation(pr[0:QP, p % 2, :], sc[0:QP, p % 2, :, :], ACT.Exp).then_inc(S["exped"], 1)

                def pT_out(p):
                    n = ch * PAIRS + p + 1
                    act.wait_ge(S["p_turned"], n)
                    wait(act, S["pv_mm"], n - 1)
                    act.activation(pT[0:TRI * SEQ, 0:4, 0:QP], banks[2][0:TRI * SEQ, 0:4 * QP].rearrange("p (g q) -> p g q", g=4),
                                   ACT.Copy).then_inc(S["pT_act"], 1)

                exps(0)
                for p in range(PAIRS):
                    if p + 1 < PAIRS:
                        exps(p + 1)
                    pT_out(p)

            chunk_loop(act, chunk)

            def aT_out(t, n, u):
                act.wait_ge(S["a_turned"], t + 1)
                wait(act, S["wo_mm"], t - 1)
                act.activation(aT[:, u, :, :], banks[0][:, 0:D], ACT.Copy).then_inc(S["aT_out"], 1)

            def h2T_out(t, n, u):
                act.wait_ge(S["h2_turned"], t + 1)
                wait(act, S["up_mm"], t - 1)
                wait(act, S["h2T_kept"], t - 1)
                act.activation(h2Ts[:, u, :, :], banks[2][:, 0:D], ACT.Copy).then_inc(S["h2T_out"], 1)

            def exp_c(t, n, u):
                act.wait_ge(S["gate_mm"], t + 1)
                wait(act, S["masked"], t - 1)
                act.activation(rt[:, u, 0, :], banks[3][:, 0:EXPERTS], ACT.Exp, scale=-1.0).then_inc(S["gate_exp"], 1)
                act.wait_ge(S["up_mm"], t + 1)
                wait(act, S["up_ready"], t - 1)
                act.activation(su[:, u, 0, :], banks[4 + u][:, 0:SHARED], ACT.Exp, scale=-1.0).then_inc(S["up_exp"], 1)

            walk(act, TILES, [(aT_out, 0), (h2T_out, 1), (exp_c, 1)])

            def expert(e, n, u):
                for b in range(NB):
                    k = e * NB + b + 1
                    act.wait_ge(S["e_up_mm"], k)
                    wait(act, S["e_act"], k - 2)
                    act.activation(ea[:, b % 2, 0, :], banks[b % 2][:, 0:3 * P], ACT.Exp, scale=-1.0).then_inc(S["e_exp"], 1)

            expert_loop(act, expert)

        @block.vector
        def _(dve):
            dve.wait_ge(S["tok_w_in"], 48)
            for c in range(PC):
                last = dve.tensor_scalar(wtg[:, c, :], wt[:, c, :], g1s[:, c:c + 1], None, ALU.mult)
            last.then_inc(S["wtg_ready"], 1)
            dve.wait_ge(S["small_in"], 32)
            dve.wait_ge(S["bias_mm"], 1)
            dve.tensor_tensor(tok_bias[:, :], banks[7][:, 0:D], brow[:, 0:D], ALU.add).then_inc(S["tok_bias_ready"], 1)
            dve.wait_ge(S["tok_bias_ready"], 1)
            dve.wait_ge(S["xi_exp"], 1)
            dve.wait_ge(S["consts_in"], 16)
            dve.reciprocal(xi[:, :], xi[:, :]).then_inc(S["xi_rec"], 1)
            dve.wait_ge(S["xi_rec"], 1)
            dve.tensor_tensor(xi[:, :], xi[:, :], k_of["decays"], ALU.mult).then_inc(S["xi_rec"], 1)
            dve.wait_ge(S["xi_rec"], 2)
            for h in range(HEADS):
                last = dve.scalar_tensor_tensor(out=bias[:, h, :], in0=k_of["dist"], scalar=xi[:, h:h + 1],
                                                in1=k_of["causal"], op0=ALU.mult, op1=ALU.add)
            last.then_inc(S["bias_set"], 1)

            def norm_stats(t, u, srcs, stats, mean_var, var_eps, eps, s_stats, s_var):
                for k, src in enumerate(srcs):
                    last = dve.bn_stats(stats[:, k, :] if len(srcs) > 1 else stats, src)
                last.then_inc(S[s_stats], 1)
                dve.wait_ge(S[s_stats], 2 * t + 1)
                settled(dve, S["steps_settled"])
                dve.bn_aggr(mean_var[:, u, :], stats.rearrange("p a b -> p (a b)") if len(srcs) > 1 else stats).then_inc(S[s_stats], 1)
                dve.wait_ge(S[s_stats], 2 * t + 2)
                dve.tensor_scalar(var_eps[:, u, :], mean_var[:, u, 1:2], eps, None, ALU.add).then_inc(S[s_var], 1)

            def x_norm(t, n, u):
                dve.wait_ge(x_in[u], 16 * (n + 1))
                norm_stats(t, u, [xs[:, u, 0:PATCH // 2], xs[:, u, PATCH // 2:]], st[:, u, :, :], mv, ve, TOK_EPS, "x_stats", "x_var")
                dve.wait_ge(S["x_rstd"], t + 1)
                dve.tensor_scalar(xs[:, u, :], xs[:, u, :], mv[:, u, 0:1], rs[:, u, :], ALU.subtract, ALU.mult).then_inc(S["x_normed"], 1)

            def h_norm(t, n, u):
                dve.wait_ge(S["tok_mm"], t + 1)
                dve.tensor_tensor(hl[:, u, :], banks[2 + u][:, 0:D], tok_bias[:, :], ALU.add).then_inc(S["h_sum"], 1)
                dve.wait_ge(S["h_sum"], t + 1)
                norm_stats(t, u, [hl[:, u, :]], st2[:, u, :], mv2, ve2, TOK_EPS, "h_stats", "h_var")
                dve.wait_ge(S["h_rstd"], t + 1)
                dve.tensor_scalar(hl[:, u, :], hl[:, u, :], mv2[:, u, 0:1], rs2[:, u, :], ALU.subtract, ALU.mult).then_inc(S["h_normed"], 1)
                dve.wait_ge(S["h_normed"], t + 1)
                dve.tensor_tensor(hl[:, u, :], hl[:, u, :], g2b, ALU.mult).then_inc(S["h_scaled"], 1)
                dve.wait_ge(S["h_scaled"], t + 1)
                wait(dve, h_stored[u], 16 * n)
                wait(dve, S["h_turned"], t - 1)
                dve.tensor_tensor(hs[:, u, :], hl[:, u, :], b2b, ALU.add).then_inc(S["h_ready"], 1)

            walk(dve, TILES, [(x_norm, 0), (h_norm, 1)])

            def per_image(ap):
                return ap.rearrange("p (a k) -> p a k", a=1).to_broadcast([P, CI, SEQ])

            def images(ap):
                return ap.rearrange("p (i k) -> p i k", i=CI)

            def chunk(ch):
                dve.wait_ge(S["qk_mm"], ch + 1)
                wait(dve, S["kexp_out"], ch)
                wait(dve, S["scores_mm"], ch * PAIRS)
                for n, (b, table, s) in enumerate(((2, "cos", "k_mul"), (3, "sin", "k_mul"), (0, "cos", "q_mul"), (1, "sin", "q_mul"))):
                    dve.tensor_tensor(images(tmp[:, n, :]), images(banks[b][:, 0:CT]), per_image(k_of[table]), ALU.mult).then_inc(S[s], 1)
                dve.wait_ge(S["k_mul"], 2 * ch + 2)
                dve.tensor_tensor(krot[:, :], tmp[:, 0, :], tmp[:, 1, :], ALU.add).then_inc(S["k_rot"], 1)
                dve.wait_ge(S["q_mul"], 2 * ch + 2)
                dve.tensor_tensor(qT[:, 0, :], tmp[:, 2, :], tmp[:, 3, :], ALU.add).then_inc(S["q_rot"], 1)

                def soft(p):
                    n = ch * PAIRS + p + 1
                    dve.wait_ge(S["scores_mm"], n)
                    wait(dve, S["exped"], n - 2)
                    for half in range(2):
                        last = dve.scalar_tensor_tensor(
                            out=sc[0:QP, p % 2, half * HALF:(half + 1) * HALF, :].rearrange("p h k -> p (h k)"),
                            in0=banks[half + 6 * (p % 2) if p % 2 == 0 else 6 + half][0:QP, 0:HALF * SEQ], scalar=DH ** -0.5,
                            in1=bias[0:QP, half * HALF:(half + 1) * HALF, :].rearrange("p h k -> p (h k)"),
                            op0=ALU.mult, op1=ALU.add)
                    last.then_inc(S["biased"], 1)
                    dve.wait_ge(S["biased"], n)
                    dve.tensor_reduce(mx[0:QP, p % 2, :], sc[0:QP, p % 2, :, :], AX.X, ALU.max).then_inc(S["maxed"], 1)

                def pT_out(p):
                    n = ch * PAIRS + p + 1
                    dve.wait_ge(S["p_turned"], n)
                    wait(dve, S["pv_mm"], n - 1)
                    dve.tensor_copy(pT[0:TRI * SEQ, 4, 0:QP], banks[3][0:TRI * SEQ, 0:QP])
                    dve.tensor_copy(pT[0:SEQ, 5, 0:QP], banks[3][0:SEQ, QP:2 * QP]).then_inc(S["pT_dve"], 1)

                def divide(p):
                    n = ch * PAIRS + p + 1
                    o = banks[4 + p % 2][0:QP, 0:HEADS * VW].rearrange("p (h w) -> p h w", w=VW)
                    dve.wait_ge(S["pv_mm"], n)
                    dve.reciprocal(si[0:QP, p % 2, :], o[:, :, DH]).then_inc(S["sum_inv"], 1)
                    dve.wait_ge(S["sum_inv"], n)
                    wait(dve, a_stored[p % 2], 32 * ((ch * PAIRS + p) // 2) if isinstance(ch, int) else 32 * (ch * (PAIRS // 2) + p // 2))
                    dve.tensor_tensor(ao[0:QP, p % 2, :].rearrange("p (h d) -> p h d", h=HEADS), o[:, :, 0:DH],
                                      si[0:QP, p % 2, :].rearrange("p (h a) -> p h a", a=1).to_broadcast([QP, HEADS, DH]),
                                      ALU.mult).then_inc(S["attended"], 1)

                soft(0)
                for p in range(PAIRS):
                    if p + 1 < PAIRS:
                        soft(p + 1)
                    pT_out(p)
                    divide(p)

            chunk_loop(dve, chunk)

            def r_norm(t, n, u):
                dve.wait_ge(S["wo_mm"], t + 1)
                dve.wait_ge(h_in[u], 16 * (n + 1))
                dve.tensor_tensor(hl[:, u, :], banks[1][:, 0:D], hi[:, u, :], ALU.add).then_inc(S["r_sum"], 1)
                dve.wait_ge(S["r_sum"], t + 1)
                norm_stats(t, u, [hl[:, u, :]], st2[:, u, :], mv2, ve, LN_EPS, "r_stats", "r_var")
                dve.wait_ge(S["r_rstd"], t + 1)
                wait(dve, S["h2_turned"], t - 1)
                wait(dve, S["acc_ready"], t - 1)
                dve.tensor_scalar(h2[:, u, :], hl[:, u, :], mv2[:, u, 0:1], rs[:, u, :], ALU.subtract, ALU.mult).then_inc(S["h2_ready"], 1)

            def route(t, n, u):
                r = rt[:, u, :, :]
                dve.wait_ge(S["gate_exp"], t + 1)
                dve.tensor_scalar(r[:, 1, :], r[:, 0, :], HUGE, 1.0, ALU.min, ALU.add).then_inc(S["gate_one"], 1)
                dve.wait_ge(S["gate_one"], t + 1)
                dve.reciprocal(r[:, 2, :], r[:, 1, :]).then_inc(S["gate_sig"], 1)
                dve.wait_ge(S["gate_sig"], t + 1)
                dve.tensor_tensor(r[:, 3, :], r[:, 2, :], gate_b, ALU.add).then_inc(S["score"], 1)
                dve.wait_ge(S["score"], t + 1)
                dve.tensor_reduce(gm[:, u, 0, :], r[:, 3, :].rearrange("p (g e) -> p g e", g=NGROUP), AX.X, ALU.max).then_inc(S["group_max"], 1)
                dve.wait_ge(S["group_max"], t + 1)
                settled(dve, S["steps_settled"])
                dve.max(gm[:, u, 1, :], gm[:, u, 0, :]).then_inc(S["group_top"], 1)
                dve.wait_ge(S["group_top"], t + 1)
                settled(dve, S["steps_settled"])
                dve.max_index(gi[:, u, :], gm[:, u, 1, :], gm[:, u, 0, :]).then_inc(S["group_idx"], 1)
                dve.wait_ge(S["group_idx"], t + 1)
                dve.tensor_tensor(geq[:, u, :, :], gi[:, u, 0:TOPG].rearrange("p (j a) -> p j a", a=1).to_broadcast([P, TOPG, NGROUP]),
                                  k_of["groups"].rearrange("p (a g) -> p a g", a=1).to_broadcast([P, TOPG, NGROUP]),
                                  ALU.is_equal).then_inc(S["group_eq"], 1)
                dve.wait_ge(S["group_eq"], t + 1)
                dve.tensor_reduce(gm[:, u, 0, :], geq[:, u, :, :].rearrange("p j g -> p g j"), AX.X, ALU.add).then_inc(S["group_mask"], 1)
                dve.wait_ge(S["group_mask"], t + 1)
                dve.tensor_tensor(r[:, 1, :].rearrange("p (g e) -> p g e", g=NGROUP), r[:, 3, :].rearrange("p (g e) -> p g e", g=NGROUP),
                                  gm[:, u, 0, :].rearrange("p (g a) -> p g a", a=1).to_broadcast([P, NGROUP, EXPERTS // NGROUP]),
                                  ALU.mult).then_inc(S["masked"], 1)
                dve.wait_ge(S["masked"], t + 1)
                settled(dve, S["steps_settled"])
                dve.max(t8[:, u, :], r[:, 1, :]).then_inc(S["top"], 1)
                dve.wait_ge(S["top"], t + 1)
                settled(dve, S["steps_settled"])
                dve.max_index(ti[:, u, :], t8[:, u, :], r[:, 1, :]).then_inc(S["top_idx"], 1)
                dve.tensor_reduce(tsum[:, u, 0:1], t8[:, u, 0:TOPK], AX.X, ALU.add).then_inc(S["top_sum"], 1)
                dve.wait_ge(S["top_sum"], t + 1)
                dve.tensor_scalar(tsum[:, u, 1:2], tsum[:, u, 0:1], 1e-8, None, ALU.add).then_inc(S["top_inv"], 1)
                dve.wait_ge(S["top_inv"], 2 * t + 1)
                dve.reciprocal(tsum[:, u, 0:1], tsum[:, u, 1:2]).then_inc(S["top_inv"], 1)
                dve.wait_ge(S["top_inv"], 2 * t + 2)
                dve.tensor_scalar(t8[:, u, :], t8[:, u, :], tsum[:, u, 0:1], None, ALU.mult).then_inc(S["top_w"], 1)
                dve.wait_ge(S["top_idx"], t + 1)
                dve.tensor_tensor(teq[:, u, :, :], ti[:, u, 0:TOPK].rearrange("p (j a) -> p j a", a=1).to_broadcast([P, TOPK, EXPERTS]),
                                  k_of["experts"].rearrange("p (a g) -> p a g", a=1).to_broadcast([P, TOPK, EXPERTS]),
                                  ALU.is_equal).then_inc(S["top_eq"], 1)
                dve.wait_ge(S["top_w"], t + 1)
                dve.wait_ge(S["top_eq"], t + 1)
                dve.tensor_tensor(teq[:, u, :, :], teq[:, u, :, :], t8[:, u, 0:TOPK].rearrange("p (j a) -> p j a", a=1).to_broadcast([P, TOPK, EXPERTS]),
                                  ALU.mult).then_inc(S["comb_part"], 1)
                dve.wait_ge(S["comb_part"], t + 1)
                dve.tensor_reduce(at(comb, t), teq[:, u, :, :].rearrange("p j g -> p g j"), AX.X, ALU.add).then_inc(S["comb_ready"], 1)

            def silu(t, n, u):
                s = su[:, u, :, :]
                dve.wait_ge(S["up_exp"], t + 1)
                dve.tensor_scalar(s[:, 1, :], s[:, 0, :], HUGE, 1.0, ALU.min, ALU.add).then_inc(S["up_one"], 1)
                dve.wait_ge(S["up_one"], t + 1)
                dve.reciprocal(s[:, 2, :], s[:, 1, :]).then_inc(S["up_inv"], 1)
                dve.wait_ge(S["up_inv"], t + 1)
                dve.tensor_tensor(s[:, 1, :], s[:, 2, :], banks[4 + u][:, 0:SHARED], ALU.mult).then_inc(S["up_silu"], 1)
                dve.wait_ge(S["up_silu"], t + 1)
                wait(dve, S["down_mm"], t - 1)
                dve.tensor_tensor(s[:, 3, :], s[:, 1, :], banks[4 + u][:, SHARED:2 * SHARED], ALU.mult).then_inc(S["up_ready"], 1)

            def add_shared(t, n, u):
                dve.wait_ge(S["down_mm"], t + 1)
                dve.tensor_tensor(at(acc, t), banks[6 + u][:, 0:D], h2[:, u, :], ALU.add).then_inc(S["acc_ready"], 1)

            walk(dve, TILES, [(add_shared, 2), (r_norm, 0), (silu, 1), (route, 1)])

            dve.wait_ge(S["acc_ready"], TILES)
            dve.wait_ge(S["comb_ready"], TILES)

            def expert(e, n, u):
                for b in range(NB + 1):
                    if b < NB:
                        k = e * NB + b + 1
                        a = ea[:, b % 2, :, :]
                        dve.wait_ge(S["e_exp"], k)
                        dve.tensor_scalar(a[:, 1, :], a[:, 0, :], HUGE, 1.0, ALU.min, ALU.add).then_inc(S["e_one"], 1)
                        dve.wait_ge(S["e_one"], k)
                        dve.reciprocal(a[:, 2, :], a[:, 1, :]).then_inc(S["e_inv"], 1)
                        dve.wait_ge(S["e_inv"], k)
                        dve.tensor_tensor(a[:, 1, :], a[:, 2, :], banks[b % 2][:, 0:3 * P], ALU.mult).then_inc(S["e_silu"], 1)
                        dve.wait_ge(S["e_silu"], k)
                        wait(dve, S["e_down_mm"], k - 2)
                        dve.tensor_tensor(a[:, 3, :], a[:, 1, :], banks[2 + b % 2][:, 0:3 * P], ALU.mult).then_inc(S["e_act"], 1)
                    if b:
                        k = e * NB + b
                        dve.wait_ge(S["e_down_mm"], k)
                        for c in range(3):
                            tile = 3 * (b - 1) + c
                            w = comb[:, tile, bass.ds(e, 1)] if not isinstance(e, int) else comb[:, tile, e:e + 1]
                            last = dve.scalar_tensor_tensor(
                                out=acc[:, tile, :], in0=banks[4 + 2 * ((b - 1) % 2) + c // 2][:, (c % 2) * D:(c % 2 + 1) * D],
                                scalar=w, in1=acc[:, tile, :], op0=ALU.mult, op1=ALU.add)
                        last.then_inc(S["e_added"], 1)

            expert_loop(dve, expert)

            dve.wait_ge(S["e_added"], EXPERTS * NB)

            def f_norm(t, n, u):
                norm_stats(t, u, [at(acc, t)], st2[:, u, :], mv2, ve, LN_EPS, "f_stats", "f_var")
                dve.wait_ge(S["f_rstd"], t + 1)
                wait(dve, o_stored[u], 16 * n)
                dve.tensor_scalar(of[:, u, :], at(acc, t), mv2[:, u, 0:1], rs[:, u, :], ALU.subtract, ALU.mult).then_inc(S["f_ready"], 1)

            walk(dve, TILES, [(f_norm, 0)])

        @block.tensor
        def _(pe):
            pe.wait_ge(S["tok_w_in"], 48)
            for c in range(PC):
                last = pe.matmul(banks[7][:, 0:D], b1s[:, c:c + 1].to_broadcast([P, P]), wt[:, c, :], start=(c == 0), stop=(c == PC - 1))
            last.then_inc(S["bias_mm"], 1)
            pe.wait_ge(S["wtg_ready"], 1)
            pe.wait_ge(S["consts_in"], 16)
            pe.wait_ge(S["weights_in"], 16 * 5)
            pe.wait_ge(S["tok_bias_ready"], 1)

            def turn_x(t, n, u):
                pe.wait_ge(S["x_normed"], t + 1)
                wait(pe, S["xT_out"], t)
                for c in range(PC):
                    last = pe.transpose(banks[c // 3][:, (c % 3) * P:(c % 3 + 1) * P], xs[:, u, c * P:(c + 1) * P], ident)
                last.then_inc(S["x_turned"], 1)

            def tok(t, n, u):
                pe.wait_ge(S["xT_out"], t + 1)
                wait(pe, S["h_sum"], t - 1)
                for c in range(PC):
                    last = pe.matmul(banks[2 + u][:, 0:D], xT[:, u, c, :], wtg[:, c, :], start=(c == 0), stop=(c == PC - 1))
                last.then_inc(S["tok_mm"], 1)

            def turn_h(t, n, u):
                pe.wait_ge(S["h_ready"], t + 1)
                wait(pe, S["hT_out"], t - 1)
                for c in range(DC):
                    last = pe.transpose(banks[4 + u][:, c * P:(c + 1) * P], hs[:, u, c * P:(c + 1) * P], ident)
                last.then_inc(S["h_turned"], 1)

            def values(t, n, u):
                pe.wait_ge(S["hT_out"], t + 1)
                wait(pe, S["v_out"], t - 1)
                for c in range(DC):
                    last = pe.matmul(banks[6 + u][:, 0:D], hTs[:, u, c, :], wv[:, c, :], start=(c == 0), stop=(c == DC - 1))
                last.then_inc(S["v_mm"], 1)

            walk(pe, TILES, [(turn_x, 0), (turn_h, 2), (tok, 1), (values, 2)])

            pe.wait_ge(S["hT_kept"], TILES)
            pe.wait_ge(S["v_out"], TILES)
            pe.wait_ge(S["h_sum"], TILES)
            pe.wait_ge(S["xT_out"], TILES)
            pe.wait_ge(S["v_ones"], 1)

            def chunk(ch):
                def tokens(c):
                    return hT[:, c, ch * CT:(ch + 1) * CT] if isinstance(ch, int) else hT[:, c, bass.ds(ch * CT, CT)]

                wait(pe, S["biased"], ch * PAIRS)
                wait(pe, S["pT_dve"], ch * PAIRS)
                wait(pe, S["pT_act"], ch * PAIRS)
                for b, w, half in ((2, wk, 0), (3, wks, 0), (7, wk, 1), (0, wq, 0), (1, wqs, 0), (6, wq, 1)):
                    for c in range(DC):
                        last = pe.matmul(banks[b][:, 0:CT], w[:, c, half * P:(half + 1) * P], tokens(c), start=(c == 0), stop=(c == DC - 1))
                last.then_inc(S["qk_mm"], 1)
                pe.wait_ge(S["q_rot"], ch + 1)
                pe.wait_ge(S["q_out"], ch + 1)
                pe.wait_ge(S["kexp_out"], ch + 1)

                def scores(p):
                    n = ch * PAIRS + p + 1
                    wait(pe, S["biased"], n - 2)
                    for half in range(2):
                        b = half if p % 2 == 0 else 6 + half
                        for i in range(2):
                            img = 2 * p + i
                            m = 64 if i == 0 else SEQ
                            last = pe.matmul(banks[b][64 * i:64 * i + m, 0:HALF * SEQ], qT[:, half, img * SEQ:img * SEQ + m],
                                             kexp[:, half, :, img * SEQ:(img + 1) * SEQ], start=True, stop=True)
                    last.then_inc(S["scores_mm"], 1)

                def turn(p):
                    n = ch * PAIRS + p + 1
                    pe.wait_ge(S["exped"], n)
                    wait(pe, S["pT_act"], n - 1)
                    wait(pe, S["pT_dve"], n - 1)
                    for g in range(GROUPS):
                        w = min(TRI, HEADS - TRI * g) * SEQ
                        b, k = (2, g) if g < 4 else (3, g - 4)
                        last = pe.transpose(banks[b][0:w, k * QP:(k + 1) * QP], pr[0:QP, p % 2, g * TRI * SEQ:g * TRI * SEQ + w], ident[0:QP, 0:QP])
                    last.then_inc(S["p_turned"], 1)

                def attend(p):
                    n = ch * PAIRS + p + 1
                    pe.wait_ge(S["pT_act"], n)
                    pe.wait_ge(S["pT_dve"], n)
                    pe.wait_ge(S["v_masked"], ch + 1)
                    wait(pe, S["attended"], n - 2)
                    for i in range(2):
                        m = 64 if i == 0 else SEQ
                        for g in range(GROUPS):
                            heads = min(TRI, HEADS - TRI * g)
                            k = heads * SEQ
                            last = pe.matmul(banks[4 + p % 2][64 * i:64 * i + m, g * TRI * VW:(g * TRI + heads) * VW],
                                             pT[0:k, g, 64 * i:64 * i + m],
                                             vbd[0:k, 2 * p + i, g * TRI:g * TRI + heads, :].rearrange("p h w -> p (h w)"),
                                             start=True, stop=True)
                    last.then_inc(S["pv_mm"], 1)

                scores(0)
                for p in range(PAIRS):
                    if p + 1 < PAIRS:
                        scores(p + 1)
                    turn(p)
                    attend(p)

            chunk_loop(pe, chunk)

            pe.wait_ge(S["late_in"], 16 * 4)
            pe.wait_ge(S["attended"], CHUNKS * PAIRS)
            pe.wait_ge(S["biased"], CHUNKS * PAIRS)

            def turn_a(t, n, u):
                pe.wait_ge(a_in[u], 16 * (n + 1))
                wait(pe, S["aT_out"], t)
                for c in range(DC):
                    last = pe.transpose(banks[0][:, c * P:(c + 1) * P], ai[:, u, c * P:(c + 1) * P], ident)
                last.then_inc(S["a_turned"], 1)

            def project(t, n, u):
                pe.wait_ge(S["aT_out"], t + 1)
                wait(pe, S["r_sum"], t)
                for c in range(DC):
                    last = pe.matmul(banks[1][:, 0:D], aT[:, u, c, :], wo[:, c, :], start=(c == 0), stop=(c == DC - 1))
                last.then_inc(S["wo_mm"], 1)

            def turn_h2(t, n, u):
                pe.wait_ge(S["h2_ready"], t + 1)
                wait(pe, S["h2T_out"], t)
                for c in range(DC):
                    last = pe.transpose(banks[2][:, c * P:(c + 1) * P], h2[:, u, c * P:(c + 1) * P], ident)
                last.then_inc(S["h2_turned"], 1)

            def gate(t, n, u):
                pe.wait_ge(S["h2T_out"], t + 1)
                wait(pe, S["gate_exp"], t)
                for c in range(DC):
                    last = pe.matmul(banks[3][:, 0:EXPERTS], h2Ts[:, u, c, :], gw[:, c, :], start=(c == 0), stop=(c == DC - 1))
                last.then_inc(S["gate_mm"], 1)
                wait(pe, S["up_ready"], t - 1)
                for m in range(2 * SHARED // P):
                    for c in range(DC):
                        last = pe.matmul(banks[4 + u][:, m * P:(m + 1) * P], wsh[:, c, m * P:(m + 1) * P], h2Ts[:, u, c, :],
                                         start=(c == 0), stop=(c == DC - 1))
                last.then_inc(S["up_mm"], 1)

            def down(t, n, u):
                pe.wait_ge(S["up_ready"], t + 1)
                wait(pe, S["acc_ready"], t - 1)
                for c in range(SHARED // P):
                    last = pe.matmul(banks[6 + u][:, 0:D], su[:, u, 3, c * P:(c + 1) * P], dsh[:, c, :], start=(c == 0), stop=(c == SHARED // P - 1))
                last.then_inc(S["down_mm"], 1)

            walk(pe, TILES, [(down, 2), (turn_a, 0), (project, 0), (turn_h2, 1), (gate, 1)])

            pe.wait_ge(S["h2T_kept"], TILES)
            pe.wait_ge(S["acc_ready"], TILES)
            pe.wait_ge(S["r_sum"], TILES)

            def expert(e, n, u):
                pe.wait_ge(w_in[u], 16 * (n + 1))
                for b in range(NB + 1):
                    if b < NB:
                        k = e * NB + b + 1
                        wait(pe, S["e_act"], k - 2)
                        for m in range(2):
                            for c in range(DC):
                                last = pe.matmul(banks[2 * m + b % 2][:, 0:3 * P], moe[:, u, (m * DC + c) * P:(m * DC + c + 1) * P],
                                                 hT[:, c, b * 3 * P:(b + 1) * 3 * P], start=(c == 0), stop=(c == DC - 1))
                        last.then_inc(S["e_up_mm"], 1)
                    if b:
                        k = e * NB + b
                        pe.wait_ge(S["e_act"], k)
                        wait(pe, S["e_added"], k - 2)
                        for c in range(3):
                            last = pe.matmul(banks[4 + 2 * ((b - 1) % 2) + c // 2][:, (c % 2) * D:(c % 2 + 1) * D],
                                             ea[:, (b - 1) % 2, 3, c * P:(c + 1) * P], moe[:, u, 2 * D:3 * D], start=True, stop=True)
                        last.then_inc(S["e_down_mm"], 1)

            expert_loop(pe, expert)


def shape_constants():
    import numpy as np
    c = np.zeros((P, CONST_W), np.float32)

    def put(name, value):
        a, w = CONST_AT[name]
        c[:, a:a + w] = value

    p = np.arange(P)[:, None]
    put("ident", p == np.arange(P)[None])
    put("k_heads", p // DH == np.arange(HALF)[None])
    put("v_heads", (p < TRI * SEQ) & (np.arange(HEADS)[None] % TRI == p // SEQ))
    pos = np.arange(SEQ, dtype=np.float32)
    inv = np.float32(10000.0) ** (-(np.arange(0, DH, 2, dtype=np.float32) / np.float32(DH)))
    theta = (pos[:, None] * inv[None, :]).astype(np.float32)
    d = np.arange(P) % DH
    put("cos", np.cos(theta).T[d // 2])
    put("sin", np.sin(theta).T[d // 2] * np.where(d % 2 == 0, -1.0, 1.0)[:, None])
    q = np.where(p < SEQ, p, p - 64)
    live = (q >= 0) & (q < SEQ)
    k = np.arange(SEQ)[None]
    put("causal", np.where(live & (k > q), MASKED, 0.0))
    put("dist", np.where(live, -np.abs(q - k), 0.0))
    put("decays", np.array([h & 1 for h in HEAD_ORDER], np.float32)[None])
    put("experts", np.arange(EXPERTS)[None])
    put("groups", np.arange(NGROUP)[None])
    return c


def kernel(**inputs):
    import numpy as np
    import concourse.bacc as bacc
    from concourse.bass_utils import run_bass_kernel_spmd

    g = {k: np.asarray(v) for k, v in inputs.items()}

    def chunks(w):
        return np.ascontiguousarray(w.reshape(w.shape[0] // P, P, -1).transpose(1, 0, 2))

    x = g["x"]
    b, ch, hh, ww = x.shape
    patches = x.reshape(b, ch, hh // 16, 16, ww // 16, 16).transpose(0, 2, 4, 3, 5, 1).reshape(TOK, PATCH)
    wqkv = g["L0_attn_w_qkv"].reshape(D, 3, HEADS, DH)[:, :, HEAD_ORDER]
    swap = np.arange(DH) ^ 1
    w_q, w_k, w_v = (wqkv[:, i].reshape(D, D) for i in range(3))
    w_qs, w_ks = (wqkv[:, i, :HALF][:, :, swap].reshape(D, P) for i in range(2))
    w_o = g["L0_attn_w_o"].reshape(HEADS, DH, D)[HEAD_ORDER].reshape(D, D)
    eg, eu, ed = (g[f"L0_ffn_{n}_w"].transpose(0, 2, 1) for n in ("eg", "eu", "ed"))
    w_moe = np.concatenate([eg.reshape(EXPERTS, DC, P, INTER).transpose(0, 2, 1, 3).reshape(EXPERTS, P, D),
                            eu.reshape(EXPERTS, DC, P, INTER).transpose(0, 2, 1, 3).reshape(EXPERTS, P, D), ed], axis=2)
    arrays = {
        "patches": patches, "w_tok": chunks(g["L0_tok_W_mlp"]),
        "rows": np.concatenate([g["L0_tok_b_mlp"], g["L0_tok_g2"], g["L0_tok_b2"], g["L0_ffn_gate_bias"]])[None],
        "b1_col": g["L0_tok_b1"].reshape(PC, P).T, "g1_col": g["L0_tok_g1"].reshape(PC, P).T,
        "w_q": chunks(w_q), "w_k": chunks(w_k), "w_qs": chunks(w_qs), "w_ks": chunks(w_ks), "w_v": chunks(w_v),
        "w_o": chunks(w_o), "gate_w": chunks(g["L0_ffn_gate_w"].T), "log_xi": g["L0_attn_log_xi"][HEAD_ORDER][None],
        "w_shared": chunks(np.concatenate([g["L0_ffn_sg_w"], g["L0_ffn_su_w"]]).T),
        "d_shared": chunks(g["L0_ffn_sd_w"].T), "w_moe": w_moe, "consts": shape_constants(),
    }
    nc = bacc.Bacc("TRN2", target_bir_lowering=False, num_devices=1)
    aps = {}
    for name, a in arrays.items():
        arrays[name] = np.ascontiguousarray(a)
        aps[name] = nc.dram_tensor(name, a.shape, mybir.dt.from_np(a.dtype), kind="ExternalInput").ap()
    out = nc.dram_tensor("result", (TOK, D), F32, kind="ExternalOutput").ap()
    program(nc, out=out, **aps)
    r = run_bass_kernel_spmd(nc, [arrays], core_ids=[0])
    return r.results[0]["result"].reshape(IMAGES, SEQ, D)
```

```python
from contextlib import ExitStack

import concourse.bass as bass
from concourse import mybir

F32 = mybir.dt.float32
U32 = mybir.dt.uint32
I32 = mybir.dt.int32
ALU = mybir.AluOpType
ACT = mybir.ActivationFunctionType
AX = mybir.AxisListType
ENG = mybir.EngineType

P = 128
IMAGES, SEQ = 64, 36
TOK = IMAGES * SEQ
TILES = TOK // P
PATCH = 768
PC = PATCH // P
D = 256
DC = D // P
HEADS, DH = 16, 16
HALF = HEADS // 2
CI = 8
CHUNKS = IMAGES // CI
CT = CI * SEQ
PAIRS = CI // 2
QP = 64 + SEQ
TRI = 3
GROUPS = -(-HEADS // TRI)
SETUP = PAIRS
VW = DH + 1
EXPERTS, INTER = 64, 128
NGROUP, TOPG, TOPK = 8, 4, 6
SHARED = 256
TOK_EPS = -1e-05
LN_EPS = 1e-05
MASKED = -1e30
ROW = D + 2
CAP = TOK + P
SPARE = EXPERTS * CAP
A_SLOTS = 3
SUMS = 4
POOL_PADS = 20
E_SLOTS = 4
E_TILES = -(-((TOK * TOPK + EXPERTS * (P - 1)) // P) // SUMS) * SUMS
W_SLOTS = 8
T_OFF, T_EXPERT, T_SLOT, T_LOAD, T_COLS = 0, 1, 2, 3, 4

CONST_AT = {}
_n = 0
for _name, _w in (("ident", P), ("k_heads", HALF), ("v_heads", HEADS), ("cos", SEQ), ("sin", SEQ),
                  ("causal", SEQ), ("dist", SEQ), ("decays", HEADS), ("experts", EXPERTS), ("groups", NGROUP),
                  ("before", P), ("ones", P), ("region", EXPERTS), ("tile", 2), ("pad_row", ROW)):
    CONST_AT[_name] = (_n, _w)
    _n += _w
CONST_W = _n
SHARED_W = 2 * HALF * CT + CI * D + CI * HEADS * VW + 4 * CT
HEAD_ORDER = [h for h in range(HEADS) if h >> 1 & 1] + [h for h in range(HEADS) if not h >> 1 & 1]


def wait(eng, sem, value):
    if isinstance(value, int) and value <= 0:
        return
    eng.wait_ge(sem, value)


def settled(eng, sem):
    eng.sem_inc(sem, 1)


CLAMPED = "the table's last step clamps every column to its range"


def entries(nc, engine, row):
    _, (off, expert, slot, load) = nc.values_load_multi_w_load_instructions(
        row, engines=(engine,), min_val=0, max_val=SPARE, skip_runtime_bounds_check_because=CLAMPED)

    def most(value, top):
        return nc.s_assert_within(value, 0, top, skip_runtime_bounds_check_because=CLAMPED)

    return off, most(expert, EXPERTS - 1), most(slot, W_SLOTS - 1), most(load, 1)


def walk(eng, tiles, steps, slots=2, peel=0, begin=None):
    lag = max(l for _, l in steps)
    head = max(peel, slots * -(-(slots + lag) // slots))
    loops = (tiles - head) // slots

    def at(s, base, first, last):
        for step, l in steps:
            slot = (s - l) % slots
            visit = base + (s - l - slot) // slots
            if first and visit < 0 or last and visit * slots + slot >= tiles:
                continue
            step(visit * slots + slot, visit, slot)

    for s in range(head):
        at(s, 0, True, False)
    with eng.Fori(head // slots, head // slots + loops) as visit:
        if begin:
            begin(visit)
        for s in range(slots):
            at(s, visit, False, False)
    for s in range(head + slots * loops, tiles + lag):
        at(s, 0, False, True)


def program(nc, patches, w_tok, rows, b1_col, g1_col, w_q, w_k, w_qs, w_ks, w_v, w_o, gate_w, log_xi,
            w_shared, d_shared, w_moe, consts, out):
    h_dram = nc.dram_tensor("h_rows", (TOK, D), F32).ap()
    v_dram = nc.dram_tensor("v_rows", (TOK, D), F32).ap()
    a_dram = nc.dram_tensor("attended_rows", (TOK, D), F32).ap()
    sent = nc.dram_tensor("dispatched_rows", (SPARE + P, ROW), F32).ap()
    sums = nc.dram_tensor("sums", (SUMS * (TOK + P), D), F32).ap()
    table_dram = nc.dram_tensor("tile_table", (2 * P, T_COLS), I32).ap()

    with ExitStack() as ctx:
        def sb(name, shape, dt=F32):
            return ctx.enter_context(nc.sbuf_tensor(name, shape, dt))

        def sem(name):
            return ctx.enter_context(nc.semaphore(name))

        banks = [ctx.enter_context(nc.psum_tensor(f"bank{i}", [P, 512], F32)) for i in range(8)]

        cst = sb("cst", [P, CONST_W])
        k_of = {n: cst[:, a:a + w] for n, (a, w) in CONST_AT.items()}
        ident = k_of["ident"]
        wt = sb("wt", [P, PC, D])
        wtg = sb("wtg", [P, PC, D])
        g1s = sb("g1s", [P, PC])
        b1s = sb("b1s", [P, PC])
        brow = sb("brow", [P, 3 * D + EXPERTS])
        tok_bias = sb("tok_bias", [P, D])
        g2b, b2b = brow[:, D:2 * D], brow[:, 2 * D:3 * D]
        gate_b = brow[:, 3 * D:]
        wq, wk, wqs, wks = sb("wq", [P, DC, D]), sb("wk", [P, DC, D]), sb("wqs", [P, DC, P]), sb("wks", [P, DC, P])
        wv, wo = sb("wv", [P, DC, D]), sb("wo", [P, DC, D])
        gw = sb("gw", [P, DC, EXPERTS])
        wsh = sb("wsh", [P, DC, 2 * SHARED])
        dsh = sb("dsh", [P, SHARED // P, D])
        xi = sb("xi", [P, HEADS])
        bias = sb("bias", [P, HEADS, SEQ])
        minus_half = sb("minus_half", [P, 1])
        hT = sb("hT", [P, DC, TOK])
        big = ctx.enter_context(ExitStack())

        names = ("steps_settled pool_settled pe_settled sp_settled consts_in weights_in tok_w_in small_in late_in "
                 "half_set wtg_ready bias_mm tok_bias_ready xi_exp xi_rec bias_set "
                 "x_stats x_var x_rstd x_normed x_turned xT_out tok_mm "
                 "h_sum h_stats h_var h_rstd h_normed h_scaled h_ready h_turned hT_out v_mm v_out "
                 "qk_mm k_mul q_mul k_rot q_rot kexp_out q_out v_masked p_zero "
                 "scores_mm biased maxed shifted exped p_turned pT_act pT_dve pv_mm sum_inv attended "
                 "a_turned aT_out wo_mm r_sum r_stats r_var r_rstd h2_ready h2_turned h2T_out "
                 "gate_mm gate_sig score route_steps "
                 "top_inv h2_copied chosen ranked place "
                 "rows_ready counted counts_start zeros_set ids_made kept_h2 "
                 "tab slots_set table_set table_out table_in ends_out pads_out pads_out_pool sums_zeroed "
                 "sh_up_mm sh_silu sh_act sh_down_mm sh_added "
                 "x_turned_e xT_out_e meta up_mm silu act_ready act_turned actT_out down_mm y_ready "
                 "f_pairs f_first f_pool f_sum f_stats f_var f_rstd f_ready").split()
        S = {n: sem(n) for n in names}
        x_in, h_stored, v_stored = ([sem(f"{n}{u}") for u in range(A_SLOTS)] for n in ("x_in", "h_stored", "v_stored"))
        vrep_in, a_stored = [sem(f"vrep_in{r}") for r in range(PAIRS)], [sem(f"a_stored{u}") for u in range(2)]
        a_in, h_in = ([sem(f"{n}{u}") for u in range(2)] for n in ("a_in", "h_in"))
        o_stored, sums_in = ([sem(f"{n}{u}") for u in range(E_SLOTS)] for n in ("o_stored", "sums_in"))
        rows_sent = [sem(f"rows_sent{u}") for u in range(2)]
        w_in, rows_in, y_added = ([sem(f"{n}{u}") for u in range(SUMS)] for n in ("w_in", "rows_in", "y_added"))

        hl = sb("hl", [P, A_SLOTS, D])
        st2 = sb("st2", [P, A_SLOTS, 6])
        mv2 = sb("mv2", [P, A_SLOTS, 2])
        ve = sb("ve", [P, A_SLOTS, 1])
        rs = sb("rs", [P, A_SLOTS, 1])
        st = sb("st", [P, A_SLOTS, 2, 6])
        mv = sb("mv", [P, A_SLOTS, 2])
        ve2 = sb("ve2", [P, A_SLOTS, 1])
        rs2 = sb("rs2", [P, A_SLOTS, 1])
        qT = sb("qT", [P, 2, 2, CT])
        krot = sb("krot", [P, CT])
        shared = sb("shared", [P, SHARED_W])

        def carve(start, shape, letters):
            size = 1
            for n in shape:
                size *= n
            flat = shared[:, start:start + size]
            names = letters.split()
            return flat.rearrange(f"p ({letters}) -> p {letters}", **dict(zip(names[1:], shape[1:]))), start + size

        xs, _n = carve(0, [A_SLOTS, PATCH], "u n")
        xT, _n = carve(_n, [A_SLOTS, PC, P], "u c n")
        hs, _n = carve(_n, [A_SLOTS, D], "u n")
        vs, _n = carve(_n, [A_SLOTS, D], "u n")
        hTs, _n = carve(_n, [A_SLOTS, DC, P], "u c n")
        assert _n <= SHARED_W
        kexp0, _n = carve(0, [2, HALF, CT], "a h t")
        vrep, _n = carve(_n, [PAIRS, 2, D], "r i d")
        vbd, _n = carve(_n, [PAIRS, 2, HEADS, VW], "r i h w")
        tmp, _n = carve(_n, [4, CT], "n t")
        assert _n <= SHARED_W
        sc = sb("sc", [P, 2, HEADS, SEQ])
        mx = sb("mx", [P, 2, HEADS])
        pr = sb("pr", [P, 2, HEADS * SEQ])
        pT = sb("pT", [P, 2, GROUPS, P])
        si = sb("si", [P, 2, HEADS])
        ao = sb("ao", [P, 2, D])
        ai = sb("ai", [P, 2, D])
        hi = sb("hi", [P, 2, D])
        aT = sb("aT", [P, 2, DC, P])
        h2Ts = sb("h2Ts", [P, 2, DC, P])
        h2 = sb("h2", [P, 2, D])
        dsp = sb("dsp", [P, 2, TOPK, ROW])
        rt = sb("rt", [P, 2, 3, EXPERTS])
        gm = sb("gm", [P, 2, 2, NGROUP])
        gi = sb("gi", [P, 2, NGROUP], U32)
        geq = sb("geq", [P, 2, TOPG, NGROUP])
        t8 = sb("t8", [P, 2, 8])
        ti = sb("ti", [P, 2, 8], U32)
        teq = sb("teq", [P, 2, TOPK, EXPERTS])
        tpl = sb("tpl", [P, 2, TOPK, EXPERTS])
        tsum = sb("tsum", [P, 2, 2])
        chosen = sb("chosen", [P, 2, EXPERTS])
        place = sb("place", [P, 2, EXPERTS])
        counts = sb("counts", [P, 2, EXPERTS])
        dest = sb("dest", [P, 2, TOPK])
        desti = sb("desti", [P, 2, TOPK], U32)
        ids = sb("ids", [P, TILES], U32)
        zeros = sb("zeros", [P, D])
        acc = sb("acc", [P, TILES, D])
        kexp = [kexp0, acc[:, :, :].rearrange("p t d -> p (t d)")[:, 0:2 * HALF * CT].rearrange("p (a h t) -> p a h t", a=2, h=HALF)]
        sha, _n = carve(W_SLOTS * 3 * D, [SHARED // P, 2, 3 * P], "m a n")
        tb = sb("tb", [P, 9, EXPERTS])
        tbi = sb("tbi", [P, EXPERTS], I32)
        tv = sb("tv", [P, 2, 8])
        tvi = sb("tvi", [P, 2, T_COLS], I32)
        ends = sb("ends", [1, EXPERTS], I32)
        table = sb("table", [1, 2 * P * T_COLS], I32)
        slot_row = sb("slot_row", [1, 2 * P], I32)
        moe, _n = carve(0, [W_SLOTS, 3 * D], "w n")
        xe = sb("xe", [P, SUMS, ROW])
        xeT = sb("xeT", [P, 2, DC, P])
        meta = sb("meta", [P, SUMS, 2])
        ids2 = sb("ids2", [P, SUMS], U32)
        sg = sb("sg", [P, 2, INTER])
        ae = sb("ae", [P, 2, INTER])
        aeT = sb("aeT", [P, 2, P])
        ye = sb("ye", [P, SUMS, D])
        si4, _n = carve(0, [E_SLOTS, SUMS, D], "u k d")
        assert _n <= SHARED_W
        of, _n = carve(_n, [E_SLOTS, D], "u d")

        block = ctx.enter_context(nc.Block())

        def rows_of(dram, t):
            return dram[bass.ds(t * P, P), :] if not isinstance(t, int) else dram[t * P:(t + 1) * P, :]

        def part_of(dram, t, rows):
            return dram[bass.ds(t * rows, rows), :] if not isinstance(t, int) else dram[t * rows:(t + 1) * rows, :]

        def cols_of(ap, t):
            return ap[:, :, bass.ds(t * P, P)] if not isinstance(t, int) else ap[:, :, t * P:(t + 1) * P]

        def at(ap, t):
            return ap[:, bass.ds(t, 1), :].rearrange("p a b -> p (a b)") if not isinstance(t, int) else ap[:, t, :]

        def in_slot(u):
            return (TILES - u + E_SLOTS - 1) // E_SLOTS

        def walk_pairs(eng, steps):
            walk(eng, IMAGES // 2, steps, 2 * PAIRS)

        def pads_out(eng, engine, first, past, signal):
            with eng.Fori(first // 4, past // 4) as e:
                _, some_ends = nc.values_load_multi_w_load_instructions(
                    ends[0:1, bass.ds(4 * e, 4)], engines=(engine,), min_val=0, max_val=SPARE - P,
                    skip_runtime_bounds_check_because="an expert has at most TOK rows in its region of TOK + P")
                for end in some_ends:
                    eng.dma_start(sent[bass.ds(end, P), :], k_of["pad_row"]).then_inc(S[signal], 16)

        def table_row(n):
            return table[0:1, n * T_COLS:(n + 1) * T_COLS] if isinstance(n, int) else table[0:1, bass.ds(n * T_COLS, T_COLS)]

        BLOCKS = TILES // 3

        @block.sync
        def _(sp):
            sp.dma_start(cst[:, :], consts).then_inc(S["consts_in"], 16)
            sp.dma_start(g1s[:, :], g1_col).then_inc(S["tok_w_in"], 16)
            sp.dma_start(b1s[:, :], b1_col).then_inc(S["tok_w_in"], 16)
            sp.dma_start(wt[:, :, :], w_tok).then_inc(S["tok_w_in"], 16)

            def load_x(t, n, u):
                wait(sp, S["x_turned"], t - A_SLOTS + 1)
                sp.dma_start(xs[:, u, :], rows_of(patches, t)).then_inc(x_in[u], 16)
                if isinstance(t, int) and t == 0:
                    sp.dma_start(brow[:, :], rows.to_broadcast([P, 3 * D + EXPERTS])).then_inc(S["small_in"], 16)
                    sp.dma_start(xi[:, :], log_xi.to_broadcast([P, HEADS])).then_inc(S["small_in"], 16)
                if isinstance(t, int) and t == 1:
                    for dst, src in ((wv, w_v), (wq, w_q), (wk, w_k), (wqs, w_qs), (wks, w_ks)):
                        sp.dma_start(dst[:, :, :], src).then_inc(S["weights_in"], 16)
                if isinstance(t, int) and t == 2 * A_SLOTS:
                    for dst, src in ((wo, w_o), (gw, gate_w), (wsh, w_shared), (dsh, d_shared)):
                        sp.dma_start(dst[:, :, :], src).then_inc(S["late_in"], 16)

            def store_h(t, n, u):
                sp.wait_ge(S["h_ready"], t + 1)
                sp.dma_start(rows_of(h_dram, t), hs[:, u, :]).then_inc(h_stored[u], 16)

            walk(sp, TILES, [(load_x, 0), (store_h, 4)], A_SLOTS)
            for u in range(A_SLOTS):
                sp.wait_ge(v_stored[u], 16 * (TILES // A_SLOTS))
                sp.wait_ge(h_stored[u], 16 * (TILES // A_SLOTS))
            sp.wait_ge(S["zeros_set"], 1)

            def load_v(t, n, u):
                wait(sp, S["v_masked"], t - PAIRS + 1)
                for c in range(TRI):
                    sp.dma_start(vrep[c * SEQ:(c + 1) * SEQ, u % PAIRS, :, :],
                                 part_of(v_dram, t, 2 * SEQ).rearrange("(i k) d -> k i d", k=SEQ)).then_inc(vrep_in[u % PAIRS], 16)

            def zero_sums(t, n, u):
                rows = SUMS * (TOK + P) // (IMAGES // 2)
                sp.dma_start(part_of(sums, t, rows).rearrange("(t p) d -> p t d", t=4),
                             zeros[0:rows // 4, :].rearrange("p (a d) -> p a d", a=1).to_broadcast([rows // 4, 4, D])).then_inc(S["sums_zeroed"], 16)

            def store_a(t, n, u):
                sp.wait_ge(S["attended"], t + 1)
                for i in range(2):
                    sp.dma_start(part_of(a_dram, 2 * t + i, SEQ), ao[64 * i:64 * i + SEQ, u % 2, :]).then_inc(a_stored[u % 2], 16)

            def load_c(t, n, u):
                if isinstance(t, int) and t < 2:
                    for k in range(2):
                        sp.wait_ge(a_stored[k], 32 * -(-(t + 1) * P // (4 * SEQ)))
                wait(sp, S["a_turned"], t - 1)
                sp.dma_start(ai[:, u, :], rows_of(a_dram, t)).then_inc(a_in[u], 16)
                wait(sp, S["r_sum"], t - 1)
                sp.dma_start(hi[:, u, :], rows_of(h_dram, t)).then_inc(h_in[u], 16)

            def store_last(t, n, u):
                if isinstance(t, int) and t == IMAGES // 2 - 1:
                    load_c(0, 0, 0)
                    load_c(1, 0, 1)
                store_a(t, n, u)

            walk_pairs(sp, [(load_v, 0), (zero_sums, 0), (store_last, SETUP + 2)])
            for u in range(2):
                sp.wait_ge(a_stored[u], 16 * 2 * CHUNKS * PAIRS // 2)

            def load_rest(t, n, u):
                if not isinstance(t, int) or t >= 2:
                    load_c(t, n, u)

            walk(sp, TILES, [(load_rest, 0)])

            sp.wait_ge(S["ends_out"], 1)
            for u in range(2):
                sp.wait_ge(rows_sent[u], 16 * TOPK * (TILES // 2))
            sp.dma_start(sent[SPARE:SPARE + P, :], k_of["pad_row"]).then_inc(S["pads_out"], 16)
            pads_out(sp, ENG.SP, POOL_PADS, EXPERTS, "pads_out")
            sp.wait_ge(S["table_in"], 16)
            sp.wait_ge(S["pads_out"], 16 * (EXPERTS - POOL_PADS + 1))
            sp.wait_ge(S["pads_out_pool"], 16 * POOL_PADS)
            sp.wait_ge(S["sums_zeroed"], 16 * (IMAGES // 2))

            def load_e(n, v, u):
                off, expert, slot, load = entries(nc, ENG.SP, table_row(n))
                wait(sp, S["meta"], n - SUMS + 1)
                wait(sp, S["x_turned_e"], n - SUMS + 1)
                settled(sp, S["sp_settled"])
                sp.dma_start(xe[:, u, :], sent[bass.ds(off, P), :]).then_inc(rows_in[u], 16)
                wait(sp, S["down_mm"], n - W_SLOTS + 1)
                settled(sp, S["sp_settled"])
                wait(sp, w_in[u], 16 * v)
                settled(sp, S["sp_settled"])
                sp.dma_start(moe[:, bass.ds(slot, 1), :].rearrange("p a n -> p (a n)"),
                             w_moe[bass.ds(expert, 1), :, :].rearrange("a p n -> (a p) n"), cond=load).then_inc(w_in[u], 16)

            walk(sp, E_TILES, [(load_e, 0)], SUMS, peel=W_SLOTS)

            for k in range(SUMS):
                sp.wait_ge(y_added[k], 16 * (E_TILES // SUMS))

            def load_sums(t, n, u):
                wait(sp, S["f_sum"], t - E_SLOTS + 1)
                each = sums.rearrange("(k n) d -> n k d", k=SUMS)
                rows = each[bass.ds(t * P, P), :, :] if not isinstance(t, int) else each[t * P:(t + 1) * P, :, :]
                sp.dma_start(si4[:, u, :, :], rows).then_inc(sums_in[u], 16)

            walk(sp, TILES, [(load_sums, 0)], E_SLOTS)
            for u in range(E_SLOTS):
                sp.wait_ge(o_stored[u], 16 * in_slot(u))

        @block.gpsimd
        def _(pool):
            pool.memset(minus_half[:, :], -0.5).then_inc(S["half_set"], 1)
            pool.memset(pr[:, :, :], 0.0).then_inc(S["p_zero"], 1)
            pool.memset(zeros[:, :], 0.0).then_inc(S["zeros_set"], 1)
            pool.memset(counts[:, 0, :], 0.0).then_inc(S["counts_start"], 1)
            pool.iota(ids[:, :], [[P, TILES]], base=0, channel_multiplier=1).then_inc(S["ids_made"], 1)
            pool.wait_ge(S["half_set"], 1)

            def power(name_in, name_out, src, dst, slots=2):
                def step(t, n, u):
                    pool.wait_ge(S[name_in], t + 1)
                    pool.tensor_tensor(dst[:, u % slots, :], src[:, u % slots, :], minus_half[:, :], ALU.pow).then_inc(S[name_out], 1)
                return step

            def h_affine(t, n, u):
                if isinstance(t, int) and t == 0:
                    pool.wait_ge(S["small_in"], 32)
                pool.wait_ge(S["h_normed"], t + 1)
                wait(pool, h_stored[u], 16 * n)
                wait(pool, S["h_turned"], t - A_SLOTS + 1)
                settled(pool, S["pool_settled"])
                pool.tensor_tensor(hs[:, u, :], hl[:, u, :], g2b, ALU.mult).then_inc(S["h_scaled"], 1)
                pool.wait_ge(S["h_scaled"], t + 1)
                pool.tensor_tensor(hs[:, u, :], hs[:, u, :], b2b, ALU.add).then_inc(S["h_ready"], 1)

            walk(pool, TILES, [(power("x_var", "x_rstd", ve, rs, A_SLOTS), 0), (power("h_var", "h_rstd", ve2, rs2, A_SLOTS), 3), (h_affine, 3)], A_SLOTS)

            v_mask = k_of["v_heads"][0:TRI * SEQ, :]
            pool.wait_ge(S["consts_in"], 16)

            pool.wait_ge(vrep_in[0], 16 * TRI)
            pool.tensor_copy(vbd[0:TRI * SEQ, :, :, :, DH].rearrange("p r i h -> p (r i) h"),
                             v_mask.rearrange("p (a h) -> p a h", a=1).to_broadcast([TRI * SEQ, CI, HEADS]))

            def mask_v(t, n, u):
                r = u % PAIRS
                pool.wait_ge(vrep_in[r], 16 * TRI * (2 * n + u // PAIRS + 1))
                wait(pool, S["pv_mm"], t - PAIRS + 1)
                for i in range(2):
                    last = pool.tensor_tensor(
                        vbd[0:TRI * SEQ, r, i, :, 0:DH], vrep[0:TRI * SEQ, r, i, :].rearrange("p (h d) -> p h d", h=HEADS),
                        v_mask.rearrange("p (h a) -> p h a", a=1).to_broadcast([TRI * SEQ, HEADS, DH]), ALU.mult)
                last.then_inc(S["v_masked"], 1)

            def shift(t, n, u):
                pool.wait_ge(S["maxed"], t + 1)
                pool.tensor_tensor(sc[0:QP, u % 2, :, :], sc[0:QP, u % 2, :, :],
                                   mx[0:QP, u % 2, :].rearrange("p (h a) -> p h a", a=1).to_broadcast([QP, HEADS, SEQ]),
                                   ALU.subtract).then_inc(S["shifted"], 1)

            walk_pairs(pool, [(shift, SETUP), (mask_v, SETUP - 1)])

            def send(t, n, u):
                pool.wait_ge(S["rows_ready"], t + 1)
                pool.wait_ge(S["h2_copied"], t + 1)
                settled(pool, S["pool_settled"])
                for j in range(TOPK):
                    pool.indirect_dma_start(sent, bass.IndirectOffsetOnAxis(ap=desti[:, u, j:j + 1], axis=0),
                                            dsp[:, u, j, :], None).then_inc(rows_sent[u], 16)

            walk(pool, TILES, [(power("r_var", "r_rstd", ve, rs), 1), (send, 5)])

            pool.wait_ge(S["ends_out"], 1)
            for u in range(2):
                pool.wait_ge(rows_sent[u], 16 * TOPK * (TILES // 2))
            pads_out(pool, ENG.Pool, 0, POOL_PADS, "pads_out_pool")

            pool.wait_ge(S["table_set"], 1)
            pool.dma_start(table_dram.rearrange("(b p) c -> p b c", p=P), tvi[:, :, :]).then_inc(S["table_out"], 16)
            pool.wait_ge(S["table_out"], 16)
            pool.dma_start(table[:, :], table_dram.rearrange("(a n) c -> a (n c)", a=1)).then_inc(S["table_in"], 16)

            def meta_out(n, v, u):
                pool.wait_ge(rows_in[u], 16 * (v + 1))
                wait(pool, S["y_ready"], n - SUMS + 1)
                settled(pool, S["pool_settled"])
                pool.tensor_copy(meta[:, u, :], xe[:, u, D:ROW]).then_inc(S["meta"], 1)

            def add_y(n, v, u):
                pool.wait_ge(S["y_ready"], n + 1)
                wait(pool, y_added[u], 16 * v)
                settled(pool, S["pool_settled"])
                pool.indirect_dma_start(sums, bass.IndirectOffsetOnAxis(ap=ids2[:, u:u + 1], axis=0),
                                        ye[:, u, :], None, compute_op=ALU.add).then_inc(y_added[u], 16)

            pool.wait_ge(S["sums_zeroed"], 16 * (IMAGES // 2))
            walk(pool, E_TILES, [(meta_out, 1), (add_y, 4)], SUMS)

            def f_pool(t, n, u):
                pool.wait_ge(sums_in[u], 16 * (n + 1))
                pool.tensor_tensor(si4[:, u, 2, :], si4[:, u, 2, :], si4[:, u, 3, :], ALU.add).then_inc(S["f_pool"], 1)

            walk(pool, TILES, [(f_pool, 0), (power("f_var", "f_rstd", ve, rs), 1)], E_SLOTS)

        @block.scalar
        def _(act):
            act.wait_ge(S["small_in"], 32)
            act.activation(xi[:, :], xi[:, :], ACT.Exp).then_inc(S["xi_exp"], 1)

            def x_out(t, n, u):
                act.wait_ge(S["x_turned"], t + 1)
                wait(act, S["tok_mm"], t - A_SLOTS + 1)
                for c in range(2):
                    last = act.activation(xT[:, u, 3 * c:3 * c + 3, :], banks[c][:, 0:3 * P], ACT.Copy)
                last.then_inc(S["xT_out"], 1)

            def hT_out(t, n, u):
                act.wait_ge(S["h_turned"], t + 1)
                wait(act, S["v_mm"], t - A_SLOTS + 1)
                turned = banks[5][:, 0:D].rearrange("p (c k) -> p c k", c=DC)
                act.activation(hTs[:, u, :, :], turned, ACT.Copy)
                act.activation(cols_of(hT, t), turned, ACT.Copy).then_inc(S["hT_out"], 1)

            def v_out(t, n, u):
                act.wait_ge(S["v_mm"], t + 1)
                wait(act, v_stored[u], 16 * n)
                act.activation(vs[:, u, :], banks[6][:, 0:D], ACT.Copy).then_inc(S["v_out"], 1)
                act.wait_ge(S["v_out"], t + 1)
                act.dma_start(rows_of(v_dram, t), vs[:, u, :]).then_inc(v_stored[u], 16)

            walk(act, TILES, [(hT_out, 4), (v_out, 5), (x_out, 0)], A_SLOTS)

            act.wait_ge(S["consts_in"], 16)
            act.wait_ge(S["p_zero"], 1)

            def spread_k(t, n, u):
                c, k_out = 2 * n + u // PAIRS, kexp[u // PAIRS]
                if u % PAIRS == 1:
                    act.wait_ge(S["k_rot"], c + 1)
                    wait(act, S["scores_mm"], (c - 1) * PAIRS)
                    for h in range(HALF):
                        last = act.activation(k_out[:, 0, h, :], krot[:, :], ACT.Copy, scale=k_of["k_heads"][:, h:h + 1])
                    last.then_inc(S["kexp_out"], 1)
                if u % PAIRS == 3:
                    act.wait_ge(S["qk_mm"], 3 * c + 3)
                    for h in range(HALF):
                        act.activation(k_out[:, 1, h, :], banks[7][:, 0:CT], ACT.Copy, scale=k_of["k_heads"][:, h:h + 1])
                    act.activation(qT[:, u // PAIRS, 1, :], banks[6][:, 0:CT], ACT.Copy).then_inc(S["q_out"], 1)

            def exps(t, n, u):
                act.wait_ge(S["shifted"], t + 1)
                wait(act, S["p_turned"], t - 1)
                act.activation(pr[0:QP, u % 2, :], sc[0:QP, u % 2, :, :], ACT.Exp).then_inc(S["exped"], 1)

            def pT_out(t, n, u):
                act.wait_ge(S["p_turned"], t + 1)
                wait(act, S["pv_mm"], t - 1)
                act.activation(pT[0:TRI * SEQ, u % 2, 0:4, 0:QP], banks[2][0:TRI * SEQ, 0:4 * QP].rearrange("p (g q) -> p g q", g=4),
                               ACT.Copy).then_inc(S["pT_act"], 1)

            walk_pairs(act, [(spread_k, 0), (pT_out, SETUP + 1), (exps, SETUP)])

            def aT_out(t, n, u):
                act.wait_ge(S["a_turned"], t + 1)
                wait(act, S["wo_mm"], t - 1)
                act.activation(aT[:, u, :, :], banks[0][:, 0:D], ACT.Copy).then_inc(S["aT_out"], 1)

            def h2T_out(t, n, u):
                act.wait_ge(S["h2_turned"], t + 1)
                wait(act, S["gate_mm"], t - 1)
                turned = banks[2][:, 0:D].rearrange("p (c k) -> p c k", c=DC)
                act.activation(h2Ts[:, u, :, :], turned, ACT.Copy)
                act.activation(cols_of(hT, t), turned, ACT.Copy).then_inc(S["h2T_out"], 1)

            def gate_out(t, n, u):
                act.wait_ge(S["gate_mm"], t + 1)
                wait(act, S["score"], t - 1)
                act.activation(rt[:, u, 0, :], banks[3][:, 0:EXPERTS], ACT.Sigmoid).then_inc(S["gate_sig"], 1)

            def keep_h2(t, n, u):
                act.wait_ge(S["h2_ready"], t + 1)
                act.activation(at(acc, t), h2[:, u, :], ACT.Copy).then_inc(S["kept_h2"], 1)

            def copy_h2(t, n, u):
                act.wait_ge(S["kept_h2"], t + 1)
                wait(act, rows_sent[u], 16 * TOPK * n)
                row = acc[:, bass.ds(t, 1), :] if not isinstance(t, int) else acc[:, t:t + 1, :]
                act.activation(dsp[:, u, :, 0:D], row.to_broadcast([P, TOPK, D]), ACT.Copy).then_inc(S["h2_copied"], 1)

            walk(act, TILES, [(h2T_out, 2), (aT_out, 0), (keep_h2, 2), (gate_out, 2), (copy_h2, 4)])

            for b in range(BLOCKS):
                for m in range(SHARED // P):
                    k = b * 2 + m + 1
                    act.wait_ge(S["sh_up_mm"], k)
                    wait(act, S["sh_act"], k - 2)
                    act.activation(sha[:, m, 0, :], banks[2 * m][:, 0:3 * P], ACT.Silu).then_inc(S["sh_silu"], 1)

            def xeT_out(n, v, u):
                act.wait_ge(S["x_turned_e"], n + 1)
                wait(act, S["up_mm"], n - 1)
                act.activation(xeT[:, u % 2, :, :], banks[u % 2][:, 0:D], ACT.Copy).then_inc(S["xT_out_e"], 1)

            def silu(n, v, u):
                act.wait_ge(S["up_mm"], n + 1)
                wait(act, S["act_ready"], n - 1)
                act.activation(sg[:, u % 2, :], banks[2 + u % 2][:, 0:INTER], ACT.Silu).then_inc(S["silu"], 1)

            def aeT_out(n, v, u):
                act.wait_ge(S["act_turned"], n + 1)
                wait(act, S["down_mm"], n - 1)
                act.activation(aeT[:, u % 2, :], banks[4 + u % 2][:, 0:P], ACT.Copy).then_inc(S["actT_out"], 1)

            walk(act, E_TILES, [(silu, 2), (aeT_out, 3), (xeT_out, 0)], SUMS)

            def store_o(t, n, u):
                act.wait_ge(S["f_ready"], t + 1)
                act.dma_start(rows_of(out, t), of[:, u, :]).then_inc(o_stored[u], 16)

            walk(act, TILES, [(store_o, 0)], E_SLOTS)

        @block.vector
        def _(dve):
            dve.wait_ge(S["tok_w_in"], 48)
            for c in range(PC):
                last = dve.tensor_scalar(wtg[:, c, :], wt[:, c, :], g1s[:, c:c + 1], None, ALU.mult)
            last.then_inc(S["wtg_ready"], 1)

            def set_tok_bias():
                dve.wait_ge(S["small_in"], 32)
                dve.wait_ge(S["bias_mm"], 1)
                dve.tensor_tensor(tok_bias[:, :], banks[7][:, 0:D], brow[:, 0:D], ALU.add).then_inc(S["tok_bias_ready"], 1)
                dve.wait_ge(S["tok_bias_ready"], 1)

            def set_score_bias():
                dve.wait_ge(S["xi_exp"], 1)
                dve.wait_ge(S["consts_in"], 16)
                dve.reciprocal(xi[:, :], xi[:, :]).then_inc(S["xi_rec"], 1)
                dve.wait_ge(S["xi_rec"], 1)
                dve.tensor_tensor(xi[:, :], xi[:, :], k_of["decays"], ALU.mult).then_inc(S["xi_rec"], 1)
                dve.wait_ge(S["xi_rec"], 2)
                for h in range(HEADS):
                    last = dve.scalar_tensor_tensor(out=bias[:, h, :], in0=k_of["dist"], scalar=xi[:, h:h + 1],
                                                    in1=k_of["causal"], op0=ALU.mult, op1=ALU.add)
                last.then_inc(S["bias_set"], 1)

            def norm_steps(srcs, stats, mean_var, var_eps, eps, s_stats, s_var, slots=2):
                def bn(t, n, u):
                    parts = srcs(u)
                    for k, src in enumerate(parts):
                        last = dve.bn_stats(stats[:, u % slots, k, :] if len(parts) > 1 else stats[:, u % slots, :], src)
                    last.then_inc(S[s_stats], 1)

                def aggregate(t, n, u):
                    dve.wait_ge(S[s_stats], 2 * t + 1)
                    settled(dve, S["steps_settled"])
                    both = stats[:, u % slots]
                    dve.bn_aggr(mean_var[:, u % slots, :], both.rearrange("p a b -> p (a b)") if len(both.shape) > 2 else both).then_inc(S[s_stats], 1)

                def add_eps(t, n, u):
                    dve.wait_ge(S[s_stats], 2 * t + 2)
                    dve.tensor_scalar(var_eps[:, u % slots, :], mean_var[:, u % slots, 1:2], eps, None, ALU.add).then_inc(S[s_var], 1)

                return bn, aggregate, add_eps

            x_bn, x_aggr, x_eps = norm_steps(lambda u: [xs[:, u, 0:PATCH // 2], xs[:, u, PATCH // 2:]], st, mv, ve, TOK_EPS, "x_stats", "x_var", A_SLOTS)
            h_bn, h_aggr, h_eps = norm_steps(lambda u: [hl[:, u, :]], st2, mv2, ve2, TOK_EPS, "h_stats", "h_var", A_SLOTS)

            def x_start(t, n, u):
                dve.wait_ge(x_in[u], 16 * (n + 1))
                x_bn(t, n, u)

            def x_norm(t, n, u):
                dve.wait_ge(S["x_rstd"], t + 1)
                dve.tensor_scalar(xs[:, u, :], xs[:, u, :], mv[:, u, 0:1], rs[:, u, :], ALU.subtract, ALU.mult).then_inc(S["x_normed"], 1)

            def h_sum(t, n, u):
                if isinstance(t, int) and t == 0:
                    set_tok_bias()
                dve.wait_ge(S["tok_mm"], t + 1)
                wait(dve, S["h_scaled"], t - A_SLOTS + 1)
                dve.tensor_tensor(hl[:, u, :], banks[2 + u][:, 0:D], tok_bias[:, :], ALU.add).then_inc(S["h_sum"], 1)

            def h_start(t, n, u):
                dve.wait_ge(S["h_sum"], t + 1)
                h_bn(t, n, u)

            def h_norm(t, n, u):
                if isinstance(t, int) and t == 1:
                    set_score_bias()
                dve.wait_ge(S["h_rstd"], t + 1)
                dve.tensor_scalar(hl[:, u, :], hl[:, u, :], mv2[:, u, 0:1], rs2[:, u, :], ALU.subtract, ALU.mult).then_inc(S["h_normed"], 1)

            walk(dve, TILES, [(x_start, 0), (h_sum, 3), (x_aggr, 0), (h_start, 3), (x_eps, 0), (h_aggr, 3), (h_eps, 3), (x_norm, 0), (h_norm, 3)], A_SLOTS)

            def per_image(ap):
                return ap.rearrange("p (a k) -> p a k", a=1).to_broadcast([P, CI, SEQ])

            def images(ap):
                return ap.rearrange("p (i k) -> p i k", i=CI)

            def rotate(t, n, u):
                c = 2 * n + u // PAIRS
                if u % PAIRS > 1:
                    return
                table = ("cos", "sin")
                mul, done, out = (("k_mul", "k_rot", krot[:, :]), ("q_mul", "q_rot", qT[:, u // PAIRS, 0, :]))[u % PAIRS]
                part = tmp[:, 2 * (u % PAIRS):2 * (u % PAIRS) + 2, :]
                dve.wait_ge(S["qk_mm"], 3 * c + 1 + u % PAIRS)
                wait(dve, S[done], c)
                for k in range(2):
                    dve.tensor_tensor(images(part[:, k, :]), images(banks[6 + k][:, 0:CT]), per_image(k_of[table[k]]), ALU.mult).then_inc(S[mul], 1)
                dve.wait_ge(S[mul], 2 * c + 2)
                if u % PAIRS == 0:
                    wait(dve, S["kexp_out"], c)
                else:
                    wait(dve, S["scores_mm"], (c - 1) * PAIRS)
                dve.tensor_tensor(out, part[:, 0, :], part[:, 1, :], ALU.add).then_inc(S[done], 1)

            def soft(t, n, u):
                dve.wait_ge(S["scores_mm"], t + 1)
                wait(dve, S["exped"], t - 1)
                for half in range(2):
                    last = dve.scalar_tensor_tensor(
                        out=sc[0:QP, u % 2, half * HALF:(half + 1) * HALF, :].rearrange("p h k -> p (h k)"),
                        in0=banks[half][0:QP, 0:HALF * SEQ], scalar=DH ** -0.5,
                        in1=bias[0:QP, half * HALF:(half + 1) * HALF, :].rearrange("p h k -> p (h k)"),
                        op0=ALU.mult, op1=ALU.add)
                last.then_inc(S["biased"], 1)
                dve.wait_ge(S["biased"], t + 1)
                dve.tensor_reduce(mx[0:QP, u % 2, :], sc[0:QP, u % 2, :, :], AX.X, ALU.max).then_inc(S["maxed"], 1)

            def pT_out(t, n, u):
                dve.wait_ge(S["p_turned"], t + 1)
                wait(dve, S["pv_mm"], t - 1)
                dve.tensor_copy(pT[0:TRI * SEQ, u % 2, 4, 0:QP], banks[3][0:TRI * SEQ, 0:QP])
                dve.tensor_copy(pT[0:SEQ, u % 2, 5, 0:QP], banks[3][0:SEQ, QP:2 * QP]).then_inc(S["pT_dve"], 1)

            def divide(t, n, u):
                o = banks[4 + u % 2][0:QP, 0:HEADS * VW].rearrange("p (h w) -> p h w", w=VW)
                dve.wait_ge(S["pv_mm"], t + 1)
                dve.reciprocal(si[0:QP, u % 2, :], o[:, :, DH]).then_inc(S["sum_inv"], 1)
                dve.wait_ge(S["sum_inv"], t + 1)
                wait(dve, a_stored[u % 2], 32 * (n * PAIRS + u // 2))
                dve.tensor_tensor(ao[0:QP, u % 2, :].rearrange("p (h d) -> p h d", h=HEADS), o[:, :, 0:DH],
                                  si[0:QP, u % 2, :].rearrange("p (h a) -> p h a", a=1).to_broadcast([QP, HEADS, DH]),
                                  ALU.mult).then_inc(S["attended"], 1)

            walk_pairs(dve, [(soft, SETUP), (rotate, 0), (pT_out, SETUP + 1), (divide, SETUP + 2)])

            def r_sum(t, n, u):
                dve.wait_ge(S["wo_mm"], t + 1)
                dve.wait_ge(h_in[u], 16 * (n + 1))
                dve.tensor_tensor(hl[:, u, :], banks[1][:, 0:D], hi[:, u, :], ALU.add).then_inc(S["r_sum"], 1)

            r_bn, r_aggr, r_eps = norm_steps(lambda u: [hl[:, u, :]], st2, mv2, ve, LN_EPS, "r_stats", "r_var")

            def r_start(t, n, u):
                dve.wait_ge(S["r_sum"], t + 1)
                r_bn(t, n, u)

            def r_norm(t, n, u):
                dve.wait_ge(S["r_rstd"], t + 1)
                wait(dve, S["h2_turned"], t - 1)
                wait(dve, S["kept_h2"], t - 1)
                dve.tensor_scalar(h2[:, u, :], hl[:, u, :], mv2[:, u, 0:1], rs[:, u, :], ALU.subtract, ALU.mult).then_inc(S["h2_ready"], 1)

            ROUTE = 10

            def after(k, t):
                dve.wait_ge(S["route_steps"], ROUTE * t + k)

            def beside(ap, axis, sizes):
                return ap.rearrange("p (x a) -> p x a" if axis == 2 else "p (a x) -> p a x", a=1).to_broadcast([P] + sizes)

            def by_group(ap):
                return ap.rearrange("p (g e) -> p g e", g=NGROUP)

            def add_bias(t, n, u):
                dve.wait_ge(S["gate_sig"], t + 1)
                dve.tensor_tensor(rt[:, u, 1, :], rt[:, u, 0, :], gate_b, ALU.add).then_inc(S["score"], 1)

            def group_max(t, n, u):
                dve.wait_ge(S["score"], t + 1)
                dve.tensor_reduce(gm[:, u, 0, :], by_group(rt[:, u, 1, :]), AX.X, ALU.max).then_inc(S["route_steps"], 1)

            def group_top(t, n, u):
                after(1, t)
                settled(dve, S["steps_settled"])
                dve.max(gm[:, u, 1, :], gm[:, u, 0, :]).then_inc(S["route_steps"], 1)

            def group_index(t, n, u):
                after(2, t)
                settled(dve, S["steps_settled"])
                dve.max_index(gi[:, u, :], gm[:, u, 1, :], gm[:, u, 0, :]).then_inc(S["route_steps"], 1)

            def group_equal(t, n, u):
                after(3, t)
                dve.tensor_tensor(geq[:, u, :, :], beside(gi[:, u, 0:TOPG], 2, [TOPG, NGROUP]), beside(k_of["groups"], 1, [TOPG, NGROUP]),
                                  ALU.is_equal).then_inc(S["route_steps"], 1)

            def group_mask(t, n, u):
                after(4, t)
                dve.tensor_reduce(gm[:, u, 0, :], geq[:, u, :, :].rearrange("p j g -> p g j"), AX.X, ALU.add).then_inc(S["route_steps"], 1)

            def mask_scores(t, n, u):
                after(5, t)
                dve.tensor_tensor(by_group(rt[:, u, 2, :]), by_group(rt[:, u, 1, :]), beside(gm[:, u, 0, :], 2, [NGROUP, EXPERTS // NGROUP]),
                                  ALU.mult).then_inc(S["route_steps"], 1)

            def top(t, n, u):
                after(6, t)
                settled(dve, S["steps_settled"])
                dve.max(t8[:, u, :], rt[:, u, 2, :]).then_inc(S["route_steps"], 1)

            def top_index(t, n, u):
                after(7, t)
                settled(dve, S["steps_settled"])
                dve.max_index(ti[:, u, :], t8[:, u, :], rt[:, u, 2, :]).then_inc(S["route_steps"], 1)

            def top_sum(t, n, u):
                after(7, t)
                dve.tensor_reduce(tsum[:, u, 0:1], t8[:, u, 0:TOPK], AX.X, ALU.add).then_inc(S["route_steps"], 1)

            def top_equal(t, n, u):
                after(8, t)
                dve.tensor_tensor(teq[:, u, :, :], beside(ti[:, u, 0:TOPK], 2, [TOPK, EXPERTS]), beside(k_of["experts"], 1, [TOPK, EXPERTS]),
                                  ALU.is_equal).then_inc(S["route_steps"], 1)

            def top_eps(t, n, u):
                after(9, t)
                dve.tensor_scalar(tsum[:, u, 1:2], tsum[:, u, 0:1], 1e-8, None, ALU.add).then_inc(S["top_inv"], 1)

            def choose(t, n, u):
                after(10, t)
                wait(dve, S["ranked"], t - 1)
                dve.tensor_reduce(chosen[:, u, :], teq[:, u, :, :].rearrange("p j g -> p g j"), AX.X, ALU.add).then_inc(S["chosen"], 1)

            def top_inverse(t, n, u):
                dve.wait_ge(S["top_inv"], 2 * t + 1)
                dve.reciprocal(tsum[:, u, 0:1], tsum[:, u, 1:2]).then_inc(S["top_inv"], 1)

            def count(t, n, u):
                dve.wait_ge(S["ranked"], t + 1)
                dve.tensor_tensor(place[:, u, :], banks[4 + u][:, 0:EXPERTS], counts[:, u, :], ALU.add).then_inc(S["place"], 1)
                dve.tensor_tensor(counts[:, 1 - u, :], banks[4 + u][:, EXPERTS:2 * EXPERTS], counts[:, u, :], ALU.add).then_inc(S["counted"], 1)

            def place_all(t, n, u):
                dve.wait_ge(S["place"], 4 * t + 1)
                dve.wait_ge(S["counted"], t + 1)
                dve.tensor_tensor(place[:, u, :], place[:, u, :], k_of["region"], ALU.add).then_inc(S["place"], 1)

            def place_chosen(t, n, u):
                dve.wait_ge(S["place"], 4 * t + 2)
                dve.tensor_tensor(tpl[:, u, :, :], teq[:, u, :, :], beside(place[:, u, :], 1, [TOPK, EXPERTS]), ALU.mult).then_inc(S["place"], 1)

            def place_sum(t, n, u):
                dve.wait_ge(S["place"], 4 * t + 3)
                dve.tensor_reduce(dest[:, u, :], tpl[:, u, :, :], AX.X, ALU.add).then_inc(S["place"], 1)

            def finish_rows(t, n, u):
                dve.wait_ge(S["place"], 4 * t + 4)
                dve.wait_ge(S["top_inv"], 2 * t + 2)
                wait(dve, rows_sent[u], 16 * TOPK * n)
                i = ids[:, t:t + 1] if isinstance(t, int) else ids[:, bass.ds(t, 1)]
                dve.tensor_copy(dsp[:, u, :, D + 1].bitcast(U32), i.to_broadcast([P, TOPK]))
                dve.tensor_scalar(dsp[:, u, :, D], t8[:, u, 0:TOPK], tsum[:, u, 0:1], None, ALU.mult)
                dve.tensor_copy(desti[:, u, :], dest[:, u, :]).then_inc(S["rows_ready"], 1)

            dve.wait_ge(S["counts_start"], 1)
            dve.wait_ge(S["ids_made"], 1)
            walk(dve, TILES, [(r_sum, 1), (add_bias, 3), (r_start, 1), (group_max, 3), (r_aggr, 1), (group_top, 3), (r_eps, 1),
                              (count, 4), (group_index, 3), (group_equal, 3), (place_all, 4), (group_mask, 3), (r_norm, 1),
                              (mask_scores, 3), (place_chosen, 4), (top, 3), (place_sum, 4), (top_index, 3), (top_sum, 3),
                              (finish_rows, 4), (top_equal, 3), (top_eps, 3), (choose, 3), (top_inverse, 3)])

            def shared_out(b):
                for m in range(SHARED // P):
                    k = b * 2 + m + 1
                    dve.wait_ge(S["sh_silu"], k)
                    wait(dve, S["sh_down_mm"], b)
                    dve.tensor_tensor(sha[:, m, 1, :], sha[:, m, 0, :], banks[2 * m + 1][:, 0:3 * P], ALU.mult).then_inc(S["sh_act"], 1)
                dve.wait_ge(S["sh_down_mm"], b + 1)
                for c in range(3):
                    tile = 3 * b + c
                    last = dve.tensor_tensor(acc[:, tile, :], banks[4 + 2 * (b % 2) + c // 2][:, (c % 2) * D:(c % 2 + 1) * D], acc[:, tile, :], ALU.add)
                last.then_inc(S["sh_added"], 1)

            step = [0]

            def then(ins):
                step[0] += 1
                ins.then_inc(S["tab"], 1)
                dve.wait_ge(S["tab"], step[0])

            cnt, tiles, until, start, some, begin = counts[:, 0, :], tb[:, 0, :], tb[:, 1, :], tb[:, 2, :], tb[:, 3, :], tb[:, 4, :]
            part = [tb[:, 5 + k, :] for k in range(4)]
            then(dve.tensor_tensor(begin, cnt, k_of["region"], ALU.add))
            then(dve.tensor_copy(ends[:, :], begin[0:1, :]))
            dve.sem_inc(S["ends_out"], 1)
            dve.wait_ge(S["kept_h2"], TILES)
            then(dve.tensor_scalar(tiles, cnt, float(P - 1), None, ALU.add))
            then(dve.tensor_copy(tbi[:, :], tiles))
            then(dve.tensor_scalar(tbi[:, :], tbi[:, :], 7, None, ALU.arith_shift_right))
            then(dve.tensor_copy(tiles, tbi[:, :]))
            then(dve.tensor_scalar(some, tiles, 0.0, None, ALU.is_gt))
            then(dve.tensor_tensor_scan(until, tiles, tiles, 0.0, ALU.add, ALU.bypass))
            then(dve.tensor_tensor(start, until, tiles, ALU.subtract))
            for b in range(2):
                shared_out(b)
                n = k_of["tile"][:, b:b + 1]
                v = [tv[:, b, k:k + 1] for k in range(8)]
                then(dve.tensor_scalar(part[0], until, n, None, ALU.is_le))
                then(dve.tensor_reduce(v[0], part[0], AX.X, ALU.add))
                then(dve.tensor_tensor(part[1], part[0], tiles, ALU.mult))
                then(dve.tensor_reduce(v[1], part[1], AX.X, ALU.add))
                then(dve.scalar_tensor_tensor(out=part[2], in0=start, scalar=n, in1=some, op0=ALU.is_le, op1=ALU.mult))
                then(dve.tensor_reduce(v[2], part[2], AX.X, ALU.add))
                then(dve.scalar_tensor_tensor(out=part[3], in0=start, scalar=n, in1=some, op0=ALU.is_equal, op1=ALU.mult))
                then(dve.tensor_reduce(v[3], part[3], AX.X, ALU.add))
                then(dve.tensor_tensor(v[4], n, v[1], ALU.subtract))
                then(dve.tensor_scalar(v[4], v[4], float(P), None, ALU.mult))
                then(dve.tensor_scalar(v[5], v[0], float(CAP), None, ALU.mult))
                then(dve.tensor_tensor(v[4], v[4], v[5], ALU.add))
                then(dve.tensor_scalar(v[4], v[4], float(SPARE), None, ALU.min))
                then(dve.tensor_copy(tvi[:, b, T_OFF:T_OFF + 1], v[4]))
                then(dve.tensor_scalar(v[6], v[0], float(EXPERTS - 1), None, ALU.min))
                then(dve.tensor_copy(tvi[:, b, T_EXPERT:T_EXPERT + 1], v[6]))
                then(dve.tensor_copy(tvi[:, b, T_SLOT:T_SLOT + 1], v[2]))
                then(dve.tensor_scalar(tvi[:, b, T_SLOT:T_SLOT + 1], tvi[:, b, T_SLOT:T_SLOT + 1], W_SLOTS - 1, None, ALU.bitwise_and))
                then(dve.tensor_copy(tvi[:, b, T_LOAD:T_LOAD + 1], v[3]))
            dve.sem_inc(S["table_set"], 1)

            for b in range(2, BLOCKS):
                shared_out(b)

            dve.wait_ge(S["table_in"], 16)
            dve.tensor_copy(slot_row[:, :], table[:, :].rearrange("a (n c) -> a n c", c=T_COLS)[:, :, T_SLOT]).then_inc(S["slots_set"], 1)

            def act_out(n, v, u):
                dve.wait_ge(S["silu"], n + 1)
                wait(dve, S["act_turned"], n - 1)
                dve.tensor_tensor(ae[:, u % 2, :], sg[:, u % 2, :], banks[2 + u % 2][:, INTER:2 * INTER], ALU.mult).then_inc(S["act_ready"], 1)

            def y_out(n, v, u):
                dve.wait_ge(S["down_mm"], n + 1)
                dve.wait_ge(S["meta"], n + 1)
                wait(dve, y_added[u], 16 * v)
                dve.tensor_scalar(ids2[:, u:u + 1], meta[:, u, 1:2].bitcast(U32), u * (TOK + P), None, ALU.add)
                dve.tensor_scalar(ye[:, u, :], banks[6 + u % 2][:, 0:D], meta[:, u, 0:1], None, ALU.mult).then_inc(S["y_ready"], 1)

            walk(dve, E_TILES, [(act_out, 2), (y_out, 4)], SUMS)

            dve.wait_ge(S["sh_added"], BLOCKS)

            def f_pairs(t, n, u):
                dve.wait_ge(sums_in[u], 16 * (n + 1))
                dve.tensor_tensor(si4[:, u, 0, :], si4[:, u, 0, :], si4[:, u, 1, :], ALU.add).then_inc(S["f_pairs"], 1)

            def f_first(t, n, u):
                dve.wait_ge(S["f_pairs"], t + 1)
                dve.tensor_tensor(hl[:, u % 2, :], at(acc, t), si4[:, u, 0, :], ALU.add).then_inc(S["f_first"], 1)

            def f_sum(t, n, u):
                dve.wait_ge(S["f_first"], t + 1)
                dve.wait_ge(S["f_pool"], t + 1)
                dve.tensor_tensor(hl[:, u % 2, :], hl[:, u % 2, :], si4[:, u, 2, :], ALU.add).then_inc(S["f_sum"], 1)

            f_bn, f_aggr, f_eps = norm_steps(lambda u: [hl[:, u % 2, :]], st2, mv2, ve, LN_EPS, "f_stats", "f_var")

            def f_start(t, n, u):
                dve.wait_ge(S["f_sum"], t + 1)
                f_bn(t, n, u)

            def f_norm(t, n, u):
                dve.wait_ge(S["f_rstd"], t + 1)
                wait(dve, o_stored[u], 16 * n)
                dve.tensor_scalar(of[:, u, :], hl[:, u % 2, :], mv2[:, u % 2, 0:1], rs[:, u % 2, :], ALU.subtract, ALU.mult).then_inc(S["f_ready"], 1)

            walk(dve, TILES, [(f_first, 1), (f_pairs, 0), (f_sum, 1), (f_start, 1), (f_norm, 2), (f_aggr, 1), (f_eps, 1)], E_SLOTS)

        @block.tensor
        def _(pe):
            pe.wait_ge(S["tok_w_in"], 48)
            for c in range(PC):
                last = pe.matmul(banks[7][:, 0:D], b1s[:, c:c + 1].to_broadcast([P, P]), wt[:, c, :], start=(c == 0), stop=(c == PC - 1))
            last.then_inc(S["bias_mm"], 1)
            pe.wait_ge(S["wtg_ready"], 1)
            pe.wait_ge(S["consts_in"], 16)

            def turn_x(t, n, u):
                pe.wait_ge(S["x_normed"], t + 1)
                wait(pe, S["xT_out"], t)
                for c in range(PC):
                    last = pe.transpose(banks[c // 3][:, (c % 3) * P:(c % 3 + 1) * P], xs[:, u, c * P:(c + 1) * P], ident)
                last.then_inc(S["x_turned"], 1)

            def tok(t, n, u):
                pe.wait_ge(S["xT_out"], t + 1)
                wait(pe, S["h_sum"], t - A_SLOTS + 1)
                for c in range(PC):
                    last = pe.matmul(banks[2 + u][:, 0:D], xT[:, u, c, :], wtg[:, c, :], start=(c == 0), stop=(c == PC - 1))
                last.then_inc(S["tok_mm"], 1)

            def turn_h(t, n, u):
                pe.wait_ge(S["h_ready"], t + 1)
                wait(pe, S["hT_out"], t)
                for c in range(DC):
                    last = pe.transpose(banks[5][:, c * P:(c + 1) * P], hs[:, u, c * P:(c + 1) * P], ident)
                last.then_inc(S["h_turned"], 1)

            def values(t, n, u):
                pe.wait_ge(S["hT_out"], t + 1)
                wait(pe, S["v_out"], t)
                if isinstance(t, int) and t == 0:
                    pe.wait_ge(S["weights_in"], 16 * 5)
                for c in range(DC):
                    last = pe.matmul(banks[6][:, 0:D], hTs[:, u, c, :], wv[:, c, :], start=(c == 0), stop=(c == DC - 1))
                last.then_inc(S["v_mm"], 1)

            walk(pe, TILES, [(turn_h, 4), (values, 5), (turn_x, 0), (tok, 1)], A_SLOTS)

            pe.wait_ge(S["hT_out"], TILES)
            pe.wait_ge(S["v_out"], TILES)
            pe.wait_ge(S["h_sum"], TILES)
            pe.wait_ge(S["xT_out"], TILES)

            def project_qk(t, n, u):
                c, r = 2 * n + u // PAIRS, u % PAIRS
                if r == 3:
                    return
                if r == 0:
                    wait(pe, S["q_out"], c)
                else:
                    pe.wait_ge(S[("k_mul", "q_mul")[r - 1]], 2 * c + 2)
                for b, w, half in (((6, wk, 0), (7, wks, 0)), ((6, wq, 0), (7, wqs, 0)), ((6, wq, 1), (7, wk, 1)))[r]:
                    for d in range(DC):
                        tokens = hT[:, d, c * CT:(c + 1) * CT] if isinstance(c, int) else hT[:, d, bass.ds(c * CT, CT)]
                        last = pe.matmul(banks[b][:, 0:CT], w[:, d, half * P:(half + 1) * P], tokens, start=(d == 0), stop=(d == DC - 1))
                last.then_inc(S["qk_mm"], 1)

            def scores(t, n, u):
                c, r = 2 * n + u // PAIRS, u % PAIRS
                pe.wait_ge(S["q_rot"], c + 1)
                pe.wait_ge(S["q_out"], c + 1)
                pe.wait_ge(S["kexp_out"], c + 1)
                wait(pe, S["biased"], t)
                for half in range(2):
                    for i in range(2):
                        img = 2 * r + i
                        m = 64 if i == 0 else SEQ
                        last = pe.matmul(banks[half][64 * i:64 * i + m, 0:HALF * SEQ], qT[:, u // PAIRS, half, img * SEQ:img * SEQ + m],
                                         kexp[u // PAIRS][:, half, :, img * SEQ:(img + 1) * SEQ], start=True, stop=True)
                last.then_inc(S["scores_mm"], 1)

            def turn(t, n, u):
                pe.wait_ge(S["exped"], t + 1)
                wait(pe, S["pT_act"], t)
                wait(pe, S["pT_dve"], t)
                for g in range(GROUPS):
                    w = min(TRI, HEADS - TRI * g) * SEQ
                    b, k = (2, g) if g < 4 else (3, g - 4)
                    last = pe.transpose(banks[b][0:w, k * QP:(k + 1) * QP], pr[0:QP, u % 2, g * TRI * SEQ:g * TRI * SEQ + w], ident[0:QP, 0:QP])
                last.then_inc(S["p_turned"], 1)

            def attend(t, n, u):
                pe.wait_ge(S["pT_act"], t + 1)
                pe.wait_ge(S["pT_dve"], t + 1)
                pe.wait_ge(S["v_masked"], t + 1)
                wait(pe, S["attended"], t - 1)
                for i in range(2):
                    m = 64 if i == 0 else SEQ
                    for g in range(GROUPS):
                        heads = min(TRI, HEADS - TRI * g)
                        k = heads * SEQ
                        last = pe.matmul(banks[4 + u % 2][64 * i:64 * i + m, g * TRI * VW:(g * TRI + heads) * VW],
                                         pT[0:k, u % 2, g, 64 * i:64 * i + m],
                                         vbd[0:k, u % PAIRS, i, g * TRI:g * TRI + heads, :].rearrange("p h w -> p (h w)"),
                                         start=True, stop=True)
                last.then_inc(S["pv_mm"], 1)

            walk_pairs(pe, [(scores, SETUP), (project_qk, 0), (turn, SETUP + 1), (attend, SETUP + 2)])

            pe.wait_ge(S["late_in"], 16 * 4)
            pe.wait_ge(S["attended"], CHUNKS * PAIRS)
            pe.wait_ge(S["biased"], CHUNKS * PAIRS)

            def turn_a(t, n, u):
                pe.wait_ge(a_in[u], 16 * (n + 1))
                wait(pe, S["aT_out"], t)
                for c in range(DC):
                    last = pe.transpose(banks[0][:, c * P:(c + 1) * P], ai[:, u, c * P:(c + 1) * P], ident)
                last.then_inc(S["a_turned"], 1)

            def project(t, n, u):
                pe.wait_ge(S["aT_out"], t + 1)
                wait(pe, S["r_sum"], t)
                for c in range(DC):
                    last = pe.matmul(banks[1][:, 0:D], aT[:, u, c, :], wo[:, c, :], start=(c == 0), stop=(c == DC - 1))
                last.then_inc(S["wo_mm"], 1)

            def turn_h2(t, n, u):
                pe.wait_ge(S["h2_ready"], t + 1)
                wait(pe, S["h2T_out"], t)
                for c in range(DC):
                    last = pe.transpose(banks[2][:, c * P:(c + 1) * P], h2[:, u, c * P:(c + 1) * P], ident)
                last.then_inc(S["h2_turned"], 1)

            def gate(t, n, u):
                pe.wait_ge(S["h2T_out"], t + 1)
                wait(pe, S["gate_sig"], t)
                for c in range(DC):
                    last = pe.matmul(banks[3][:, 0:EXPERTS], h2Ts[:, u, c, :], gw[:, c, :], start=(c == 0), stop=(c == DC - 1))
                last.then_inc(S["gate_mm"], 1)

            def rank(t, n, u):
                pe.wait_ge(S["chosen"], t + 1)
                wait(pe, S["counted"], t - 1)
                pe.matmul(banks[4 + u][:, 0:EXPERTS], k_of["before"], chosen[:, u, :], start=True, stop=True)
                pe.matmul(banks[4 + u][:, EXPERTS:2 * EXPERTS], k_of["ones"], chosen[:, u, :], start=True, stop=True).then_inc(S["ranked"], 1)

            walk(pe, TILES, [(rank, 4), (turn_h2, 2), (turn_a, 0), (gate, 2), (project, 0)])

            pe.wait_ge(S["h2T_out"], TILES)
            pe.wait_ge(S["gate_sig"], TILES)
            pe.wait_ge(S["counted"], TILES)

            def shared_down(b):
                pe.wait_ge(S["sh_act"], 2 * b + 2)
                wait(pe, S["sh_added"], b - 1)
                for t in range(3):
                    for m in range(SHARED // P):
                        last = pe.matmul(banks[4 + 2 * (b % 2) + t // 2][:, (t % 2) * D:(t % 2 + 1) * D], sha[:, m, 1, t * P:(t + 1) * P],
                                         dsh[:, m, :], start=(m == 0), stop=(m == SHARED // P - 1))
                last.then_inc(S["sh_down_mm"], 1)

            for b in range(BLOCKS):
                for m in range(SHARED // P):
                    wait(pe, S["sh_act"], 2 * b + m - 1)
                    for up in range(2):
                        for c in range(DC):
                            w = (up * (SHARED // P) + m) * P
                            last = pe.matmul(banks[2 * m + up][:, 0:3 * P], wsh[:, c, w:w + P], hT[:, c, b * 3 * P:(b + 1) * 3 * P],
                                             start=(c == 0), stop=(c == DC - 1))
                    last.then_inc(S["sh_up_mm"], 1)
                    if m == 0 and b:
                        shared_down(b - 1)
            shared_down(BLOCKS - 1)

            pe.wait_ge(S["sh_act"], 2 * BLOCKS)
            pe.wait_ge(S["sh_added"], BLOCKS)
            pe.wait_ge(S["slots_set"], 1)

            def turn_xe(n, v, u):
                pe.wait_ge(rows_in[u], 16 * (v + 1))
                wait(pe, S["xT_out_e"], n - 1)
                for c in range(DC):
                    last = pe.transpose(banks[u % 2][:, c * P:(c + 1) * P], xe[:, u, c * P:(c + 1) * P], ident)
                last.then_inc(S["x_turned_e"], 1)

            of_tiles = {}

            def load_slots(v):
                settled(pe, S["pe_settled"])
                _, slots = nc.values_load_multi_w_load_instructions(
                    slot_row[0:1, bass.ds((v - 1) * SUMS, 2 * SUMS)], engines=(ENG.PE,), min_val=0, max_val=W_SLOTS - 1,
                    skip_runtime_bounds_check_because=CLAMPED)
                of_tiles.update({k - SUMS: slot for k, slot in enumerate(slots)})

            def weights(n, place, cols):
                if isinstance(n, int):
                    _, (slot,) = nc.values_load_multi_w_load_instructions(
                        slot_row[0:1, n:n + 1], engines=(ENG.PE,), min_val=0, max_val=W_SLOTS - 1, skip_runtime_bounds_check_because=CLAMPED)
                else:
                    slot = of_tiles[place]
                return moe[:, bass.ds(slot, 1), cols].rearrange("p a n -> p (a n)")

            def up(n, v, u):
                pe.wait_ge(S["xT_out_e"], n + 1)
                pe.wait_ge(w_in[u], 16 * (v + 1))
                wait(pe, S["act_ready"], n - 1)
                w = weights(n, u if u < 2 else u - SUMS, slice(0, 2 * D))
                for c in range(DC):
                    last = pe.matmul(banks[2 + u % 2][:, 0:2 * INTER], xeT[:, u % 2, c, :], w[:, c * 2 * INTER:(c + 1) * 2 * INTER],
                                     start=(c == 0), stop=(c == DC - 1))
                last.then_inc(S["up_mm"], 1)

            def turn_act(n, v, u):
                pe.wait_ge(S["act_ready"], n + 1)
                wait(pe, S["actT_out"], n - 1)
                pe.transpose(banks[4 + u % 2][:, 0:P], ae[:, u % 2, :], ident).then_inc(S["act_turned"], 1)

            def down(n, v, u):
                pe.wait_ge(S["actT_out"], n + 1)
                wait(pe, S["y_ready"], n - 1)
                pe.matmul(banks[6 + u % 2][:, 0:D], aeT[:, u % 2, :], weights(n, u - SUMS, slice(2 * D, 3 * D)), start=True, stop=True).then_inc(S["down_mm"], 1)

            walk(pe, E_TILES, [(up, 2), (turn_act, 3), (turn_xe, 0), (down, 4)], SUMS, begin=load_slots)


def shape_constants():
    import numpy as np
    c = np.zeros((P, CONST_W), np.float32)

    def put(name, value):
        a, w = CONST_AT[name]
        c[:, a:a + w] = value

    p = np.arange(P)[:, None]
    put("ident", p == np.arange(P)[None])
    put("k_heads", p // DH == np.arange(HALF)[None])
    put("v_heads", (p < TRI * SEQ) & (np.arange(HEADS)[None] % TRI == p // SEQ))
    pos = np.arange(SEQ, dtype=np.float32)
    inv = np.float32(10000.0) ** (-(np.arange(0, DH, 2, dtype=np.float32) / np.float32(DH)))
    theta = (pos[:, None] * inv[None, :]).astype(np.float32)
    d = np.arange(P) % DH
    put("cos", np.cos(theta).T[d // 2])
    put("sin", np.sin(theta).T[d // 2] * np.where(d % 2 == 0, -1.0, 1.0)[:, None])
    q = np.where(p < SEQ, p, p - 64)
    live = (q >= 0) & (q < SEQ)
    k = np.arange(SEQ)[None]
    put("causal", np.where(live & (k > q), MASKED, 0.0))
    put("dist", np.where(live, -np.abs(q - k), 0.0))
    put("decays", np.array([h & 1 for h in HEAD_ORDER], np.float32)[None])
    put("experts", np.arange(EXPERTS)[None])
    put("groups", np.arange(NGROUP)[None])
    put("before", p < np.arange(P)[None])
    put("ones", 1.0)
    put("region", np.arange(EXPERTS)[None] * CAP)
    put("tile", p + P * np.arange(2)[None])
    pad = np.zeros((P, ROW), np.float32)
    pad[:, D + 1] = (TOK + np.arange(P)).astype(np.uint32).view(np.float32)
    put("pad_row", pad)
    return c


def kernel(**inputs):
    import numpy as np
    import concourse.bacc as bacc
    from concourse.bass_utils import run_bass_kernel_spmd

    g = {k: np.asarray(v) for k, v in inputs.items()}

    def chunks(w):
        return np.ascontiguousarray(w.reshape(w.shape[0] // P, P, -1).transpose(1, 0, 2))

    x = g["x"]
    b, ch, hh, ww = x.shape
    patches = x.reshape(b, ch, hh // 16, 16, ww // 16, 16).transpose(0, 2, 4, 3, 5, 1).reshape(TOK, PATCH)
    wqkv = g["L0_attn_w_qkv"].reshape(D, 3, HEADS, DH)[:, :, HEAD_ORDER]
    swap = np.arange(DH) ^ 1
    w_q, w_k, w_v = (wqkv[:, i].reshape(D, D) for i in range(3))
    w_qs, w_ks = (wqkv[:, i, :HALF][:, :, swap].reshape(D, P) for i in range(2))
    w_o = g["L0_attn_w_o"].reshape(HEADS, DH, D)[HEAD_ORDER].reshape(D, D)
    eg, eu, ed = (g[f"L0_ffn_{n}_w"].transpose(0, 2, 1) for n in ("eg", "eu", "ed"))
    up = np.concatenate([eg, eu], axis=2).reshape(EXPERTS, DC, P, 2 * INTER).transpose(0, 2, 1, 3).reshape(EXPERTS, P, 2 * D)
    w_moe = np.concatenate([up, ed], axis=2)
    arrays = {
        "patches": patches, "w_tok": chunks(g["L0_tok_W_mlp"]),
        "rows": np.concatenate([g["L0_tok_b_mlp"], g["L0_tok_g2"], g["L0_tok_b2"], g["L0_ffn_gate_bias"]])[None],
        "b1_col": g["L0_tok_b1"].reshape(PC, P).T, "g1_col": g["L0_tok_g1"].reshape(PC, P).T,
        "w_q": chunks(w_q), "w_k": chunks(w_k), "w_qs": chunks(w_qs), "w_ks": chunks(w_ks), "w_v": chunks(w_v),
        "w_o": chunks(w_o), "gate_w": chunks(g["L0_ffn_gate_w"].T), "log_xi": g["L0_attn_log_xi"][HEAD_ORDER][None],
        "w_shared": chunks(np.concatenate([g["L0_ffn_sg_w"], g["L0_ffn_su_w"]]).T),
        "d_shared": chunks(g["L0_ffn_sd_w"].T), "w_moe": w_moe, "consts": shape_constants(),
    }
    nc = bacc.Bacc("TRN2", target_bir_lowering=False, num_devices=1)
    aps = {}
    for name, a in arrays.items():
        arrays[name] = np.ascontiguousarray(a)
        aps[name] = nc.dram_tensor(name, a.shape, mybir.dt.from_np(a.dtype), kind="ExternalInput").ap()
    out = nc.dram_tensor("result", (TOK, D), F32, kind="ExternalOutput").ap()
    program(nc, out=out, **aps)
    r = run_bass_kernel_spmd(nc, [arrays], core_ids=[0])
    return r.results[0]["result"].reshape(IMAGES, SEQ, D)
```

```python
from contextlib import ExitStack

import concourse.bass as bass
from concourse import mybir

F32 = mybir.dt.float32
U32 = mybir.dt.uint32
I32 = mybir.dt.int32
ALU = mybir.AluOpType
ACT = mybir.ActivationFunctionType
AX = mybir.AxisListType
ENG = mybir.EngineType

P = 128
IMAGES, SEQ = 64, 36
TOK = IMAGES * SEQ
TILES = TOK // P
PATCH = 768
PC = PATCH // P
D = 256
DC = D // P
HEADS, DH = 16, 16
HALF = HEADS // 2
CI = 8
CHUNKS = IMAGES // CI
CT = CI * SEQ
PAIRS = CI // 2
QP = 64 + SEQ
TRI = 3
GROUPS = -(-HEADS // TRI)
SETUP = PAIRS
VW = DH + 1
EXPERTS, INTER = 64, 128
NGROUP, TOPG, TOPK = 8, 4, 6
SHARED = 256
TOK_EPS = -1e-05
LN_EPS = 1e-05
MASKED = -1e30
ROW = D + 2
CAP = TOK + P
SPARE = EXPERTS * CAP
A_SLOTS = 3
SUMS = 4
POOL_PADS, ACT_PADS = 16, 20
E_SLOTS = 4
E_TILES = -(-((TOK * TOPK + EXPERTS * (P - 1)) // P) // SUMS) * SUMS
W_SLOTS = 8
T_OFF, T_EXPERT, T_SLOT, T_LOAD, T_COLS = 0, 1, 2, 3, 4

CONST_AT = {}
_n = 0
for _name, _w in (("ident", P), ("k_heads", HALF), ("v_heads", HEADS), ("cos", SEQ), ("sin", SEQ),
                  ("causal", SEQ), ("dist", SEQ), ("decays", HEADS), ("experts", EXPERTS), ("groups", NGROUP),
                  ("before", P), ("ones", P), ("region", EXPERTS), ("tile", 2), ("pad_row", ROW)):
    CONST_AT[_name] = (_n, _w)
    _n += _w
CONST_W = _n
SHARED_W = 2 * HALF * CT + CI * D + CI * HEADS * VW + 4 * CT
HEAD_ORDER = [h for h in range(HEADS) if h >> 1 & 1] + [h for h in range(HEADS) if not h >> 1 & 1]


def wait(eng, sem, value):
    if isinstance(value, int) and value <= 0:
        return
    eng.wait_ge(sem, value)


def settled(eng, sem):
    eng.sem_inc(sem, 1)


CLAMPED = "the table's last step clamps every column to its range"


def entries(nc, engine, row):
    _, (off, expert, slot, load) = nc.values_load_multi_w_load_instructions(
        row, engines=(engine,), min_val=0, max_val=SPARE, skip_runtime_bounds_check_because=CLAMPED)

    def most(value, top):
        return nc.s_assert_within(value, 0, top, skip_runtime_bounds_check_because=CLAMPED)

    return off, most(expert, EXPERTS - 1), most(slot, W_SLOTS - 1), most(load, 1)


def walk(eng, tiles, steps, slots=2, peel=0, begin=None, before=(), hold=False):
    lag = max(l for _, l in steps)
    head = max(peel, slots * -(-(slots + lag) // slots))
    loops = (tiles - head) // slots

    def at(s, base, first, last):
        for step, l in steps:
            slot = (s - l) % slots
            visit = base + (s - l - slot) // slots
            if first and visit < 0 or last and visit * slots + slot >= tiles:
                continue
            step(visit * slots + slot, visit, slot)

    for s in range(head):
        if s < len(before):
            before[s]()
        at(s, 0, True, False)
    with eng.Fori(head // slots, head // slots + loops) as visit:
        if begin:
            begin(visit)
        for s in range(slots):
            at(s, visit, False, False)
    for s in range(head + slots * loops, tiles if hold else tiles + lag):
        at(s, 0, False, True)
    return [lambda s=s: at(s, 0, False, True) for s in range(tiles, tiles + lag)]


def program(nc, patches, w_tok, rows, b1_col, g1_col, w_q, w_k, w_qs, w_ks, w_v, w_o, gate_w, log_xi,
            w_shared, d_shared, w_moe, consts, out):
    h_dram = nc.dram_tensor("h_rows", (TOK, D), F32).ap()
    v_dram = nc.dram_tensor("v_rows", (TOK, D), F32).ap()
    a_dram = nc.dram_tensor("attended_rows", (TOK, D), F32).ap()
    sent = nc.dram_tensor("dispatched_rows", (SPARE + P, ROW), F32).ap()
    sums = nc.dram_tensor("sums", (SUMS * (TOK + P), D), F32).ap()
    table_dram = nc.dram_tensor("tile_table", (2 * P, T_COLS), I32).ap()

    with ExitStack() as ctx:
        def sb(name, shape, dt=F32):
            return ctx.enter_context(nc.sbuf_tensor(name, shape, dt))

        def sem(name):
            return ctx.enter_context(nc.semaphore(name))

        banks = [ctx.enter_context(nc.psum_tensor(f"bank{i}", [P, 512], F32)) for i in range(8)]

        cst = sb("cst", [P, CONST_W])
        const = {n: cst[:, a:a + w] for n, (a, w) in CONST_AT.items()}
        ident = const["ident"]
        wt = sb("wt", [P, PC, D])
        wtg = sb("wtg", [P, PC, D])
        g1s = sb("g1s", [P, PC])
        b1s = sb("b1s", [P, PC])
        brow = sb("brow", [P, 3 * D + EXPERTS])
        tok_bias = sb("tok_bias", [P, D])
        g2b, b2b = brow[:, D:2 * D], brow[:, 2 * D:3 * D]
        gate_b = brow[:, 3 * D:]
        wq, wk, wqs, wks = sb("wq", [P, DC, D]), sb("wk", [P, DC, D]), sb("wqs", [P, DC, P]), sb("wks", [P, DC, P])
        wv, wo = sb("wv", [P, DC, D]), sb("wo", [P, DC, D])
        gw = sb("gw", [P, DC, EXPERTS])
        wsh = sb("wsh", [P, DC, 2 * SHARED])
        dsh = sb("dsh", [P, SHARED // P, D])
        xi = sb("xi", [P, HEADS])
        bias = sb("bias", [P, HEADS, SEQ])
        minus_half = sb("minus_half", [P, 1])
        hT = sb("hT", [P, DC, TOK])

        names = ("steps_settled pool_settled pe_settled sp_settled consts_in weights_in tok_w_in small_in late_in "
                 "half_set wtg_ready bias_mm tok_bias_ready xi_exp xi_rec bias_set "
                 "x_stats x_var x_rstd x_normed x_turned xT_out tok_mm "
                 "h_sum h_stats h_var h_rstd h_normed h_scaled h_ready h_turned hT_out v_mm v_out "
                 "qk_mm k_mul q_mul k_rot q_rot kexp_out q_out v_masked p_zero "
                 "scores_mm biased maxed shifted exped p_turned pT_act pT_dve pv_mm sum_inv attended "
                 "a_turned aT_out wo_mm r_sum r_stats r_var r_rstd h2_ready h2_turned h2T_out "
                 "gate_mm gate_sig score route_steps "
                 "top_inv h2_copied chosen ranked place "
                 "rows_ready counted counts_start zeros_set ids_made kept_h2 "
                 "tab slots_set table_set table_out table_in ends_out pads_out pads_out_pool sums_zeroed "
                 "sh_up_mm sh_silu sh_act sh_down_mm sh_added "
                 "x_turned_e xT_out_e meta up_mm silu act_ready act_turned actT_out down_mm y_ready "
                 "f_pairs f_first f_pool f_sum f_stats f_var f_rstd f_ready").split()
        S = {n: sem(n) for n in names}
        x_in, h_stored, v_stored = ([sem(f"{n}{u}") for u in range(A_SLOTS)] for n in ("x_in", "h_stored", "v_stored"))
        vrep_in, a_stored = [sem(f"vrep_in{r}") for r in range(PAIRS)], [sem(f"a_stored{u}") for u in range(2)]
        a_in, h_in = ([sem(f"{n}{u}") for u in range(2)] for n in ("a_in", "h_in"))
        o_stored, sums_in = ([sem(f"{n}{u}") for u in range(E_SLOTS)] for n in ("o_stored", "sums_in"))
        rows_sent = [sem(f"rows_sent{u}") for u in range(2)]
        w_in, rows_in, y_added = ([sem(f"{n}{u}") for u in range(SUMS)] for n in ("w_in", "rows_in", "y_added"))

        hl = sb("hl", [P, A_SLOTS, D])
        st2 = sb("st2", [P, A_SLOTS, 6])
        mv2 = sb("mv2", [P, A_SLOTS, 2])
        ve = sb("ve", [P, A_SLOTS, 1])
        rs = sb("rs", [P, A_SLOTS, 1])
        st = sb("st", [P, A_SLOTS, 2, 6])
        mv = sb("mv", [P, A_SLOTS, 2])
        ve2 = sb("ve2", [P, A_SLOTS, 1])
        rs2 = sb("rs2", [P, A_SLOTS, 1])
        qT = sb("qT", [P, 2, 2, CT])
        krot = sb("krot", [P, CT])
        kplain = sb("kplain", [P, CT])
        shared = sb("shared", [P, SHARED_W])

        def carve(start, shape, letters):
            size = 1
            for n in shape:
                size *= n
            flat = shared[:, start:start + size]
            names = letters.split()
            return flat.rearrange(f"p ({letters}) -> p {letters}", **dict(zip(names[1:], shape[1:]))), start + size

        xs, _n = carve(0, [A_SLOTS, PATCH], "u n")
        xT, _n = carve(_n, [A_SLOTS, PC, P], "u c n")
        hs, _n = carve(_n, [A_SLOTS, D], "u n")
        vs, _n = carve(_n, [A_SLOTS, D], "u n")
        hTs, _n = carve(_n, [A_SLOTS, DC, P], "u c n")
        assert _n <= SHARED_W
        kexp0, _n = carve(0, [2, HALF, CT], "a h t")
        vrep, _n = carve(_n, [PAIRS, 2, D], "r i d")
        vbd, _n = carve(_n, [PAIRS, 2, HEADS, VW], "r i h w")
        tmp, _n = carve(_n, [4, CT], "n t")
        assert _n <= SHARED_W
        sc = sb("sc", [P, 2, HEADS, SEQ])
        mx = sb("mx", [P, 2, HEADS])
        pr = sb("pr", [P, 2, HEADS * SEQ])
        pT = sb("pT", [P, 2, GROUPS, P])
        si = sb("si", [P, 2, HEADS])
        ao = sb("ao", [P, 2, D])
        ai = sb("ai", [P, 2, D])
        hi = sb("hi", [P, 2, D])
        aT = sb("aT", [P, 2, DC, P])
        h2Ts = sb("h2Ts", [P, 2, DC, P])
        h2 = sb("h2", [P, 2, D])
        dsp = sb("dsp", [P, 2, TOPK, ROW])
        rt = sb("rt", [P, 2, 3, EXPERTS])
        group_best = sb("group_best", [P, 2, 2, NGROUP])
        gi = sb("gi", [P, 2, NGROUP], U32)
        geq = sb("geq", [P, 2, TOPG, NGROUP])
        t8 = sb("t8", [P, 2, 8])
        ti = sb("ti", [P, 2, 8], U32)
        teq = sb("teq", [P, 2, TOPK, EXPERTS])
        tpl = sb("tpl", [P, 2, TOPK, EXPERTS])
        tsum = sb("tsum", [P, 2, 2])
        chosen = sb("chosen", [P, 2, EXPERTS])
        place = sb("place", [P, 2, EXPERTS])
        counts = sb("counts", [P, 2, EXPERTS])
        dest = sb("dest", [P, 2, TOPK])
        desti = sb("desti", [P, 2, TOPK], U32)
        ids = sb("ids", [P, TILES], U32)
        zeros = sb("zeros", [P, D])
        acc = sb("acc", [P, TILES, D])
        kexp = [kexp0, acc[:, :, :].rearrange("p t d -> p (t d)")[:, 0:2 * HALF * CT].rearrange("p (a h t) -> p a h t", a=2, h=HALF)]
        sha, _n = carve(W_SLOTS * 3 * D, [2, 2, SHARED], "u a n")
        tb = sb("tb", [P, 9, EXPERTS])
        tbi = sb("tbi", [P, EXPERTS], I32)
        tv = sb("tv", [P, 2, 8])
        tvi = sb("tvi", [P, 2, T_COLS], I32)
        ends = sb("ends", [1, EXPERTS], I32)
        table = sb("table", [1, 2 * P * T_COLS], I32)
        slot_row = sb("slot_row", [1, 2 * P], I32)
        moe, _n = carve(0, [W_SLOTS, 3 * D], "w n")
        xe = sb("xe", [P, SUMS, ROW])
        xeT = sb("xeT", [P, 2, DC, P])
        meta = sb("meta", [P, SUMS, 2])
        ids2 = sb("ids2", [P, SUMS], U32)
        sg = sb("sg", [P, 2, INTER])
        ae = sb("ae", [P, 2, INTER])
        aeT = sb("aeT", [P, 2, P])
        ye = sb("ye", [P, SUMS, D])
        si4, _n = carve(0, [E_SLOTS, SUMS, D], "u k d")
        assert _n <= SHARED_W
        of, _n = carve(_n, [E_SLOTS, D], "u d")

        block = ctx.enter_context(nc.Block())

        def rows_of(dram, t):
            return dram[bass.ds(t * P, P), :] if not isinstance(t, int) else dram[t * P:(t + 1) * P, :]

        def part_of(dram, t, rows):
            return dram[bass.ds(t * rows, rows), :] if not isinstance(t, int) else dram[t * rows:(t + 1) * rows, :]

        def cols_of(ap, t):
            return ap[:, :, bass.ds(t * P, P)] if not isinstance(t, int) else ap[:, :, t * P:(t + 1) * P]

        def at(ap, t):
            return ap[:, bass.ds(t, 1), :].rearrange("p a b -> p (a b)") if not isinstance(t, int) else ap[:, t, :]

        def in_slot(u):
            return (TILES - u + E_SLOTS - 1) // E_SLOTS

        def walk_pairs(eng, steps, before=()):
            walk(eng, IMAGES // 2, steps, 2 * PAIRS, before=before)

        def pads_out(eng, engine, first, past, signal):
            with eng.Fori(first // 4, past // 4) as e:
                _, some_ends = nc.values_load_multi_w_load_instructions(
                    ends[0:1, bass.ds(4 * e, 4)], engines=(engine,), min_val=0, max_val=SPARE - P,
                    skip_runtime_bounds_check_because="an expert has at most TOK rows in its region of TOK + P")
                for end in some_ends:
                    eng.dma_start(sent[bass.ds(end, P), :], const["pad_row"]).then_inc(S[signal], 16)

        def table_row(n):
            return table[0:1, n * T_COLS:(n + 1) * T_COLS] if isinstance(n, int) else table[0:1, bass.ds(n * T_COLS, T_COLS)]


        @block.sync
        def _(sp):
            sp.dma_start(cst[:, :], consts).then_inc(S["consts_in"], 16)
            sp.dma_start(g1s[:, :], g1_col).then_inc(S["tok_w_in"], 16)
            sp.dma_start(b1s[:, :], b1_col).then_inc(S["tok_w_in"], 16)
            sp.dma_start(wt[:, :, :], w_tok).then_inc(S["tok_w_in"], 16)

            def load_x(t, n, u):
                wait(sp, S["x_turned"], t - A_SLOTS + 1)
                sp.dma_start(xs[:, u, :], rows_of(patches, t)).then_inc(x_in[u], 16)
                if isinstance(t, int) and t == 0:
                    sp.dma_start(brow[:, :], rows.to_broadcast([P, 3 * D + EXPERTS])).then_inc(S["small_in"], 16)
                    sp.dma_start(xi[:, :], log_xi.to_broadcast([P, HEADS])).then_inc(S["small_in"], 16)
                if isinstance(t, int) and t == 1:
                    for dst, src in ((wv, w_v), (wq, w_q), (wk, w_k), (wqs, w_qs), (wks, w_ks)):
                        sp.dma_start(dst[:, :, :], src).then_inc(S["weights_in"], 16)
                if isinstance(t, int) and t == 2 * A_SLOTS:
                    for dst, src in ((wo, w_o), (gw, gate_w), (wsh, w_shared), (dsh, d_shared)):
                        sp.dma_start(dst[:, :, :], src).then_inc(S["late_in"], 16)

            def store_h(t, n, u):
                sp.wait_ge(S["h_ready"], t + 1)
                sp.dma_start(rows_of(h_dram, t), hs[:, u, :]).then_inc(h_stored[u], 16)

            walk(sp, TILES, [(load_x, 0), (store_h, 4)], A_SLOTS)
            for u in range(A_SLOTS):
                sp.wait_ge(v_stored[u], 16 * (TILES // A_SLOTS))
                sp.wait_ge(h_stored[u], 16 * (TILES // A_SLOTS))
            sp.wait_ge(S["zeros_set"], 1)

            def load_v(t, n, u):
                wait(sp, S["v_masked"], t - PAIRS + 1)
                for c in range(TRI):
                    sp.dma_start(vrep[c * SEQ:(c + 1) * SEQ, u % PAIRS, :, :],
                                 part_of(v_dram, t, 2 * SEQ).rearrange("(i k) d -> k i d", k=SEQ)).then_inc(vrep_in[u % PAIRS], 16)

            def zero_sums(t, n, u):
                rows = SUMS * (TOK + P) // (IMAGES // 2)
                sp.dma_start(part_of(sums, t, rows).rearrange("(t p) d -> p t d", t=4),
                             zeros[0:rows // 4, :].rearrange("p (a d) -> p a d", a=1).to_broadcast([rows // 4, 4, D])).then_inc(S["sums_zeroed"], 16)

            def store_a(t, n, u):
                sp.wait_ge(S["attended"], t + 1)
                for i in range(2):
                    sp.dma_start(part_of(a_dram, 2 * t + i, SEQ), ao[64 * i:64 * i + SEQ, u % 2, :]).then_inc(a_stored[u % 2], 16)

            def load_c(t, n, u):
                if isinstance(t, int) and t < 2:
                    for k in range(2):
                        sp.wait_ge(a_stored[k], 32 * -(-(t + 1) * P // (4 * SEQ)))
                wait(sp, S["a_turned"], t - 1)
                sp.dma_start(ai[:, u, :], rows_of(a_dram, t)).then_inc(a_in[u], 16)
                wait(sp, S["r_sum"], t - 1)
                sp.dma_start(hi[:, u, :], rows_of(h_dram, t)).then_inc(h_in[u], 16)

            def store_last(t, n, u):
                if isinstance(t, int) and t == IMAGES // 2 - 1:
                    load_c(0, 0, 0)
                    load_c(1, 0, 1)
                store_a(t, n, u)

            walk_pairs(sp, [(load_v, 0), (zero_sums, 0), (store_last, SETUP + 2)])
            for u in range(2):
                sp.wait_ge(a_stored[u], 16 * 2 * CHUNKS * PAIRS // 2)

            def load_rest(t, n, u):
                if not isinstance(t, int) or t >= 2:
                    load_c(t, n, u)

            walk(sp, TILES, [(load_rest, 0)])

            sp.wait_ge(S["ends_out"], 1)
            sp.dma_start(sent[SPARE:SPARE + P, :], const["pad_row"]).then_inc(S["pads_out"], 16)
            pads_out(sp, ENG.SP, POOL_PADS + ACT_PADS, EXPERTS, "pads_out")
            sp.wait_ge(S["table_in"], 16)
            for u in range(2):
                sp.wait_ge(rows_sent[u], 16 * TOPK * (TILES // 2))
            sp.wait_ge(S["pads_out"], 16 * (EXPERTS - POOL_PADS + 1))
            sp.wait_ge(S["pads_out_pool"], 16 * POOL_PADS)
            sp.wait_ge(S["sums_zeroed"], 16 * (IMAGES // 2))

            def load_e(n, v, u):
                off, expert, slot, load = entries(nc, ENG.SP, table_row(n))
                wait(sp, S["meta"], n - SUMS + 1)
                wait(sp, S["x_turned_e"], n - SUMS + 1)
                settled(sp, S["sp_settled"])
                sp.dma_start(xe[:, u, :], sent[bass.ds(off, P), :]).then_inc(rows_in[u], 16)
                wait(sp, S["down_mm"], n - W_SLOTS + 1)
                settled(sp, S["sp_settled"])
                wait(sp, w_in[u], 16 * v)
                settled(sp, S["sp_settled"])
                sp.dma_start(moe[:, bass.ds(slot, 1), :].rearrange("p a n -> p (a n)"),
                             w_moe[bass.ds(expert, 1), :, :].rearrange("a p n -> (a p) n"), cond=load).then_inc(w_in[u], 16)

            walk(sp, E_TILES, [(load_e, 0)], SUMS, peel=W_SLOTS)

            for k in range(SUMS):
                sp.wait_ge(y_added[k], 16 * (E_TILES // SUMS))

            def load_sums(t, n, u):
                wait(sp, S["f_sum"], t - E_SLOTS + 1)
                each = sums.rearrange("(k n) d -> n k d", k=SUMS)
                rows = each[bass.ds(t * P, P), :, :] if not isinstance(t, int) else each[t * P:(t + 1) * P, :, :]
                sp.dma_start(si4[:, u, :, :], rows).then_inc(sums_in[u], 16)

            walk(sp, TILES, [(load_sums, 0)], E_SLOTS)
            for u in range(E_SLOTS):
                sp.wait_ge(o_stored[u], 16 * in_slot(u))

        @block.gpsimd
        def _(pool):
            pool.memset(minus_half[:, :], -0.5).then_inc(S["half_set"], 1)
            pool.memset(pr[:, :, :], 0.0).then_inc(S["p_zero"], 1)
            pool.memset(zeros[:, :], 0.0).then_inc(S["zeros_set"], 1)
            pool.memset(counts[:, 0, :], 0.0).then_inc(S["counts_start"], 1)
            pool.iota(ids[:, :], [[P, TILES]], base=0, channel_multiplier=1).then_inc(S["ids_made"], 1)
            pool.wait_ge(S["half_set"], 1)

            def power(name_in, name_out, src, dst, slots=2):
                def step(t, n, u):
                    pool.wait_ge(S[name_in], t + 1)
                    pool.tensor_tensor(dst[:, u % slots, :], src[:, u % slots, :], minus_half[:, :], ALU.pow).then_inc(S[name_out], 1)
                return step

            def h_affine(t, n, u):
                if isinstance(t, int) and t == 0:
                    pool.wait_ge(S["small_in"], 32)
                pool.wait_ge(S["h_normed"], t + 1)
                wait(pool, h_stored[u], 16 * n)
                wait(pool, S["h_turned"], t - A_SLOTS + 1)
                settled(pool, S["pool_settled"])
                pool.tensor_tensor(hs[:, u, :], hl[:, u, :], g2b, ALU.mult).then_inc(S["h_scaled"], 1)
                pool.wait_ge(S["h_scaled"], t + 1)
                pool.tensor_tensor(hs[:, u, :], hs[:, u, :], b2b, ALU.add).then_inc(S["h_ready"], 1)

            tail = walk(pool, TILES, [(power("x_var", "x_rstd", ve, rs, A_SLOTS), 0), (power("h_var", "h_rstd", ve2, rs2, A_SLOTS), 3), (h_affine, 3)], A_SLOTS, hold=True)

            v_mask = const["v_heads"][0:TRI * SEQ, :]
            pool.wait_ge(S["consts_in"], 16)

            def mask_v(t, n, u):
                r = u % PAIRS
                pool.wait_ge(vrep_in[r], 16 * TRI * (2 * n + u // PAIRS + 1))
                wait(pool, S["pv_mm"], t - PAIRS + 1)
                if isinstance(t, int) and t == 0:
                    pool.tensor_copy(vbd[0:TRI * SEQ, :, :, :, DH].rearrange("p r i h -> p (r i) h"),
                                     v_mask.rearrange("p (a h) -> p a h", a=1).to_broadcast([TRI * SEQ, CI, HEADS]))
                for i in range(2):
                    last = pool.tensor_tensor(
                        vbd[0:TRI * SEQ, r, i, :, 0:DH], vrep[0:TRI * SEQ, r, i, :].rearrange("p (h d) -> p h d", h=HEADS),
                        v_mask.rearrange("p (h a) -> p h a", a=1).to_broadcast([TRI * SEQ, HEADS, DH]), ALU.mult)
                last.then_inc(S["v_masked"], 1)

            def shift(t, n, u):
                pool.wait_ge(S["maxed"], t + 1)
                pool.tensor_tensor(sc[0:QP, u % 2, :, :], sc[0:QP, u % 2, :, :],
                                   mx[0:QP, u % 2, :].rearrange("p (h a) -> p h a", a=1).to_broadcast([QP, HEADS, SEQ]),
                                   ALU.subtract).then_inc(S["shifted"], 1)

            walk_pairs(pool, [(shift, SETUP), (mask_v, SETUP)], tail)

            def send(t, n, u):
                pool.wait_ge(S["rows_ready"], t + 1)
                pool.wait_ge(S["h2_copied"], t + 1)
                settled(pool, S["pool_settled"])
                for j in range(TOPK):
                    pool.indirect_dma_start(sent, bass.IndirectOffsetOnAxis(ap=desti[:, u, j:j + 1], axis=0),
                                            dsp[:, u, j, :], None).then_inc(rows_sent[u], 16)

            walk(pool, TILES, [(power("r_var", "r_rstd", ve, rs), 1), (send, 5)])

            pool.wait_ge(S["ends_out"], 1)
            pads_out(pool, ENG.Pool, 0, POOL_PADS, "pads_out_pool")

            def meta_out(n, v, u):
                pool.wait_ge(rows_in[u], 16 * (v + 1))
                wait(pool, S["y_ready"], n - SUMS + 1)
                settled(pool, S["pool_settled"])
                pool.tensor_copy(meta[:, u, :], xe[:, u, D:ROW]).then_inc(S["meta"], 1)

            def add_y(n, v, u):
                pool.wait_ge(S["y_ready"], n + 1)
                wait(pool, y_added[u], 16 * v)
                settled(pool, S["pool_settled"])
                pool.indirect_dma_start(sums, bass.IndirectOffsetOnAxis(ap=ids2[:, u:u + 1], axis=0),
                                        ye[:, u, :], None, compute_op=ALU.add).then_inc(y_added[u], 16)

            pool.wait_ge(S["sums_zeroed"], 16 * (IMAGES // 2))
            walk(pool, E_TILES, [(meta_out, 1), (add_y, 4)], SUMS)

            def f_pool(t, n, u):
                pool.wait_ge(sums_in[u], 16 * (n + 1))
                pool.tensor_tensor(si4[:, u, 2, :], si4[:, u, 2, :], si4[:, u, 3, :], ALU.add).then_inc(S["f_pool"], 1)

            walk(pool, TILES, [(f_pool, 0), (power("f_var", "f_rstd", ve, rs), 1)], E_SLOTS)

        @block.scalar
        def _(act):
            act.wait_ge(S["small_in"], 32)
            act.activation(xi[:, :], xi[:, :], ACT.Exp).then_inc(S["xi_exp"], 1)

            def x_out(t, n, u):
                act.wait_ge(S["x_turned"], t + 1)
                wait(act, S["tok_mm"], t - A_SLOTS + 1)
                for c in range(2):
                    last = act.activation(xT[:, u, 3 * c:3 * c + 3, :], banks[c][:, 0:3 * P], ACT.Copy)
                last.then_inc(S["xT_out"], 1)

            def hT_out(t, n, u):
                act.wait_ge(S["h_turned"], t + 1)
                wait(act, S["v_mm"], t - A_SLOTS + 1)
                turned = banks[5][:, 0:D].rearrange("p (c k) -> p c k", c=DC)
                act.activation(hTs[:, u, :, :], turned, ACT.Copy)
                act.activation(cols_of(hT, t), turned, ACT.Copy).then_inc(S["hT_out"], 1)

            def v_out(t, n, u):
                act.wait_ge(S["v_mm"], t + 1)
                wait(act, v_stored[u], 16 * n)
                act.activation(vs[:, u, :], banks[6][:, 0:D], ACT.Copy).then_inc(S["v_out"], 1)
                act.wait_ge(S["v_out"], t + 1)
                act.dma_start(rows_of(v_dram, t), vs[:, u, :]).then_inc(v_stored[u], 16)

            tail = walk(act, TILES, [(hT_out, 4), (v_out, 5), (x_out, 0)], A_SLOTS, hold=True)

            act.wait_ge(S["consts_in"], 16)
            act.wait_ge(S["p_zero"], 1)

            def spread_k(t, n, u):
                c, r, k_out = 2 * n + u // PAIRS, u % PAIRS, kexp[u // PAIRS]

                def spread(half, src, first, past):
                    for h in range(first, past):
                        last = act.activation(k_out[:, half, h, :], src[:, :], ACT.Copy, scale=const["k_heads"][:, h:h + 1])
                    return last

                if r == 1:
                    act.wait_ge(S["q_out"], c + 1)
                    if isinstance(t, int) and c == 0:
                        act.wait_ge(S["tok_mm"], TILES)
                    wait(act, S["scores_mm"], (c - 1) * PAIRS)
                    spread(1, kplain, 0, 5)
                if r == 2:
                    spread(1, kplain, 5, HALF).then_inc(S["kexp_out"], 1)
                    act.wait_ge(S["k_rot"], c + 1)
                    spread(0, krot, 0, 2)
                if r == 3:
                    spread(0, krot, 2, HALF).then_inc(S["kexp_out"], 1)

            def exps(t, n, u):
                act.wait_ge(S["shifted"], t + 1)
                wait(act, S["p_turned"], t - 1)
                act.activation(pr[0:QP, u % 2, :], sc[0:QP, u % 2, :, :], ACT.Exp).then_inc(S["exped"], 1)

            def pT_out(t, n, u):
                act.wait_ge(S["p_turned"], t + 1)
                wait(act, S["pv_mm"], t - 1)
                act.activation(pT[0:TRI * SEQ, u % 2, 0:4, 0:QP], banks[2][0:TRI * SEQ, 0:4 * QP].rearrange("p (g q) -> p g q", g=4),
                               ACT.Copy).then_inc(S["pT_act"], 1)

            walk_pairs(act, [(spread_k, 0), (pT_out, SETUP + 1), (exps, SETUP)], tail)

            def aT_out(t, n, u):
                act.wait_ge(S["a_turned"], t + 1)
                wait(act, S["wo_mm"], t - 1)
                act.activation(aT[:, u, :, :], banks[0][:, 0:D], ACT.Copy).then_inc(S["aT_out"], 1)

            def h2T_out(t, n, u):
                act.wait_ge(S["h2_turned"], t + 1)
                wait(act, S["gate_mm"], t - 1)
                wait(act, S["sh_up_mm"], t - 1)
                act.activation(h2Ts[:, u, :, :], banks[2][:, 0:D], ACT.Copy).then_inc(S["h2T_out"], 1)

            def gate_out(t, n, u):
                act.wait_ge(S["gate_mm"], t + 1)
                wait(act, S["score"], t - 1)
                act.activation(rt[:, u, 0, :], banks[3][:, 0:EXPERTS], ACT.Sigmoid).then_inc(S["gate_sig"], 1)

            def keep_h2(t, n, u):
                act.wait_ge(S["h2_ready"], t + 1)
                act.activation(at(acc, t), h2[:, u, :], ACT.Copy).then_inc(S["kept_h2"], 1)

            def shared_silu(t, n, u):
                act.wait_ge(S["sh_up_mm"], t + 1)
                wait(act, S["sh_act"], t - 1)
                act.activation(sha[:, u, 0, :], banks[6][:, 0:SHARED], ACT.Silu).then_inc(S["sh_silu"], 1)

            def copy_h2(t, n, u):
                act.wait_ge(S["kept_h2"], t + 1)
                wait(act, rows_sent[u], 16 * TOPK * n)
                row = acc[:, bass.ds(t, 1), :] if not isinstance(t, int) else acc[:, t:t + 1, :]
                act.activation(dsp[:, u, :, 0:D], row.to_broadcast([P, TOPK, D]), ACT.Copy).then_inc(S["h2_copied"], 1)

            walk(act, TILES, [(h2T_out, 2), (aT_out, 0), (keep_h2, 2), (gate_out, 2), (shared_silu, 3), (copy_h2, 4)])

            act.wait_ge(S["ends_out"], 1)
            pads_out(act, ENG.Activation, POOL_PADS, POOL_PADS + ACT_PADS, "pads_out")
            act.wait_ge(S["table_set"], 1)
            act.dma_start(table_dram.rearrange("(b p) c -> p b c", p=P), tvi[:, :, :]).then_inc(S["table_out"], 16)
            act.wait_ge(S["table_out"], 16)
            act.dma_start(table[:, :], table_dram.rearrange("(a n) c -> a (n c)", a=1)).then_inc(S["table_in"], 16)

            def xeT_out(n, v, u):
                act.wait_ge(S["x_turned_e"], n + 1)
                wait(act, S["up_mm"], n - 1)
                act.activation(xeT[:, u % 2, :, :], banks[u % 2][:, 0:D], ACT.Copy).then_inc(S["xT_out_e"], 1)

            def silu(n, v, u):
                act.wait_ge(S["up_mm"], n + 1)
                wait(act, S["act_ready"], n - 1)
                act.activation(sg[:, u % 2, :], banks[2 + u % 2][:, 0:INTER], ACT.Silu).then_inc(S["silu"], 1)

            def aeT_out(n, v, u):
                act.wait_ge(S["act_turned"], n + 1)
                wait(act, S["down_mm"], n - 1)
                act.activation(aeT[:, u % 2, :], banks[4 + u % 2][:, 0:P], ACT.Copy).then_inc(S["actT_out"], 1)

            walk(act, E_TILES, [(silu, 2), (aeT_out, 3), (xeT_out, 0)], SUMS)

            def store_o(t, n, u):
                act.wait_ge(S["f_ready"], t + 1)
                act.dma_start(rows_of(out, t), of[:, u, :]).then_inc(o_stored[u], 16)

            walk(act, TILES, [(store_o, 0)], E_SLOTS)

        @block.vector
        def _(dve):
            dve.wait_ge(S["tok_w_in"], 48)
            for c in range(PC):
                last = dve.tensor_scalar(wtg[:, c, :], wt[:, c, :], g1s[:, c:c + 1], None, ALU.mult)
            last.then_inc(S["wtg_ready"], 1)

            def set_tok_bias():
                dve.wait_ge(S["small_in"], 32)
                dve.wait_ge(S["bias_mm"], 1)
                dve.tensor_tensor(tok_bias[:, :], banks[7][:, 0:D], brow[:, 0:D], ALU.add).then_inc(S["tok_bias_ready"], 1)
                dve.wait_ge(S["tok_bias_ready"], 1)

            def set_score_bias():
                dve.wait_ge(S["xi_exp"], 1)
                dve.wait_ge(S["consts_in"], 16)
                dve.reciprocal(xi[:, :], xi[:, :]).then_inc(S["xi_rec"], 1)
                dve.wait_ge(S["xi_rec"], 1)
                dve.tensor_tensor(xi[:, :], xi[:, :], const["decays"], ALU.mult).then_inc(S["xi_rec"], 1)
                dve.wait_ge(S["xi_rec"], 2)
                for h in range(HEADS):
                    last = dve.scalar_tensor_tensor(out=bias[:, h, :], in0=const["dist"], scalar=xi[:, h:h + 1],
                                                    in1=const["causal"], op0=ALU.mult, op1=ALU.add)
                last.then_inc(S["bias_set"], 1)

            def norm_steps(srcs, stats, mean_var, var_eps, eps, s_stats, s_var, slots=2):
                def bn(t, n, u):
                    parts = srcs(u)
                    for k, src in enumerate(parts):
                        last = dve.bn_stats(stats[:, u % slots, k, :] if len(parts) > 1 else stats[:, u % slots, :], src)
                    last.then_inc(S[s_stats], 1)

                def aggregate(t, n, u):
                    dve.wait_ge(S[s_stats], 2 * t + 1)
                    settled(dve, S["steps_settled"])
                    both = stats[:, u % slots]
                    dve.bn_aggr(mean_var[:, u % slots, :], both.rearrange("p a b -> p (a b)") if len(both.shape) > 2 else both).then_inc(S[s_stats], 1)

                def add_eps(t, n, u):
                    dve.wait_ge(S[s_stats], 2 * t + 2)
                    dve.tensor_scalar(var_eps[:, u % slots, :], mean_var[:, u % slots, 1:2], eps, None, ALU.add).then_inc(S[s_var], 1)

                return bn, aggregate, add_eps

            x_bn, x_aggr, x_eps = norm_steps(lambda u: [xs[:, u, 0:PATCH // 2], xs[:, u, PATCH // 2:]], st, mv, ve, TOK_EPS, "x_stats", "x_var", A_SLOTS)
            h_bn, h_aggr, h_eps = norm_steps(lambda u: [hl[:, u, :]], st2, mv2, ve2, TOK_EPS, "h_stats", "h_var", A_SLOTS)

            def x_start(t, n, u):
                dve.wait_ge(x_in[u], 16 * (n + 1))
                x_bn(t, n, u)

            def x_norm(t, n, u):
                dve.wait_ge(S["x_rstd"], t + 1)
                dve.tensor_scalar(xs[:, u, :], xs[:, u, :], mv[:, u, 0:1], rs[:, u, :], ALU.subtract, ALU.mult).then_inc(S["x_normed"], 1)

            def h_sum(t, n, u):
                if isinstance(t, int) and t == 0:
                    set_tok_bias()
                dve.wait_ge(S["tok_mm"], t + 1)
                wait(dve, S["h_scaled"], t - A_SLOTS + 1)
                dve.tensor_tensor(hl[:, u, :], banks[2 + u][:, 0:D], tok_bias[:, :], ALU.add).then_inc(S["h_sum"], 1)

            def h_start(t, n, u):
                dve.wait_ge(S["h_sum"], t + 1)
                h_bn(t, n, u)

            def h_norm(t, n, u):
                if isinstance(t, int) and t == 1:
                    set_score_bias()
                dve.wait_ge(S["h_rstd"], t + 1)
                dve.tensor_scalar(hl[:, u, :], hl[:, u, :], mv2[:, u, 0:1], rs2[:, u, :], ALU.subtract, ALU.mult).then_inc(S["h_normed"], 1)

            tail = walk(dve, TILES, [(x_start, 0), (h_sum, 3), (x_aggr, 0), (h_start, 3), (x_eps, 0), (h_aggr, 3), (h_eps, 3), (x_norm, 0), (h_norm, 3)], A_SLOTS, hold=True)

            def per_image(ap):
                return ap.rearrange("p (a k) -> p a k", a=1).to_broadcast([P, CI, SEQ])

            def images(ap):
                return ap.rearrange("p (i k) -> p i k", i=CI)

            def rotate(t, n, u):
                c, r = 2 * n + u // PAIRS, u % PAIRS
                if r == 3:
                    return
                dve.wait_ge(S["qk_mm"], 3 * c + 1 + r)
                if r == 0:
                    wait(dve, S["scores_mm"], (c - 1) * PAIRS)
                    wait(dve, S["kexp_out"], 2 * c - 1)
                    dve.tensor_copy(qT[:, u // PAIRS, 1, :], banks[0][:, 0:CT])
                    dve.tensor_copy(kplain[:, :], banks[1][:, 0:CT]).then_inc(S["q_out"], 1)
                    return
                mul, done, out = (("k_mul", "k_rot", krot[:, :]), ("q_mul", "q_rot", qT[:, u // PAIRS, 0, :]))[r - 1]
                part = tmp[:, 2 * (r - 1):2 * r, :]
                wait(dve, S[done], c)
                for k, table in enumerate(("cos", "sin")):
                    dve.tensor_tensor(images(part[:, k, :]), images(banks[k][:, 0:CT]), per_image(const[table]), ALU.mult).then_inc(S[mul], 1)
                dve.wait_ge(S[mul], 2 * c + 2)
                if r == 1:
                    wait(dve, S["kexp_out"], 2 * c)
                else:
                    wait(dve, S["scores_mm"], (c - 1) * PAIRS)
                dve.tensor_tensor(out, part[:, 0, :], part[:, 1, :], ALU.add).then_inc(S[done], 1)

            def soft(t, n, u):
                dve.wait_ge(S["scores_mm"], t + 1)
                wait(dve, S["exped"], t - 1)
                for half in range(2):
                    last = dve.scalar_tensor_tensor(
                        out=sc[0:QP, u % 2, half * HALF:(half + 1) * HALF, :].rearrange("p h k -> p (h k)"),
                        in0=banks[6 + half][0:QP, 0:HALF * SEQ], scalar=DH ** -0.5,
                        in1=bias[0:QP, half * HALF:(half + 1) * HALF, :].rearrange("p h k -> p (h k)"),
                        op0=ALU.mult, op1=ALU.add)
                last.then_inc(S["biased"], 1)
                dve.wait_ge(S["biased"], t + 1)
                dve.tensor_reduce(mx[0:QP, u % 2, :], sc[0:QP, u % 2, :, :], AX.X, ALU.max).then_inc(S["maxed"], 1)

            def pT_out(t, n, u):
                dve.wait_ge(S["p_turned"], t + 1)
                wait(dve, S["pv_mm"], t - 1)
                dve.tensor_copy(pT[0:TRI * SEQ, u % 2, 4, 0:QP], banks[3][0:TRI * SEQ, 0:QP])
                dve.tensor_copy(pT[0:SEQ, u % 2, 5, 0:QP], banks[3][0:SEQ, QP:2 * QP]).then_inc(S["pT_dve"], 1)

            def divide(t, n, u):
                o = banks[4 + u % 2][0:QP, 0:HEADS * VW].rearrange("p (h w) -> p h w", w=VW)
                dve.wait_ge(S["pv_mm"], t + 1)
                dve.reciprocal(si[0:QP, u % 2, :], o[:, :, DH]).then_inc(S["sum_inv"], 1)
                dve.wait_ge(S["sum_inv"], t + 1)
                wait(dve, a_stored[u % 2], 32 * (n * PAIRS + u // 2))
                dve.tensor_tensor(ao[0:QP, u % 2, :].rearrange("p (h d) -> p h d", h=HEADS), o[:, :, 0:DH],
                                  si[0:QP, u % 2, :].rearrange("p (h a) -> p h a", a=1).to_broadcast([QP, HEADS, DH]),
                                  ALU.mult).then_inc(S["attended"], 1)

            walk_pairs(dve, [(soft, SETUP), (rotate, 0), (pT_out, SETUP + 1), (divide, SETUP + 2)], tail)

            def r_sum(t, n, u):
                dve.wait_ge(S["wo_mm"], t + 1)
                dve.wait_ge(h_in[u], 16 * (n + 1))
                dve.tensor_tensor(hl[:, u, :], banks[1][:, 0:D], hi[:, u, :], ALU.add).then_inc(S["r_sum"], 1)

            r_bn, r_aggr, r_eps = norm_steps(lambda u: [hl[:, u, :]], st2, mv2, ve, LN_EPS, "r_stats", "r_var")

            def r_start(t, n, u):
                dve.wait_ge(S["r_sum"], t + 1)
                r_bn(t, n, u)

            def r_norm(t, n, u):
                dve.wait_ge(S["r_rstd"], t + 1)
                wait(dve, S["h2_turned"], t - 1)
                wait(dve, S["kept_h2"], t - 1)
                dve.tensor_scalar(h2[:, u, :], hl[:, u, :], mv2[:, u, 0:1], rs[:, u, :], ALU.subtract, ALU.mult).then_inc(S["h2_ready"], 1)

            ROUTE = 10

            def after(k, t):
                dve.wait_ge(S["route_steps"], ROUTE * t + k)

            def beside(ap, axis, sizes):
                return ap.rearrange("p (x a) -> p x a" if axis == 2 else "p (a x) -> p a x", a=1).to_broadcast([P] + sizes)

            def by_group(ap):
                return ap.rearrange("p (g e) -> p g e", g=NGROUP)

            def add_bias(t, n, u):
                dve.wait_ge(S["gate_sig"], t + 1)
                dve.tensor_tensor(rt[:, u, 1, :], rt[:, u, 0, :], gate_b, ALU.add).then_inc(S["score"], 1)

            def group_max(t, n, u):
                dve.wait_ge(S["score"], t + 1)
                dve.tensor_reduce(group_best[:, u, 0, :], by_group(rt[:, u, 1, :]), AX.X, ALU.max).then_inc(S["route_steps"], 1)

            def group_top(t, n, u):
                after(1, t)
                settled(dve, S["steps_settled"])
                dve.max(group_best[:, u, 1, :], group_best[:, u, 0, :]).then_inc(S["route_steps"], 1)

            def group_index(t, n, u):
                after(2, t)
                settled(dve, S["steps_settled"])
                dve.max_index(gi[:, u, :], group_best[:, u, 1, :], group_best[:, u, 0, :]).then_inc(S["route_steps"], 1)

            def group_equal(t, n, u):
                after(3, t)
                dve.tensor_tensor(geq[:, u, :, :], beside(gi[:, u, 0:TOPG], 2, [TOPG, NGROUP]), beside(const["groups"], 1, [TOPG, NGROUP]),
                                  ALU.is_equal).then_inc(S["route_steps"], 1)

            def group_mask(t, n, u):
                after(4, t)
                dve.tensor_reduce(group_best[:, u, 0, :], geq[:, u, :, :].rearrange("p j g -> p g j"), AX.X, ALU.add).then_inc(S["route_steps"], 1)

            def mask_scores(t, n, u):
                after(5, t)
                dve.tensor_tensor(by_group(rt[:, u, 2, :]), by_group(rt[:, u, 1, :]), beside(group_best[:, u, 0, :], 2, [NGROUP, EXPERTS // NGROUP]),
                                  ALU.mult).then_inc(S["route_steps"], 1)

            def top(t, n, u):
                after(6, t)
                settled(dve, S["steps_settled"])
                dve.max(t8[:, u, :], rt[:, u, 2, :]).then_inc(S["route_steps"], 1)

            def top_index(t, n, u):
                after(7, t)
                settled(dve, S["steps_settled"])
                dve.max_index(ti[:, u, :], t8[:, u, :], rt[:, u, 2, :]).then_inc(S["route_steps"], 1)

            def top_sum(t, n, u):
                after(7, t)
                dve.tensor_reduce(tsum[:, u, 0:1], t8[:, u, 0:TOPK], AX.X, ALU.add).then_inc(S["route_steps"], 1)

            def top_equal(t, n, u):
                after(8, t)
                dve.tensor_tensor(teq[:, u, :, :], beside(ti[:, u, 0:TOPK], 2, [TOPK, EXPERTS]), beside(const["experts"], 1, [TOPK, EXPERTS]),
                                  ALU.is_equal).then_inc(S["route_steps"], 1)

            def top_eps(t, n, u):
                after(9, t)
                dve.tensor_scalar(tsum[:, u, 1:2], tsum[:, u, 0:1], 1e-8, None, ALU.add).then_inc(S["top_inv"], 1)

            def choose(t, n, u):
                after(10, t)
                wait(dve, S["ranked"], t - 1)
                dve.tensor_reduce(chosen[:, u, :], teq[:, u, :, :].rearrange("p j g -> p g j"), AX.X, ALU.add).then_inc(S["chosen"], 1)

            def top_inverse(t, n, u):
                dve.wait_ge(S["top_inv"], 2 * t + 1)
                dve.reciprocal(tsum[:, u, 0:1], tsum[:, u, 1:2]).then_inc(S["top_inv"], 1)

            def count(t, n, u):
                dve.wait_ge(S["ranked"], t + 1)
                dve.tensor_tensor(place[:, u, :], banks[4 + u][:, 0:EXPERTS], counts[:, u, :], ALU.add).then_inc(S["place"], 1)
                dve.tensor_tensor(counts[:, 1 - u, :], banks[4 + u][:, EXPERTS:2 * EXPERTS], counts[:, u, :], ALU.add).then_inc(S["counted"], 1)

            def place_all(t, n, u):
                dve.wait_ge(S["place"], 4 * t + 1)
                dve.wait_ge(S["counted"], t + 1)
                dve.tensor_tensor(place[:, u, :], place[:, u, :], const["region"], ALU.add).then_inc(S["place"], 1)

            def place_chosen(t, n, u):
                dve.wait_ge(S["place"], 4 * t + 2)
                dve.tensor_tensor(tpl[:, u, :, :], teq[:, u, :, :], beside(place[:, u, :], 1, [TOPK, EXPERTS]), ALU.mult).then_inc(S["place"], 1)

            def place_sum(t, n, u):
                dve.wait_ge(S["place"], 4 * t + 3)
                dve.tensor_reduce(dest[:, u, :], tpl[:, u, :, :], AX.X, ALU.add).then_inc(S["place"], 1)

            def finish_rows(t, n, u):
                dve.wait_ge(S["place"], 4 * t + 4)
                dve.wait_ge(S["top_inv"], 2 * t + 2)
                wait(dve, rows_sent[u], 16 * TOPK * n)
                i = ids[:, t:t + 1] if isinstance(t, int) else ids[:, bass.ds(t, 1)]
                dve.tensor_copy(dsp[:, u, :, D + 1].bitcast(U32), i.to_broadcast([P, TOPK]))
                dve.tensor_scalar(dsp[:, u, :, D], t8[:, u, 0:TOPK], tsum[:, u, 0:1], None, ALU.mult)
                dve.tensor_copy(desti[:, u, :], dest[:, u, :]).then_inc(S["rows_ready"], 1)

            def shared_multiply(t, n, u):
                dve.wait_ge(S["sh_silu"], t + 1)
                wait(dve, S["sh_down_mm"], t - 1)
                dve.tensor_tensor(sha[:, u, 1, :], sha[:, u, 0, :], banks[6][:, SHARED:2 * SHARED], ALU.mult).then_inc(S["sh_act"], 1)

            def shared_add(t, n, u):
                dve.wait_ge(S["sh_down_mm"], t + 1)
                dve.wait_ge(S["h2_copied"], t + 1)
                dve.tensor_tensor(at(acc, t), banks[7][:, 0:D], at(acc, t), ALU.add).then_inc(S["sh_added"], 1)

            dve.wait_ge(S["counts_start"], 1)
            dve.wait_ge(S["ids_made"], 1)
            walk(dve, TILES, [(r_sum, 1), (add_bias, 3), (r_start, 1), (group_max, 3), (r_aggr, 1), (group_top, 3), (r_eps, 1),
                              (count, 4), (group_index, 3), (shared_add, 6), (group_equal, 3), (place_all, 4), (group_mask, 3),
                              (r_norm, 1), (mask_scores, 3), (place_chosen, 4), (top, 3), (shared_multiply, 4), (top_index, 3),
                              (place_sum, 4), (top_sum, 3), (top_equal, 3), (top_eps, 3), (finish_rows, 4), (choose, 3), (top_inverse, 3)])

            step = [0]

            def then(ins):
                step[0] += 1
                ins.then_inc(S["tab"], 1)
                dve.wait_ge(S["tab"], step[0])

            cnt, tiles, until, start, some, begin = counts[:, 0, :], tb[:, 0, :], tb[:, 1, :], tb[:, 2, :], tb[:, 3, :], tb[:, 4, :]
            part = [tb[:, 5 + k, :] for k in range(4)]
            then(dve.tensor_tensor(begin, cnt, const["region"], ALU.add))
            then(dve.tensor_copy(ends[:, :], begin[0:1, :]))
            dve.sem_inc(S["ends_out"], 1)
            then(dve.tensor_scalar(tiles, cnt, float(P - 1), None, ALU.add))
            then(dve.tensor_copy(tbi[:, :], tiles))
            then(dve.tensor_scalar(tbi[:, :], tbi[:, :], 7, None, ALU.arith_shift_right))
            then(dve.tensor_copy(tiles, tbi[:, :]))
            then(dve.tensor_scalar(some, tiles, 0.0, None, ALU.is_gt))
            then(dve.tensor_tensor_scan(until, tiles, tiles, 0.0, ALU.add, ALU.bypass))
            then(dve.tensor_tensor(start, until, tiles, ALU.subtract))
            for b in range(2):
                n = const["tile"][:, b:b + 1]
                v = [tv[:, b, k:k + 1] for k in range(8)]
                then(dve.tensor_scalar(part[0], until, n, None, ALU.is_le))
                then(dve.tensor_reduce(v[0], part[0], AX.X, ALU.add))
                then(dve.tensor_tensor(part[1], part[0], tiles, ALU.mult))
                then(dve.tensor_reduce(v[1], part[1], AX.X, ALU.add))
                then(dve.scalar_tensor_tensor(out=part[2], in0=start, scalar=n, in1=some, op0=ALU.is_le, op1=ALU.mult))
                then(dve.tensor_reduce(v[2], part[2], AX.X, ALU.add))
                then(dve.scalar_tensor_tensor(out=part[3], in0=start, scalar=n, in1=some, op0=ALU.is_equal, op1=ALU.mult))
                then(dve.tensor_reduce(v[3], part[3], AX.X, ALU.add))
                then(dve.tensor_tensor(v[4], n, v[1], ALU.subtract))
                then(dve.tensor_scalar(v[4], v[4], float(P), None, ALU.mult))
                then(dve.tensor_scalar(v[5], v[0], float(CAP), None, ALU.mult))
                then(dve.tensor_tensor(v[4], v[4], v[5], ALU.add))
                then(dve.tensor_scalar(v[4], v[4], float(SPARE), None, ALU.min))
                then(dve.tensor_copy(tvi[:, b, T_OFF:T_OFF + 1], v[4]))
                then(dve.tensor_scalar(v[6], v[0], float(EXPERTS - 1), None, ALU.min))
                then(dve.tensor_copy(tvi[:, b, T_EXPERT:T_EXPERT + 1], v[6]))
                then(dve.tensor_copy(tvi[:, b, T_SLOT:T_SLOT + 1], v[2]))
                then(dve.tensor_scalar(tvi[:, b, T_SLOT:T_SLOT + 1], tvi[:, b, T_SLOT:T_SLOT + 1], W_SLOTS - 1, None, ALU.bitwise_and))
                then(dve.tensor_copy(tvi[:, b, T_LOAD:T_LOAD + 1], v[3]))
            dve.sem_inc(S["table_set"], 1)

            dve.wait_ge(S["table_in"], 16)
            dve.tensor_copy(slot_row[:, :], table[:, :].rearrange("a (n c) -> a n c", c=T_COLS)[:, :, T_SLOT]).then_inc(S["slots_set"], 1)

            def act_out(n, v, u):
                dve.wait_ge(S["silu"], n + 1)
                wait(dve, S["act_turned"], n - 1)
                dve.tensor_tensor(ae[:, u % 2, :], sg[:, u % 2, :], banks[2 + u % 2][:, INTER:2 * INTER], ALU.mult).then_inc(S["act_ready"], 1)

            def y_out(n, v, u):
                dve.wait_ge(S["down_mm"], n + 1)
                dve.wait_ge(S["meta"], n + 1)
                wait(dve, y_added[u], 16 * v)
                dve.tensor_scalar(ids2[:, u:u + 1], meta[:, u, 1:2].bitcast(U32), u * (TOK + P), None, ALU.add)
                dve.tensor_scalar(ye[:, u, :], banks[6 + u % 2][:, 0:D], meta[:, u, 0:1], None, ALU.mult).then_inc(S["y_ready"], 1)

            walk(dve, E_TILES, [(act_out, 2), (y_out, 4)], SUMS)

            dve.wait_ge(S["sh_added"], TILES)

            def f_pairs(t, n, u):
                dve.wait_ge(sums_in[u], 16 * (n + 1))
                dve.tensor_tensor(si4[:, u, 0, :], si4[:, u, 0, :], si4[:, u, 1, :], ALU.add).then_inc(S["f_pairs"], 1)

            def f_first(t, n, u):
                dve.wait_ge(S["f_pairs"], t + 1)
                dve.tensor_tensor(hl[:, u % 2, :], at(acc, t), si4[:, u, 0, :], ALU.add).then_inc(S["f_first"], 1)

            def f_sum(t, n, u):
                dve.wait_ge(S["f_first"], t + 1)
                dve.wait_ge(S["f_pool"], t + 1)
                dve.tensor_tensor(hl[:, u % 2, :], hl[:, u % 2, :], si4[:, u, 2, :], ALU.add).then_inc(S["f_sum"], 1)

            f_bn, f_aggr, f_eps = norm_steps(lambda u: [hl[:, u % 2, :]], st2, mv2, ve, LN_EPS, "f_stats", "f_var")

            def f_start(t, n, u):
                dve.wait_ge(S["f_sum"], t + 1)
                f_bn(t, n, u)

            def f_norm(t, n, u):
                dve.wait_ge(S["f_rstd"], t + 1)
                wait(dve, o_stored[u], 16 * n)
                dve.tensor_scalar(of[:, u, :], hl[:, u % 2, :], mv2[:, u % 2, 0:1], rs[:, u % 2, :], ALU.subtract, ALU.mult).then_inc(S["f_ready"], 1)

            walk(dve, TILES, [(f_first, 1), (f_pairs, 0), (f_sum, 1), (f_start, 1), (f_norm, 2), (f_aggr, 1), (f_eps, 1)], E_SLOTS)

        @block.tensor
        def _(pe):
            pe.wait_ge(S["tok_w_in"], 48)
            for c in range(PC):
                last = pe.matmul(banks[7][:, 0:D], b1s[:, c:c + 1].to_broadcast([P, P]), wt[:, c, :], start=(c == 0), stop=(c == PC - 1))
            last.then_inc(S["bias_mm"], 1)
            pe.wait_ge(S["wtg_ready"], 1)
            pe.wait_ge(S["consts_in"], 16)

            def turn_x(t, n, u):
                pe.wait_ge(S["x_normed"], t + 1)
                wait(pe, S["xT_out"], t)
                for c in range(PC):
                    last = pe.transpose(banks[c // 3][:, (c % 3) * P:(c % 3 + 1) * P], xs[:, u, c * P:(c + 1) * P], ident)
                last.then_inc(S["x_turned"], 1)

            def tok(t, n, u):
                pe.wait_ge(S["xT_out"], t + 1)
                wait(pe, S["h_sum"], t - A_SLOTS + 1)
                for c in range(PC):
                    last = pe.matmul(banks[2 + u][:, 0:D], xT[:, u, c, :], wtg[:, c, :], start=(c == 0), stop=(c == PC - 1))
                last.then_inc(S["tok_mm"], 1)

            def turn_h(t, n, u):
                pe.wait_ge(S["h_ready"], t + 1)
                wait(pe, S["hT_out"], t)
                for c in range(DC):
                    last = pe.transpose(banks[5][:, c * P:(c + 1) * P], hs[:, u, c * P:(c + 1) * P], ident)
                last.then_inc(S["h_turned"], 1)

            def values(t, n, u):
                pe.wait_ge(S["hT_out"], t + 1)
                wait(pe, S["v_out"], t)
                if isinstance(t, int) and t == 0:
                    pe.wait_ge(S["weights_in"], 16 * 5)
                for c in range(DC):
                    last = pe.matmul(banks[6][:, 0:D], hTs[:, u, c, :], wv[:, c, :], start=(c == 0), stop=(c == DC - 1))
                last.then_inc(S["v_mm"], 1)

            tail = walk(pe, TILES, [(turn_h, 4), (values, 5), (turn_x, 0), (tok, 1)], A_SLOTS, hold=True)

            def project_qk(t, n, u):
                c, r = 2 * n + u // PAIRS, u % PAIRS
                if r == 3:
                    return
                if isinstance(t, int):
                    pe.wait_ge(S["xT_out"], TILES)
                    pe.wait_ge(S["hT_out"], -(-(c + 1) * CT // P))
                if r == 0:
                    wait(pe, S["q_mul"], 2 * c)
                elif r == 1:
                    pe.wait_ge(S["q_out"], c + 1)
                else:
                    pe.wait_ge(S["k_mul"], 2 * c + 2)
                for b, w, half in (((0, wq, 1), (1, wk, 1)), ((0, wk, 0), (1, wks, 0)), ((0, wq, 0), (1, wqs, 0)))[r]:
                    for d in range(DC):
                        tokens = hT[:, d, c * CT:(c + 1) * CT] if isinstance(c, int) else hT[:, d, bass.ds(c * CT, CT)]
                        last = pe.matmul(banks[b][:, 0:CT], w[:, d, half * P:(half + 1) * P], tokens, start=(d == 0), stop=(d == DC - 1))
                last.then_inc(S["qk_mm"], 1)

            def scores(t, n, u):
                c, r = 2 * n + u // PAIRS, u % PAIRS
                pe.wait_ge(S["q_rot"], c + 1)
                pe.wait_ge(S["q_out"], c + 1)
                pe.wait_ge(S["kexp_out"], 2 * c + 2)
                wait(pe, S["biased"], t)
                if isinstance(t, int) and t == 0:
                    for done in ("hT_out", "v_out", "h_sum"):
                        pe.wait_ge(S[done], TILES)
                for half in range(2):
                    for i in range(2):
                        img = 2 * r + i
                        m = 64 if i == 0 else SEQ
                        last = pe.matmul(banks[6 + half][64 * i:64 * i + m, 0:HALF * SEQ], qT[:, u // PAIRS, half, img * SEQ:img * SEQ + m],
                                         kexp[u // PAIRS][:, half, :, img * SEQ:(img + 1) * SEQ], start=True, stop=True)
                last.then_inc(S["scores_mm"], 1)

            def turn(t, n, u):
                pe.wait_ge(S["exped"], t + 1)
                wait(pe, S["pT_act"], t)
                wait(pe, S["pT_dve"], t)
                for g in range(GROUPS):
                    w = min(TRI, HEADS - TRI * g) * SEQ
                    b, k = (2, g) if g < 4 else (3, g - 4)
                    last = pe.transpose(banks[b][0:w, k * QP:(k + 1) * QP], pr[0:QP, u % 2, g * TRI * SEQ:g * TRI * SEQ + w], ident[0:QP, 0:QP])
                last.then_inc(S["p_turned"], 1)

            def attend(t, n, u):
                pe.wait_ge(S["pT_act"], t + 1)
                pe.wait_ge(S["pT_dve"], t + 1)
                pe.wait_ge(S["v_masked"], t + 1)
                wait(pe, S["attended"], t - 1)
                for i in range(2):
                    m = 64 if i == 0 else SEQ
                    for g in range(GROUPS):
                        heads = min(TRI, HEADS - TRI * g)
                        k = heads * SEQ
                        last = pe.matmul(banks[4 + u % 2][64 * i:64 * i + m, g * TRI * VW:(g * TRI + heads) * VW],
                                         pT[0:k, u % 2, g, 64 * i:64 * i + m],
                                         vbd[0:k, u % PAIRS, i, g * TRI:g * TRI + heads, :].rearrange("p h w -> p (h w)"),
                                         start=True, stop=True)
                last.then_inc(S["pv_mm"], 1)

            walk_pairs(pe, [(scores, SETUP), (project_qk, 0), (turn, SETUP + 1), (attend, SETUP + 2)], tail)

            pe.wait_ge(S["late_in"], 16 * 4)
            pe.wait_ge(S["attended"], CHUNKS * PAIRS)
            pe.wait_ge(S["biased"], CHUNKS * PAIRS)

            def turn_a(t, n, u):
                pe.wait_ge(a_in[u], 16 * (n + 1))
                wait(pe, S["aT_out"], t)
                for c in range(DC):
                    last = pe.transpose(banks[0][:, c * P:(c + 1) * P], ai[:, u, c * P:(c + 1) * P], ident)
                last.then_inc(S["a_turned"], 1)

            def project(t, n, u):
                pe.wait_ge(S["aT_out"], t + 1)
                wait(pe, S["r_sum"], t)
                for c in range(DC):
                    last = pe.matmul(banks[1][:, 0:D], aT[:, u, c, :], wo[:, c, :], start=(c == 0), stop=(c == DC - 1))
                last.then_inc(S["wo_mm"], 1)

            def turn_h2(t, n, u):
                pe.wait_ge(S["h2_ready"], t + 1)
                wait(pe, S["h2T_out"], t)
                for c in range(DC):
                    last = pe.transpose(banks[2][:, c * P:(c + 1) * P], h2[:, u, c * P:(c + 1) * P], ident)
                last.then_inc(S["h2_turned"], 1)

            def gate(t, n, u):
                pe.wait_ge(S["h2T_out"], t + 1)
                wait(pe, S["gate_sig"], t)
                for c in range(DC):
                    last = pe.matmul(banks[3][:, 0:EXPERTS], h2Ts[:, u, c, :], gw[:, c, :], start=(c == 0), stop=(c == DC - 1))
                last.then_inc(S["gate_mm"], 1)

            def rank(t, n, u):
                pe.wait_ge(S["chosen"], t + 1)
                wait(pe, S["counted"], t - 1)
                pe.matmul(banks[4 + u][:, 0:EXPERTS], const["before"], chosen[:, u, :], start=True, stop=True)
                pe.matmul(banks[4 + u][:, EXPERTS:2 * EXPERTS], const["ones"], chosen[:, u, :], start=True, stop=True).then_inc(S["ranked"], 1)

            def shared_up(t, n, u):
                pe.wait_ge(S["h2T_out"], t + 1)
                wait(pe, S["sh_act"], t)
                for part in range(2 * SHARED // P):
                    for c in range(DC):
                        last = pe.matmul(banks[6][:, part * P:(part + 1) * P], wsh[:, c, part * P:(part + 1) * P], h2Ts[:, u, c, :],
                                         start=(c == 0), stop=(c == DC - 1))
                last.then_inc(S["sh_up_mm"], 1)

            def shared_down(t, n, u):
                pe.wait_ge(S["sh_act"], t + 1)
                wait(pe, S["sh_added"], t)
                for m in range(SHARED // P):
                    last = pe.matmul(banks[7][:, 0:D], sha[:, u, 1, m * P:(m + 1) * P], dsh[:, m, :], start=(m == 0), stop=(m == SHARED // P - 1))
                last.then_inc(S["sh_down_mm"], 1)

            walk(pe, TILES, [(rank, 4), (turn_h2, 2), (turn_a, 0), (shared_down, 5), (gate, 2), (project, 0), (shared_up, 3)])

            pe.wait_ge(S["h2T_out"], TILES)
            pe.wait_ge(S["gate_sig"], TILES)
            pe.wait_ge(S["counted"], TILES)

            pe.wait_ge(S["sh_act"], TILES)
            pe.wait_ge(S["sh_added"], TILES)
            pe.wait_ge(S["slots_set"], 1)

            PE_TURN = 2 * SUMS

            def turn_xe(n, v, u):
                pe.wait_ge(rows_in[u % SUMS], 16 * (2 * v + u // SUMS + 1))
                wait(pe, S["xT_out_e"], n - 1)
                for c in range(DC):
                    last = pe.transpose(banks[u % 2][:, c * P:(c + 1) * P], xe[:, u % SUMS, c * P:(c + 1) * P], ident)
                last.then_inc(S["x_turned_e"], 1)

            of_tiles = {}

            def load_slots(v):
                settled(pe, S["pe_settled"])
                _, slots = nc.values_load_multi_w_load_instructions(
                    slot_row[0:1, bass.ds(v * PE_TURN - SUMS, PE_TURN + SUMS)], engines=(ENG.PE,), min_val=0, max_val=W_SLOTS - 1,
                    skip_runtime_bounds_check_because=CLAMPED)
                of_tiles.update({k - SUMS: slot for k, slot in enumerate(slots)})

            def weights(n, place, cols):
                if isinstance(n, int):
                    _, (slot,) = nc.values_load_multi_w_load_instructions(
                        slot_row[0:1, n:n + 1], engines=(ENG.PE,), min_val=0, max_val=W_SLOTS - 1, skip_runtime_bounds_check_because=CLAMPED)
                else:
                    slot = of_tiles[place]
                return moe[:, bass.ds(slot, 1), cols].rearrange("p a n -> p (a n)")

            def up(n, v, u):
                pe.wait_ge(S["xT_out_e"], n + 1)
                pe.wait_ge(w_in[u % SUMS], 16 * (2 * v + u // SUMS + 1))
                wait(pe, S["act_ready"], n - 1)
                w = weights(n, u if u < PE_TURN - 2 else u - PE_TURN, slice(0, 2 * D))
                for c in range(DC):
                    last = pe.matmul(banks[2 + u % 2][:, 0:2 * INTER], xeT[:, u % 2, c, :], w[:, c * 2 * INTER:(c + 1) * 2 * INTER],
                                     start=(c == 0), stop=(c == DC - 1))
                last.then_inc(S["up_mm"], 1)

            def turn_act(n, v, u):
                pe.wait_ge(S["act_ready"], n + 1)
                wait(pe, S["actT_out"], n - 1)
                pe.transpose(banks[4 + u % 2][:, 0:P], ae[:, u % 2, :], ident).then_inc(S["act_turned"], 1)

            def down(n, v, u):
                pe.wait_ge(S["actT_out"], n + 1)
                wait(pe, S["y_ready"], n - 1)
                pe.matmul(banks[6 + u % 2][:, 0:D], aeT[:, u % 2, :], weights(n, u if u < PE_TURN - SUMS else u - PE_TURN, slice(2 * D, 3 * D)), start=True, stop=True).then_inc(S["down_mm"], 1)

            walk(pe, E_TILES, [(up, 2), (turn_act, 3), (turn_xe, 0), (down, 4)], PE_TURN, begin=load_slots)


def shape_constants():
    import numpy as np
    c = np.zeros((P, CONST_W), np.float32)

    def put(name, value):
        a, w = CONST_AT[name]
        c[:, a:a + w] = value

    p = np.arange(P)[:, None]
    put("ident", p == np.arange(P)[None])
    put("k_heads", p // DH == np.arange(HALF)[None])
    put("v_heads", (p < TRI * SEQ) & (np.arange(HEADS)[None] % TRI == p // SEQ))
    pos = np.arange(SEQ, dtype=np.float32)
    inv = np.float32(10000.0) ** (-(np.arange(0, DH, 2, dtype=np.float32) / np.float32(DH)))
    theta = (pos[:, None] * inv[None, :]).astype(np.float32)
    d = np.arange(P) % DH
    put("cos", np.cos(theta).T[d // 2])
    put("sin", np.sin(theta).T[d // 2] * np.where(d % 2 == 0, -1.0, 1.0)[:, None])
    q = np.where(p < SEQ, p, p - 64)
    live = (q >= 0) & (q < SEQ)
    k = np.arange(SEQ)[None]
    put("causal", np.where(live & (k > q), MASKED, 0.0))
    put("dist", np.where(live, -np.abs(q - k), 0.0))
    put("decays", np.array([h & 1 for h in HEAD_ORDER], np.float32)[None])
    put("experts", np.arange(EXPERTS)[None])
    put("groups", np.arange(NGROUP)[None])
    put("before", p < np.arange(P)[None])
    put("ones", 1.0)
    put("region", np.arange(EXPERTS)[None] * CAP)
    put("tile", p + P * np.arange(2)[None])
    pad = np.zeros((P, ROW), np.float32)
    pad[:, D + 1] = (TOK + np.arange(P)).astype(np.uint32).view(np.float32)
    put("pad_row", pad)
    return c


def kernel(**inputs):
    import numpy as np
    import concourse.bacc as bacc
    from concourse.bass_utils import run_bass_kernel_spmd

    g = {k: np.asarray(v) for k, v in inputs.items()}

    def chunks(w):
        return np.ascontiguousarray(w.reshape(w.shape[0] // P, P, -1).transpose(1, 0, 2))

    x = g["x"]
    b, ch, hh, ww = x.shape
    patches = x.reshape(b, ch, hh // 16, 16, ww // 16, 16).transpose(0, 2, 4, 3, 5, 1).reshape(TOK, PATCH)
    wqkv = g["L0_attn_w_qkv"].reshape(D, 3, HEADS, DH)[:, :, HEAD_ORDER]
    swap = np.arange(DH) ^ 1
    w_q, w_k, w_v = (wqkv[:, i].reshape(D, D) for i in range(3))
    w_qs, w_ks = (wqkv[:, i, :HALF][:, :, swap].reshape(D, P) for i in range(2))
    w_o = g["L0_attn_w_o"].reshape(HEADS, DH, D)[HEAD_ORDER].reshape(D, D)
    eg, eu, ed = (g[f"L0_ffn_{n}_w"].transpose(0, 2, 1) for n in ("eg", "eu", "ed"))
    up = np.concatenate([eg, eu], axis=2).reshape(EXPERTS, DC, P, 2 * INTER).transpose(0, 2, 1, 3).reshape(EXPERTS, P, 2 * D)
    w_moe = np.concatenate([up, ed], axis=2)
    arrays = {
        "patches": patches, "w_tok": chunks(g["L0_tok_W_mlp"]),
        "rows": np.concatenate([g["L0_tok_b_mlp"], g["L0_tok_g2"], g["L0_tok_b2"], g["L0_ffn_gate_bias"]])[None],
        "b1_col": g["L0_tok_b1"].reshape(PC, P).T, "g1_col": g["L0_tok_g1"].reshape(PC, P).T,
        "w_q": chunks(w_q), "w_k": chunks(w_k), "w_qs": chunks(w_qs), "w_ks": chunks(w_ks), "w_v": chunks(w_v),
        "w_o": chunks(w_o), "gate_w": chunks(g["L0_ffn_gate_w"].T), "log_xi": g["L0_attn_log_xi"][HEAD_ORDER][None],
        "w_shared": chunks(np.concatenate([g["L0_ffn_sg_w"], g["L0_ffn_su_w"]]).T),
        "d_shared": chunks(g["L0_ffn_sd_w"].T), "w_moe": w_moe, "consts": shape_constants(),
    }
    nc = bacc.Bacc("TRN2", target_bir_lowering=False, num_devices=1)
    aps = {}
    for name, a in arrays.items():
        arrays[name] = np.ascontiguousarray(a)
        aps[name] = nc.dram_tensor(name, a.shape, mybir.dt.from_np(a.dtype), kind="ExternalInput").ap()
    out = nc.dram_tensor("result", (TOK, D), F32, kind="ExternalOutput").ap()
    program(nc, out=out, **aps)
    r = run_bass_kernel_spmd(nc, [arrays], core_ids=[0])
    return r.results[0]["result"].reshape(IMAGES, SEQ, D)
```
